# Optimizing a Trainium2 kernel written in Bass

```python
import numpy as np
import jax
import jax.numpy as jnp

def _softmax(x, axis=-1):
    return jax.nn.softmax(x, axis=axis)

def _gelu(x):
    return jax.nn.gelu(x, approximate=True)

def _silu(x):
    return jax.nn.silu(x)

def _sigmoid(x):
    return jax.nn.sigmoid(x)

def _layernorm(x, axis=-1, eps=1e-05):
    m = jnp.mean(x, axis=axis, keepdims=True)
    v = jnp.var(x, axis=axis, keepdims=True)
    return (x - m) / jnp.sqrt(v + eps)

def _scatter_add(tgt, idx, src, axis=0):
    return tgt.at[idx].add(src)

def _segment_sum(src, seg, n):
    return jax.ops.segment_sum(src, seg, n)
kernel_name = 'mk_xattn_ffn_d1_seqx_r4_150a1f'

def setup_inputs(seed: int=0):
    np.random.seed(seed)
    _w = jnp.asarray

    def _rec_inputs():
        import jax
        import jax.numpy as jnp
        _rk = jax.random.key(seed)
        x = 7.22e-05 + 1 * jax.random.normal(jax.random.fold_in(_rk, 1), (16, 256, 512), jnp.float32)
        _lenS = 256 - jax.random.randint(jax.random.fold_in(_rk, 7), (16,), 0, max(1, 256 // 4) + 1, jnp.int32)
        _lenS2 = 256 - jax.random.randint(jax.random.fold_in(_rk, 8), (16,), 0, max(1, 256 // 4) + 1, jnp.int32)
        _ctx_1024P = jax.random.normal(jax.random.fold_in(_rk, 11), (16, 16, 256), jnp.float32)
        _ctx_1024c = jax.random.dirichlet(jax.random.fold_in(_rk, 511), 0.3 * jnp.ones((16,), jnp.float32), (16, 256))
        _ctx_1024t = jnp.einsum('bsk,bkd->bsd', _ctx_1024c, _ctx_1024P)
        _ctx_1024t = _ctx_1024t * jax.lax.rsqrt(jnp.mean(jnp.square(_ctx_1024t)) + 1e-12) * 0.953939
        ctx_1024 = -0.000673644 + 1.00013 * (_ctx_1024t + 0.3 * jax.random.normal(jax.random.fold_in(_rk, 611), (16, 256, 256), jnp.float32))
        return (x, ctx_1024)
    x, ctx_1024 = _rec_inputs()

    def _L0_xattn_setup():
        import jax, jax.numpy as jnp
        import numpy as np
        B, S1, S2, DCA = (2, 512, 256, 16)
        QDIM, KDIM, H = (512, 256, 16)
        HD = QDIM // H
        SCALE = HD ** (-0.5)
        EPS = 1e-06
        DCA_WEIGHT = 1.0

        def _ln(t, w, b):
            m = jnp.mean(t, axis=-1, keepdims=True)
            v = jnp.var(t, axis=-1, keepdims=True)
            return (t - m) * jax.lax.rsqrt(v + EPS) * w + b

        def _attn(q, k, v):
            s = jnp.einsum('bhqd,bhkd->bhqk', q, k) * SCALE
            p = jax.nn.softmax(s, axis=-1)
            return jnp.einsum('bhqk,bhkd->bhqd', p, v)
        key = jax.random.key(seed)
        ks = jax.random.split(key, 8)
        w = lambda k, shape: jax.random.normal(k, shape, jnp.float32) * 0.02
        return {'x': jax.random.normal(ks[0], (B, S1, QDIM), jnp.float32), 'y': jax.random.normal(ks[1], (B, S2 + DCA, KDIM), jnp.float32), 'Wq': w(ks[2], (QDIM, QDIM)), 'bq': jnp.zeros((QDIM,), jnp.float32), 'Wk': w(ks[3], (KDIM, QDIM)), 'bk': jnp.zeros((QDIM,), jnp.float32), 'Wv': w(ks[4], (KDIM, QDIM)), 'bv': jnp.zeros((QDIM,), jnp.float32), 'Wkv_dca': w(ks[5], (KDIM, 2 * QDIM)), 'bkv_dca': jnp.zeros((2 * QDIM,), jnp.float32), 'qn_w': jnp.ones((HD,), jnp.float32), 'qn_b': jnp.zeros((HD,), jnp.float32), 'kn_w': jnp.ones((HD,), jnp.float32), 'kn_b': jnp.zeros((HD,), jnp.float32), 'kn_dca_w': jnp.ones((HD,), jnp.float32), 'kn_dca_b': jnp.zeros((HD,), jnp.float32), 'Wo': w(ks[6], (QDIM, QDIM)), 'bo': jnp.zeros((QDIM,), jnp.float32)}
    _L0_xattn_all = _L0_xattn_setup()
    _L0_xattn_in = {k: v for k, v in _L0_xattn_all.items() if k in ('Wq', 'bq', 'Wk', 'bk', 'Wv', 'bv', 'Wkv_dca', 'bkv_dca', 'qn_w', 'qn_b', 'kn_w', 'kn_b', 'kn_dca_w', 'kn_dca_b', 'Wo', 'bo')}
    del _L0_xattn_all

    def _L0_ffn_setup():
        import jax, jax.numpy as jnp
        import numpy as np
        D_MODEL = 512
        D_FF = 352
        N_EXPERTS = 6
        TOP_K = 2
        B, S = (8, 1024)
        key = jax.random.key(seed)
        ks = jax.random.split(key, 6)
        x = jax.random.normal(ks[0], (B, S, D_MODEL), dtype=jnp.float32)
        W1 = jax.random.normal(ks[1], (N_EXPERTS, D_MODEL, D_FF), dtype=jnp.float32) * 0.02
        b1 = jax.random.normal(ks[2], (N_EXPERTS, D_FF), dtype=jnp.float32) * 0.02
        W2 = jax.random.normal(ks[3], (N_EXPERTS, D_FF, D_MODEL), dtype=jnp.float32) * 0.02
        b2 = jax.random.normal(ks[4], (N_EXPERTS, D_MODEL), dtype=jnp.float32) * 0.02
        gate_W = jax.random.normal(ks[5], (N_EXPERTS, D_MODEL), dtype=jnp.float32) * 0.02
        return {'x': x, 'gate_W': gate_W, 'W1': W1, 'b1': b1, 'W2': W2, 'b2': b2}
    _L0_ffn_all = _L0_ffn_setup()
    _L0_ffn_in = {k: v for k, v in _L0_ffn_all.items() if k in ('gate_W', 'W1', 'b1', 'W2', 'b2')}
    del _L0_ffn_all
    return {'x': x, 'ctx_1024': ctx_1024, 'L0_xattn_Wq': _L0_xattn_in['Wq'], 'L0_xattn_bq': _L0_xattn_in['bq'], 'L0_xattn_Wk': _L0_xattn_in['Wk'], 'L0_xattn_bk': _L0_xattn_in['bk'], 'L0_xattn_Wv': _L0_xattn_in['Wv'], 'L0_xattn_bv': _L0_xattn_in['bv'], 'L0_xattn_Wkv_dca': _L0_xattn_in['Wkv_dca'], 'L0_xattn_bkv_dca': _L0_xattn_in['bkv_dca'], 'L0_xattn_qn_w': _L0_xattn_in['qn_w'], 'L0_xattn_qn_b': _L0_xattn_in['qn_b'], 'L0_xattn_kn_w': _L0_xattn_in['kn_w'], 'L0_xattn_kn_b': _L0_xattn_in['kn_b'], 'L0_xattn_kn_dca_w': _L0_xattn_in['kn_dca_w'], 'L0_xattn_kn_dca_b': _L0_xattn_in['kn_dca_b'], 'L0_xattn_Wo': _L0_xattn_in['Wo'], 'L0_xattn_bo': _L0_xattn_in['bo'], 'L0_ffn_gate_W': _L0_ffn_in['gate_W'], 'L0_ffn_W1': _L0_ffn_in['W1'], 'L0_ffn_b1': _L0_ffn_in['b1'], 'L0_ffn_W2': _L0_ffn_in['W2'], 'L0_ffn_b2': _L0_ffn_in['b2']}

def reference(x, ctx_1024, L0_xattn_Wq, L0_xattn_bq, L0_xattn_Wk, L0_xattn_bk, L0_xattn_Wv, L0_xattn_bv, L0_xattn_Wkv_dca, L0_xattn_bkv_dca, L0_xattn_qn_w, L0_xattn_qn_b, L0_xattn_kn_w, L0_xattn_kn_b, L0_xattn_kn_dca_w, L0_xattn_kn_dca_b, L0_xattn_Wo, L0_xattn_bo, L0_ffn_gate_W, L0_ffn_W1, L0_ffn_b1, L0_ffn_W2, L0_ffn_b2):
    import jax
    import jax.numpy as jnp

    def _L0_xattn_ref(x, y, Wq, bq, Wk, bk, Wv, bv, Wkv_dca, bkv_dca, qn_w, qn_b, kn_w, kn_b, kn_dca_w, kn_dca_b, Wo, bo):
        import jax, jax.numpy as jnp
        import numpy as np
        B, S1, S2, DCA = (2, 512, 256, 16)
        QDIM, KDIM, H = (512, 256, 16)
        HD = QDIM // H
        SCALE = HD ** (-0.5)
        EPS = 1e-06
        DCA_WEIGHT = 1.0

        def _ln(t, w, b):
            m = jnp.mean(t, axis=-1, keepdims=True)
            v = jnp.var(t, axis=-1, keepdims=True)
            return (t - m) * jax.lax.rsqrt(v + EPS) * w + b

        def _attn(q, k, v):
            s = jnp.einsum('bhqd,bhkd->bhqk', q, k) * SCALE
            p = jax.nn.softmax(s, axis=-1)
            return jnp.einsum('bhqk,bhkd->bhqd', p, v)
        b, s1, _ = x.shape
        y_dca = y[:, -DCA:, :]
        y_main = y[:, :-DCA, :]
        kv_dca = (y_dca @ Wkv_dca + bkv_dca).reshape(b, DCA, 2, H, HD)
        k_dca = _ln(kv_dca[:, :, 0], kn_dca_w, kn_dca_b)
        v_dca = kv_dca[:, :, 1]
        s2 = y_main.shape[1]
        q = _ln((x @ Wq + bq).reshape(b, s1, H, HD), qn_w, qn_b)
        kv = jnp.concatenate([y_main @ Wk + bk, y_main @ Wv + bv], axis=-1)
        kv = kv.reshape(b, s2, H, 2 * HD)
        k = _ln(kv[..., :HD], kn_w, kn_b)
        v = kv[..., HD:]
        qT = q.transpose(0, 2, 1, 3)
        ctx = _attn(qT, k.transpose(0, 2, 1, 3), v.transpose(0, 2, 1, 3))
        ctx = ctx.transpose(0, 2, 1, 3).reshape(b, s1, QDIM)
        ctx_dca = _attn(qT, k_dca.transpose(0, 2, 1, 3), v_dca.transpose(0, 2, 1, 3))
        ctx_dca = ctx_dca.transpose(0, 2, 1, 3).reshape(b, s1, QDIM)
        ctx = ctx + DCA_WEIGHT * ctx_dca
        return ctx @ Wo + bo

    def _L0_ffn_ref(x, gate_W, W1, b1, W2, b2):
        import jax, jax.numpy as jnp
        import numpy as np
        D_MODEL = 512
        D_FF = 352
        N_EXPERTS = 6
        TOP_K = 2
        B, S = (8, 1024)
        gate_logits = jnp.einsum('bd,ed->be', x.mean(axis=1), gate_W)
        gate_probs = jax.nn.softmax(gate_logits, axis=-1)
        topk_vals, topk_idx = jax.lax.top_k(gate_probs, TOP_K)
        topk_vals = topk_vals / topk_vals.sum(axis=-1, keepdims=True)
        W1g = W1[topk_idx]
        b1g = b1[topk_idx]
        W2g = W2[topk_idx]
        b2g = b2[topk_idx]
        h = jnp.einsum('bsd,bkdf->bksf', x, W1g) + b1g[:, :, None, :]
        h = jax.nn.gelu(h, approximate=False)
        eo = jnp.einsum('bksf,bkfd->bksd', h, W2g) + b2g[:, :, None, :]
        return jnp.einsum('bk,bksd->bsd', topk_vals, eo)
    x = x + _L0_xattn_ref(_layernorm(x, axis=-1), ctx_1024, L0_xattn_Wq, L0_xattn_bq, L0_xattn_Wk, L0_xattn_bk, L0_xattn_Wv, L0_xattn_bv, L0_xattn_Wkv_dca, L0_xattn_bkv_dca, L0_xattn_qn_w, L0_xattn_qn_b, L0_xattn_kn_w, L0_xattn_kn_b, L0_xattn_kn_dca_w, L0_xattn_kn_dca_b, L0_xattn_Wo, L0_xattn_bo)
    x = x + _L0_ffn_ref(_layernorm(x, axis=-1), L0_ffn_gate_W, L0_ffn_W1, L0_ffn_b1, L0_ffn_W2, L0_ffn_b2)
    return x

_drawn_inputs = setup_inputs


def setup_inputs(seed=0):
    import zlib

    import numpy as np

    out = dict(_drawn_inputs(seed))
    spreads = {'L0_xattn_bq': (0.0, 0.307),
     'L0_xattn_bk': (0.0, 0.1),
     'L0_xattn_bv': (0.0, 0.1),
     'L0_xattn_bkv_dca': (0.0, 0.1),
     'L0_xattn_qn_w': (1.0, 0.6),
     'L0_xattn_qn_b': (0.0, 0.8),
     'L0_xattn_kn_w': (1.0, 0.6),
     'L0_xattn_kn_b': (0.0, 0.8),
     'L0_xattn_kn_dca_w': (1.0, 0.6),
     'L0_xattn_kn_dca_b': (0.0, 0.8),
     'L0_xattn_bo': (0.0, 0.1)}
    factors = {'L0_ffn_b1': 8.0, 'L0_ffn_b2': 4.07}
    for name, (base, spread) in spreads.items():
        noise = np.random.default_rng([zlib.crc32(name.encode()), seed]).standard_normal(out[name].shape)
        drawn = base * np.exp(spread * noise) if base else spread * noise
        out[name] = jnp.asarray(drawn.astype(out[name].dtype))
    for name, factor in factors.items():
        out[name] = (out[name] * factor).astype(out[name].dtype)
    return out
```

```python
from contextlib import ExitStack

import numpy as np
import concourse.bass as bass
from concourse import mybir

F32 = mybir.dt.float32
F32R = mybir.dt.float32r
U32 = mybir.dt.uint32
ALU = mybir.AluOpType
ACT = mybir.ActivationFunctionType
AX_X = mybir.AxisListType.X

P = 128
BANK = 512
H = 16
HD = 32
HP = P // HD
DCA = 16
SCALE = HD ** -0.5
EPS_LN = 1e-5
EPS_QK = 1e-6
EULER = float(np.e)
LEAST = -3.0e38


class Units:

    def __init__(self, banks, steps):
        self.place, self.slope, self.first = {}, {}, {}
        base = [0] * banks
        for step, names, first_b, times in steps:
            per = [len(range(k, len(names), banks)) for k in range(banks)]
            for n, name in enumerate(names):
                self.place[step, name] = (n % banks, base[n % banks] + n // banks)
            self.slope[step], self.first[step] = per, first_b
            base = [base[k] + per[k] * times for k in range(banks)]

    def bank(self, step, name):
        return self.place[step, name][0]

    def count(self, step, name, b):
        k, n = self.place[step, name]
        return (b - self.first[step]) * self.slope[step][k] + n


def wait(eng, sem, value):
    if not isinstance(value, int) or value > 0:
        eng.wait_ge(sem, value)


def bass_xattn_moe(nc, x, ctx, Wq, bq, Wk, bk, Wv, bv, Wdca, bdca, qn_w, qn_b, kn_w, kn_b,
                   kd_w, kd_b, Wo, bo, gate_W, W1, b1, W2, b2, out):
    B, S, D = x.shape
    x2_dram = nc.dram_tensor("x2_scratch", (B, P, S // P, D), F32, kind="Internal").ap()
    vd_dram = nc.dram_tensor("vdca_scratch", (B, DCA, D), F32, kind="Internal").ap()
    with ExitStack() as stack:
        attention_phase(nc, stack, x, ctx, Wq, bq, Wk, bk, Wv, bv, Wdca, bdca, qn_w, qn_b, kn_w,
                        kn_b, kd_w, kd_b, Wo, bo, x2_dram, vd_dram)
    with ExitStack() as stack:
        ffn_phase(nc, stack, x2_dram, gate_W, W1, b1, W2, b2, out)


def carry_wait(dve, scratch):
    dve.tensor_copy(scratch[:, 0:1], scratch[:, 1:2])


def attention_phase(nc, stack, x, ctx, Wq, bq, Wk, bk, Wv, bv, Wdca, bdca, qn_w, qn_b, kn_w, kn_b,
                    kd_w, kd_b, Wo, bo, x2_dram, vd_dram):
    B, S, D = x.shape
    KD = ctx.shape[2]
    KEYS = ctx.shape[1] - DCA
    T = S // P
    KC = D // P
    CC = KD // P
    NC = 2
    CK = KEYS // NC
    G = H // HP
    HH = H // 2
    W = 2 * HD
    BLK = 3 * HD
    ST = BLK + 2
    STACKED = 3 * HP * 16
    ND = 2
    BD = B // ND

    x_t = x.rearrange("b (t p) d -> b p t d", p=P)
    ctx_main = ctx[:, 0:KEYS, :].rearrange("b (c p) d -> b p c d", p=CK)

    def sem(name):
        return stack.enter_context(nc.semaphore(name))

    def sb(name, shape, dt=F32):
        return stack.enter_context(nc.sbuf_tensor(name, shape, dt))

    ident = sb("ident", [P, P])
    wq = sb("wq", [P, KC, D])
    wkv = sb("wkv", [P, CC, 2 * D])
    wo = sb("wo", [P, KC, D])
    bq_b = sb("bq_b", [P, D])
    bkv_b = sb("bkv_b", [P, 2 * D])
    bo_b = sb("bo_b", [P, D])
    affine = sb("affine", [P, 6])
    sel = sb("sel", [2 * H, 2, P], F32R)
    mask = sb("mask", [P, 2, HH * HD])
    neg_half = sb("neg_half", [P, H])
    eps_qk, eps_ln = sb("eps_qk", [P, H]), sb("eps_ln", [P, T])
    scratch = sb("scratch", [P, 2])
    xin = sb("xin", [P, T, D])
    xh = sb("xh", [P, T, D])
    xT = sb("xT", [P, KC, S])
    kn = xh
    cin = sb("cin", [P, NC, KD])
    cT = sb("cT", [P, CC, KEYS])
    xres = sb("xres", [P, T, D])
    q1 = sb("q1", [P, T, D])
    kv1 = [sb(f"kv1_{i}", [P, NC, 2, HH, W]) for i in range(2)]
    sq = [sb(f"sq{i}", [P, D]) for i in range(2)]
    vs = sb("vs", [P, 6, H])
    qf = [sb(f"qf{i}", [P, G, S]) for i in range(2)]
    kf = sb("kf", [P, G, KEYS])
    q_hi, q_lo = sb("q_hi", [P, G, S], F32R), sb("q_lo", [P, G, S], F32R)
    k_hi, k_lo = sb("k_hi", [P, G, KEYS], F32R), sb("k_lo", [P, G, KEYS], F32R)
    QS = [sb(f"QS{i}", [ST, H, S], F32R) for i in range(2)]
    KS = [sb(f"KS{i}", [ST, H, KEYS], F32R) for i in range(2)]
    st6, mv, rs = sb("st6", [P, T, 6]), sb("mv", [P, T, 2]), sb("rs", [P, T])
    mxa, den, ld, lt = (sb(n, [P, T, 2 * H]) for n in ("mxa", "den", "ld", "lt"))
    nm = sb("nm", [P, T, H])
    ed = sb("ed", [P, T, H, DCA])
    s_hi, s_lo = sb("s_hi", [2 * H, S], F32R), sb("s_lo", [2 * H, S], F32R)
    pt = [sb(f"pt{i}", [P, HP, NC * S]) for i in range(2)]
    pdt = sb("pdt", [P, 2, S])
    kdT = sb("kdT", [P, G, B * DCA])
    kdb = sb("kdb", [P, G, HP * DCA])
    vrep, vbd = sb("vrep", [P, D]), sb("vbd", [P, D])
    ot = sb("ot", [P, G, S])
    wdca = pt[0][:, :, :].rearrange("p a n -> p (a n)").rearrange("p (c n) -> p c n", c=CC)
    spare = pt[1][:, :, :].rearrange("p a n -> p (a n)")
    bd_b = spare[:, 0:2 * D]
    ydca = spare[:, 2 * D:2 * D + ND * KD].rearrange("p (c n) -> p c n", c=ND)
    ydT = spare[:, 3 * D:3 * D + CC * ND * P].rearrange("p (c n) -> p c n", c=CC)
    vdca = ot[:, :, :].rearrange("p a n -> p (a n)").rearrange("p (c n) -> p c n", c=ND)
    wsum = vs[:, :, :].rearrange("p a n -> p (a n)")

    ring = [stack.enter_context(nc.psum_tensor(f"ring{i}", [P, BANK], F32)) for i in range(4)]
    sc = [stack.enter_context(nc.psum_tensor(f"sc{i}", [P, 2, BANK], F32)) for i in range(2)]

    full = [sem(f"full{i}") for i in range(4)]
    evac = [sem(f"evac{i}") for i in range(4)]
    sc_full = [sem(f"sc_full{i}") for i in range(2)]
    sc_evac = [sem(f"sc_evac{i}") for i in range(2)]
    w_ld, y_ld, x_ld, c_ld, r_ld, vr_ld = (sem(n) for n in "w_ld y_ld x_ld c_ld r_ld vr_ld".split())
    q_in, k_in, sh_in = sem("q_in"), sem("k_in"), sem("sh_in")
    x2_st, vd_st = sem("x2_st"), sem("vd_st")
    const, ones, prep = sem("const"), sem("ones"), sem("prep")
    ln_st, ln_ag, ln_rs, xh_rdy = sem("ln_st"), sem("ln_ag"), sem("ln_rs"), sem("xh_rdy")
    sq_rdy, var_rdy, rstd, norm = sem("sq_rdy"), sem("var_rdy"), sem("rstd"), sem("norm")
    split = sem("split")
    res_rdy, kd_rdy, vbd_rdy = sem("res_rdy"), sem("kd_rdy"), sem("vbd_rdy")
    d_max, d_exp, d_den = sem("d_max"), sem("d_exp"), sem("d_den")
    g_max, ln_rdy, lt_rdy, sh_hi = sem("g_max"), sem("ln_rdy"), sem("lt_rdy"), sem("sh_hi")

    GEMM = ["Q0", "Q1", "KV00", "KV01", "KV10", "KV11"]
    BODY = ["SD", "WO0", "WO1", "XT0", "XT1", "CT", "Q0", "Q1", "KV00", "LT", "KV01", "KV10", "QT0",
            "KV11", "QT1", "SDT", "PV0", "PV1", "KT0", "KT1", "PV2", "PV3"]
    ATTN = ["SD", "LT", "SDT", "PV0", "PV1", "PV2", "PV3"]
    WOUT = ["WO0", "WO1"]
    u = Units(4, [
        ("dca", ["YT", "DK0", "DV0", "DK1", "DV1", "KD0", "KD1"], 0, 1),
        ("pro", [n for n in BODY if n not in ATTN + WOUT], -1, 1),
        ("first", [n for n in BODY if n not in WOUT], 0, 1),
        ("body", BODY, 1, B - 2),
        ("last", [n for n in BODY if n in ATTN + WOUT], B - 1, 1),
        ("tail", WOUT, B, 1)])
    DOES_ATTN, DOES_PROJ, DOES_WO = ("first", "body", "last"), ("pro", "first", "body"), (
        "body", "last", "tail")

    def begin(eng, step, name, b):
        wait(eng, evac[u.bank(step, name)], u.count(step, name, b))
        return ring[u.bank(step, name)]

    def taken(step, name):
        return evac[u.bank(step, name)]

    def wait_full(eng, step, name, b):
        eng.wait_ge(full[u.bank(step, name)], u.count(step, name, b) + 1)
        return ring[u.bank(step, name)]

    def wait_evac(eng, step, name, b):
        eng.wait_ge(evac[u.bank(step, name)], u.count(step, name, b) + 1)

    def walk(eng, body):
        body("pro", -1, 1)
        body("first", 0, 0)
        with eng.Fori(0, (B - 2) // 2) as i:
            body("body", 2 * i + 1, 1)
            body("body", 2 * i + 2, 0)
        body("last", B - 1, 1)
        body("tail", B, 0)

    def head_norm_values(k, par):
        if k < T:
            return q1[:, k, :].rearrange("p (h d) -> p h d", h=H)
        return kv1[par][0:CK, (k - T) // 2, (k - T) % 2, :, 0:HD]

    def packed_k(k):
        c, half = (k - T) // 2, (k - T) % 2
        return kn[0:CK, c, half * HH * HD:(half + 1) * HH * HD].rearrange("p (h d) -> p h d", h=HH)

    def squares(n, values):
        return sq[n % 2][0:values.shape[0], 0:values.shape[1] * HD].rearrange("p (h d) -> p h d", d=HD)

    block = stack.enter_context(nc.Block())

    @block.sync
    def _(sp):
        for dst, src in (
            (wdca, Wdca.rearrange("(c p) n -> p c n", p=P)),
            (bd_b, bdca.partition_broadcast(P)),
            (wq[:, :, :], Wq.rearrange("(c p) n -> p c n", p=P)),
            (wkv[:, :, 0:D], Wk.rearrange("(c p) n -> p c n", p=P)),
            (wkv[:, :, D:2 * D], Wv.rearrange("(c p) n -> p c n", p=P)),
            (bq_b[:, :], bq.partition_broadcast(P)),
            (bkv_b[:, 0:D], bk.partition_broadcast(P)),
            (bkv_b[:, D:2 * D], bv.partition_broadcast(P)),
            (bo_b[:, :], bo.partition_broadcast(P)),
            (wo[:, :, :], Wo.rearrange("(c p) n -> p c n", p=P)),
        ):
            sp.dma_start(dst, src).then_inc(w_ld, 16)
        for c in range(ND):
            wait_evac(sp, "dca", f"DV{c}", 0)
            sp.dma_start(vd_dram[c * BD:(c + 1) * BD].rearrange("b k n -> (b k) n"),
                         vdca[:, c, :]).then_inc(vd_st, 16)
        sp.wait_ge(vd_st, 16 * ND)

        def load_vrep(b):
            if not isinstance(b, int) or b != 0:
                sp.wait_ge(vbd_rdy, b)
            for h in range(HH):
                sp.dma_start(vrep[h * DCA:(h + 1) * DCA, :], vd_dram[b]).then_inc(vr_ld, 16)

        def stack_parts(b, par):
            for tensor, hi, lo, order, done, n in ((QS, q_hi, q_lo, (0, 2, 1), q_in, 2),
                                                   (KS, k_hi, k_lo, (0, 1, 2), k_in, 4)):
                sp.wait_ge(split, 4 * b + n)
                dst = tensor[par][:, :, :].rearrange("p (g h) n -> p g h n", h=HP)
                for part, blk in zip((hi, hi, lo), order):
                    for h in range(HP):
                        sp.dma_start(dst[blk * HD:(blk + 1) * HD, :, h, :].bitcast(F32),
                                     part[h * HD:(h + 1) * HD, :, :].bitcast(F32)).then_inc(done, 16)

        def body(step, b, par):
            if step in DOES_PROJ:
                if step != "pro":
                    sp.wait_ge(xh_rdy, T * (b + 1))
                sp.dma_start(xin[:, :, :], x_t[b + 1]).then_inc(x_ld, 16)
                if step != "pro":
                    sp.wait_ge(sq_rdy, ND + 6 * b + 1)
                sp.dma_start(cin[0:CK, :, :], ctx_main[b + 1]).then_inc(c_ld, 16)
                load_vrep(b + 1)
            if step in DOES_WO:
                wait_evac(sp, step, "WO0", b)
                wait_evac(sp, step, "WO1", b)
                sp.dma_start(x2_dram[b - 1], xres[:, :, :]).then_inc(x2_st, 16)
                sp.wait_ge(x2_st, 16 * b)
            if step in DOES_ATTN:
                sp.dma_start(xres[:, :, :], x_t[b]).then_inc(r_ld, 16)
                wait_evac(sp, step, "LT", b)
                for row, part in ((BLK, s_hi), (BLK + 1, s_lo)):
                    sp.dma_start(QS[par][row:row + 1, :, :].bitcast(F32),
                                 part[0:H, :].bitcast(F32)).then_inc(sh_in, 16)
            if step in DOES_PROJ:
                stack_parts(b + 1, 1 - par)

        walk(sp, body)

    @block.gpsimd
    def _(pool):
        sel32 = sq[0][0:2 * H, 0:2 * P]
        pool.memset(ident[:, :], 0.0).then_inc(const, 1)
        pool.memset(sel32, 0.0).then_inc(const, 1)
        pool.memset(mask[:, :, :], 1.0).then_inc(const, 1)
        pool.memset(neg_half[:, :], -0.5).then_inc(const, 1)
        pool.memset(kdb[:, :, :], 0.0).then_inc(const, 1)
        pool.memset(eps_qk[:, :], EPS_QK).then_inc(const, 1)
        pool.memset(eps_ln[:, :], EPS_LN).then_inc(const, 1)
        pool.memset(scratch[:, :], 0.0).then_inc(const, 1)
        pool.wait_ge(const, 8)
        pool.affine_select(out=ident[:, :], in_=ident[:, :], compare_op=ALU.not_equal, fill=1.0,
                           base=0, pattern=[[-1, P]], channel_multiplier=1).then_inc(const, 1)
        sel_v = sel32.rearrange("j (a h k) -> j (a h) k", a=2, h=HH)
        pool.affine_select(out=sel_v, in_=sel_v, compare_op=ALU.not_equal, fill=1.0, base=-H,
                           pattern=[[-1, H], [0, DCA]], channel_multiplier=1).then_inc(const, 1)
        for a in range(2):
            m = mask[:, a, :].rearrange("p (h d) -> p h d", h=HH)
            pool.affine_select(out=m, in_=m, compare_op=ALU.is_ge, fill=0.0, base=0,
                               pattern=[[-DCA, HH], [0, HD]], channel_multiplier=1).then_inc(const, 1)
        pool.wait_ge(const, 12)
        for a in range(2):
            m = mask[:, a, :].rearrange("p (h d) -> p h d", h=HH)
            pool.affine_select(out=m, in_=m, compare_op=ALU.is_ge, fill=0.0, base=DCA - 1,
                               pattern=[[DCA, HH], [0, HD]], channel_multiplier=-1).then_inc(const, 1)
        pool.tensor_copy(sel[:, :, :].rearrange("j a p -> j (a p)"), sel32).then_inc(const, 1)

        def normalise(k, n, values, normal):
            rows, heads = values.shape[0], values.shape[1]
            w = vs[0:rows, k, 0:heads]
            pool.wait_ge(var_rdy, n + 1)
            pool.tensor_tensor(w, w, eps_qk[0:rows, 0:heads], ALU.add).then_inc(rstd, 1)
            pool.wait_ge(rstd, 2 * n + 1)
            pool.tensor_tensor(w, w, neg_half[0:rows, 0:heads], ALU.pow).then_inc(rstd, 1)
            pool.wait_ge(rstd, 2 * n + 2)
            pool.tensor_tensor(normal, values, w.unsqueeze(2).broadcast_to([rows, heads, HD]),
                               ALU.mult).then_inc(norm, 1)

        for c in range(ND):
            values = q1[:, c, :].rearrange("p (h d) -> p h d", h=H)
            normalise(c, c, values, values)
        def body(step, b, par):
            if step in DOES_PROJ:
                pool.wait_ge(ln_ag, T * (b + 2))
                pool.tensor_tensor(rs[:, :], mv[:, :, 1], eps_ln[:, :], ALU.add).then_inc(ln_rs, 1)
                pool.wait_ge(ln_rs, 2 * (b + 1) + 1)
                pool.tensor_tensor(rs[:, :], rs[:, :], neg_half[:, 0:T], ALU.pow).then_inc(ln_rs, 1)
            if step in DOES_ATTN:
                pool.wait_ge(r_ld, 16 * (b + 1))
                pool.wait_ge(w_ld, 16 * 34)
                pool.tensor_tensor(xres[:, :, :], xres[:, :, :],
                                   bo_b[:, :].unsqueeze(1).broadcast_to([P, T, D]),
                                   ALU.add).then_inc(res_rdy, 1)
            if step in DOES_PROJ:
                for k in range(6):
                    values = head_norm_values(k, 1 - par)
                    normalise(k, ND + 6 * (b + 1) + k, values, values if k < T else packed_k(k))
                pool.wait_ge(vr_ld, 16 * HH * (b + 2))
                if step in DOES_ATTN:
                    pool.wait_ge(full[u.bank(step, "PV3")], u.count(step, "PV3", b) + 1)
                pool.tensor_tensor(vbd[:, :], vrep[:, :], mask[:, :, :].rearrange("p a n -> p (a n)"),
                                   ALU.mult).then_inc(vbd_rdy, 1)

        walk(pool, body)

    @block.tensor
    def _(pe):
        pe.wait_ge(const, 15)
        pe.wait_ge(y_ld, 16 * B)
        bank = begin(pe, "dca", "YT", 0)
        for cc in range(CC):
            for c in range(ND):
                last = pe.transpose(bank[:, (cc * ND + c) * P:(cc * ND + c + 1) * P],
                                    ydca[:, c, cc * P:(cc + 1) * P], ident[:, :])
        last.then_inc(full[u.bank("dca", "YT")], 1)
        wait_evac(pe, "dca", "YT", 0)
        pe.wait_ge(prep, 14)
        for c in range(ND):
            for half, name in enumerate((f"DK{c}", f"DV{c}")):
                bank = begin(pe, "dca", name, 0)
                for cc in range(CC):
                    last = pe.matmul(bank[:, :], ydT[:, cc, c * P:(c + 1) * P],
                                     wdca[:, cc, half * D:(half + 1) * D],
                                     start=(cc == 0), stop=(cc == CC - 1))
                last.then_inc(full[u.bank("dca", name)], 1)
        for j in range(2):
            bank = begin(pe, "dca", f"KD{j}", 0)
            pe.wait_ge(norm, ND)
            for g in range(2):
                for c in range(ND):
                    last = pe.transpose(bank[:, (g * ND + c) * P:(g * ND + c + 1) * P],
                                        q1[:, c, (2 * j + g) * P:(2 * j + g + 1) * P], ident[:, :])
            last.then_inc(full[u.bank("dca", f"KD{j}")], 1)

        def x_transposes(step, b):
            pe.wait_ge(xh_rdy, T * (b + 2))
            for j in range(2):
                bank = begin(pe, step, f"XT{j}", b)
                for k in range(2):
                    for t in range(T):
                        last = pe.transpose(bank[:, (k * T + t) * P:(k * T + t + 1) * P],
                                            xh[:, t, (2 * j + k) * P:(2 * j + k + 1) * P], ident[:, :])
                last.then_inc(full[u.bank(step, f"XT{j}")], 1)
            pe.wait_ge(c_ld, 16 * (b + 2))
            bank = begin(pe, step, "CT", b)
            for cc in range(CC):
                for c in range(NC):
                    last = pe.transpose(bank[:, cc * KEYS + c * CK:cc * KEYS + (c + 1) * CK],
                                        cin[0:CK, c, cc * P:(cc + 1) * P], ident[0:CK, 0:CK])
            last.then_inc(full[u.bank(step, "CT")], 1)

        def project(step, b, k):
            name = GEMM[k]
            bank = begin(pe, step, name, b)
            if k < T:
                wait_evac(pe, step, "XT0", b)
                wait_evac(pe, step, "XT1", b)
                for kc in range(KC):
                    last = pe.matmul(bank[:, :], xT[:, kc, k * P:(k + 1) * P], wq[:, kc, :],
                                     start=(kc == 0), stop=(kc == KC - 1))
            else:
                c, half = (k - T) // 2, (k - T) % 2
                wait_evac(pe, step, "CT", b)
                for cc in range(CC):
                    last = pe.matmul(bank[0:CK, :], cT[:, cc, c * CK:(c + 1) * CK],
                                     wkv[:, cc, half * D:(half + 1) * D],
                                     start=(cc == 0), stop=(cc == CC - 1))
            last.then_inc(full[u.bank(step, name)], 1)

        def q_transposes(step, b, j):
            bank = begin(pe, step, f"QT{j}", b)
            pe.wait_ge(norm, ND + 6 * (b + 1) + T)
            for g in range(2):
                for t in range(T):
                    last = pe.transpose(bank[:, g * S + t * P:g * S + (t + 1) * P],
                                        q1[:, t, (2 * j + g) * P:(2 * j + g + 1) * P], ident[:, :])
            last.then_inc(full[u.bank(step, f"QT{j}")], 1)

        def k_transposes(step, b):
            pe.wait_ge(norm, ND + 6 * (b + 2))
            for j in range(2):
                bank = begin(pe, step, f"KT{j}", b)
                for g in range(2):
                    for c in range(NC):
                        last = pe.transpose(bank[:, g * KEYS + c * CK:g * KEYS + (c + 1) * CK],
                                            kn[0:CK, c, (2 * j + g) * P:(2 * j + g + 1) * P],
                                            ident[0:CK, 0:CK])
                last.then_inc(full[u.bank(step, f"KT{j}")], 1)

        def dca_scores(step, b, par):
            bank = begin(pe, step, "SD", b)
            pe.wait_ge(split, 4 * b + 1)
            pe.wait_ge(kd_rdy, b + 1)
            for t in range(T):
                for g in range(G):
                    o = (t * G + g) * HP * DCA
                    last = pe.matmul(bank[:, o:o + HP * DCA], qf[par][:, g, t * P:(t + 1) * P],
                                     kdb[:, g, :], start=True, stop=True)
            last.then_inc(full[u.bank(step, "SD")], 1)

        def scores(b, par, k):
            if k == 0:
                pe.wait_ge(q_in, STACKED * (b + 1))
                pe.wait_ge(k_in, STACKED * (b + 1))
            wait(pe, sc_evac[k % 2], 8 * b + k // 2)
            t, quad = k // G, k % G
            for i in range(HP):
                h = quad * HP + i
                last = pe.matmul(sc[k % 2][:, i // 2, (i % 2) * KEYS:(i % 2 + 1) * KEYS],
                                 QS[par][0:BLK, h, t * P:(t + 1) * P], KS[par][0:BLK, h, :],
                                 start=True, stop=True)
            last.then_inc(sc_full[k % 2], 1)

        def shift_transposes(step, b):
            bank = begin(pe, step, "LT", b)
            pe.wait_ge(lt_rdy, b + 1)
            for t in range(T):
                last = pe.transpose(bank[0:2 * H, t * P:(t + 1) * P], lt[:, t, :], ident[:, :])
            last.then_inc(full[u.bank(step, "LT")], 1)

        def dca_scores_t(step, b, par):
            bank = begin(pe, step, "SDT", b)
            wait_evac(pe, step, "LT", b)
            for a in range(2):
                cols = bank[:, a * S:(a + 1) * S]
                pe.matmul(cols, sel[:, a, :], s_hi[:, :], start=True, stop=False, skip_group_check=True)
                pe.matmul(cols, sel[:, a, :], s_lo[:, :], start=False, stop=False, skip_group_check=True)
                for g in range(2):
                    last = pe.matmul(bank[g * 64:(g + 1) * 64, a * S:(a + 1) * S],
                                     kdb[:, 2 * a + g, :], qf[par][:, 2 * a + g, :],
                                     start=False, stop=True, skip_group_check=True)
            last.then_inc(full[u.bank(step, "SDT")], 1)

        def scores_t(b, par, p):
            if p == 0:
                pe.wait_ge(sh_in, 32 * (b + 1))
                pe.wait_ge(ones, 2)
            pe.wait_ge(sc_evac[p % 2], 8 * b + 4 + p // 2)
            for i in range(2):
                for c in range(NC):
                    last = pe.matmul(sc[p % 2][0:CK, i, c * S:(c + 1) * S],
                                     KS[par][:, 2 * p + i, c * CK:(c + 1) * CK],
                                     QS[par][:, 2 * p + i, :], start=True, stop=True)
            last.then_inc(sc_full[p % 2], 1)

        def values(step, b, par, g):
            bank = begin(pe, step, f"PV{g}", b)
            for i in range(2):
                pe.wait_ge(sc_evac[i], 8 * b + 4 + g + 1)
            for c in range(NC):
                for i in range(HP):
                    h = g * HP + i
                    pe.matmul(bank[i * HD:(i + 1) * HD, 0:S],
                              kv1[par][0:CK, c, h // HH, h % HH, HD:W],
                              pt[g % 2][0:CK, i, c * S:(c + 1) * S],
                              start=(c == 0), stop=False, skip_group_check=True)
            if g == 0:
                wait_evac(pe, step, "SDT", b)
                pe.wait_ge(vbd_rdy, b + 1)
            pe.matmul(bank[:, 0:S], vbd[:, g * P:(g + 1) * P], pdt[:, g // 2, :],
                      start=False, stop=True, skip_group_check=True
                      ).then_inc(full[u.bank(step, f"PV{g}")], 1)

        def out_projection(step, b, t):
            bank = begin(pe, step, f"WO{t}", b)
            for g in range(G):
                last = pe.matmul(bank[:, :], ot[:, g, t * P:(t + 1) * P], wo[:, g, :],
                                 start=(g == 0), stop=(g == G - 1))
            last.then_inc(full[u.bank(step, f"WO{t}")], 1)

        def body(step, b, par):
            attn, proj, wout = step in DOES_ATTN, step in DOES_PROJ, step in DOES_WO
            if attn:
                dca_scores(step, b, par)
                scores(b, par, 0)
                scores(b, par, 1)
            if wout:
                if attn:
                    wait_evac(pe, step, "SD", b)
                else:
                    wait_evac(pe, "last", "PV3", B - 1)
                out_projection(step, b, 0)
            if attn:
                scores(b, par, 2)
            if wout:
                out_projection(step, b, 1)
            if attn:
                scores(b, par, 3)
            if proj:
                x_transposes(step, b)
            if attn:
                scores(b, par, 4)
            if proj:
                project(step, b, 0)
            if attn:
                scores(b, par, 5)
            if proj:
                project(step, b, 1)
            if attn:
                scores(b, par, 6)
                scores(b, par, 7)
            if proj:
                project(step, b, 2)
            if attn:
                shift_transposes(step, b)
            if proj:
                project(step, b, 3)
                project(step, b, 4)
                q_transposes(step, b, 0)
                project(step, b, 5)
                q_transposes(step, b, 1)
            if attn:
                dca_scores_t(step, b, par)
                for p in range(4):
                    scores_t(b, par, p)
                values(step, b, par, 0)
                scores_t(b, par, 4)
                scores_t(b, par, 5)
                values(step, b, par, 1)
            if proj:
                k_transposes(step, b)
            if attn:
                scores_t(b, par, 6)
                scores_t(b, par, 7)
                values(step, b, par, 2)
                values(step, b, par, 3)

        walk(pe, body)

    @block.scalar
    def _(act):
        for b in range(B):
            act.dma_start(ydca[(b % BD) * DCA:(b % BD + 1) * DCA, b // BD, :],
                          ctx[b, KEYS:KEYS + DCA, :]).then_inc(y_ld, 16)
        for n, vec in enumerate((qn_w, qn_b, kn_w, kn_b, kd_w, kd_b)):
            for h in range(HP):
                act.dma_start(affine[h * HD:(h + 1) * HD, n:n + 1], vec.unsqueeze(1)).then_inc(w_ld, 16)

        def copy_out(step, b, name, dst, cols):
            bank = wait_full(act, step, name, b)
            act.activation(dst, bank[:, 0:cols].rearrange("p (a n) -> p a n", a=dst.shape[1]),
                           ACT.Copy).then_inc(taken(step, name), 1)

        def square(step, b, name, n, values):
            wait_evac(act, step, name, b)
            wait(act, var_rdy, n - 1)
            act.activation(squares(n, values), values, ACT.Square, scale=HD ** -0.5).then_inc(sq_rdy, 1)

        def affine_out(step, b, name, dst, cols, n):
            bank = wait_full(act, step, name, b)
            act.activation(dst, bank[:, 0:cols].rearrange("p (a n) -> p a n", a=2), ACT.Identity,
                           bias=affine[:, n + 1:n + 2], scale=affine[:, n:n + 1]
                           ).then_inc(taken(step, name), 1)

        copy_out("dca", 0, "YT", ydT, CC * ND * P)
        act.wait_ge(w_ld, 16 * 34)
        act.wait_ge(const, 15)
        for c in range(ND):
            square("dca", 0, f"DK{c}", c, q1[:, c, :].rearrange("p (h d) -> p h d", h=H))
        for j in range(2):
            affine_out("dca", 0, f"KD{j}", kdT[:, 2 * j:2 * j + 2, :], 2 * ND * P, 4)

        def exps(b, k):
            act.wait_ge(g_max, 16 * b + 2 * k + 2)
            t, quad = k // G, k % G
            for i in range(HP):
                h = quad * HP + i
                s = sc[k % 2][:, i // 2, (i % 2) * KEYS:(i % 2 + 1) * KEYS]
                last = act.activation(s, s, ACT.Exp, bias=nm[:, t, h:h + 1], scale=SCALE,
                                      accum_out=den[:, t, h:h + 1])
            last.then_inc(sc_evac[k % 2], 1)

        def probabilities(step, b, p):
            g = p // 2
            act.wait_ge(sc_full[p % 2], 8 * b + 4 + p // 2 + 1)
            if g >= 2 and p % 2 == 0:
                wait_full(act, step, f"PV{g - 2}", b)
            act.activation(pt[g % 2][0:CK, (p % 2) * 2:(p % 2) * 2 + 2, :], sc[p % 2][0:CK, :, :],
                           ACT.Exp, scale=SCALE).then_inc(sc_evac[p % 2], 1)

        def body(step, b, par):
            attn, proj = step in DOES_ATTN, step in DOES_PROJ
            n = ND + 6 * (b + 1)

            def sq_unit(k):
                values = head_norm_values(k, 1 - par)
                wait_evac(act, step, GEMM[k], b)
                act.wait_ge(var_rdy, n + k - 1)
                act.activation(squares(k, values), values, ACT.Square, scale=HD ** -0.5).then_inc(sq_rdy, 1)

            if attn:
                wait_evac(act, step, "SD", b)
                act.activation(ed[:, :, :, :], ed[:, :, :, :], ACT.Exp, scale=SCALE).then_inc(d_exp, 1)
                for k in range(4):
                    exps(b, k)
            if proj:
                copy_out(step, b, "XT0", xT[:, 0:2, :], 2 * S)
                copy_out(step, b, "XT1", xT[:, 2:4, :], 2 * S)
                copy_out(step, b, "CT", cT[:, :, :], CC * KEYS)
            if attn:
                exps(b, 4)
                exps(b, 5)
            if proj:
                sq_unit(0)
            if attn:
                exps(b, 6)
            if proj:
                sq_unit(1)
            if attn:
                exps(b, 7)
                act.wait_ge(d_den, b + 1)
                for i in range(2):
                    act.wait_ge(sc_evac[i], 8 * b + 4)
                act.activation(ld[:, :, :], den[:, :, :], ACT.Ln).then_inc(ln_rdy, 1)
            if proj:
                sq_unit(2)
                sq_unit(3)
                affine_out(step, b, "QT0", qf[1 - par][:, 0:2, :], 2 * S, 0)
                sq_unit(4)
                affine_out(step, b, "QT1", qf[1 - par][:, 2:4, :], 2 * S, 0)
                sq_unit(5)
            if attn:
                bank = wait_full(act, step, "SDT", b)
                act.activation(pdt[:, :, :], bank[:, :].rearrange("p (a n) -> p a n", a=2), ACT.Exp,
                               scale=SCALE).then_inc(taken(step, "SDT"), 1)
                for p in range(6):
                    probabilities(step, b, p)
            if proj:
                wait(act, split, 4 * (b + 1))
                affine_out(step, b, "KT0", kf[:, 0:2, :], 2 * KEYS, 2)
                affine_out(step, b, "KT1", kf[:, 2:4, :], 2 * KEYS, 2)
            if attn:
                for p in range(6, 8):
                    probabilities(step, b, p)

        walk(act, body)

    @block.vector
    def _(dve):
        for i in range(2):
            dve.memset(KS[i][BLK:ST, :, :].bitcast(F32), 1.0).then_inc(ones, 1)
        dve.wait_ge(w_ld, 16 * 34)
        dve.wait_ge(const, 15)
        heads = (
            wdca[:, 0, 0:D].rearrange("p (h d) -> p h d", d=HD),
            wdca[:, 1, 0:D].rearrange("p (h d) -> p h d", d=HD),
            bd_b[:, 0:D].rearrange("p (h d) -> p h d", d=HD),
            wq[:, :, :].rearrange("p c (h d) -> p (c h) d", d=HD),
            wkv[:, :, :].rearrange("p c (h w) -> p (c h) w", w=W)[:, :, 0:HD],
            bq_b[:, :].rearrange("p (h d) -> p h d", d=HD),
        )
        bk_heads = bkv_b[:, :].rearrange("p (h w) -> p h w", w=W)[:, :, 0:HD]
        for n, w in enumerate(heads + (bk_heads,)):
            sums = wsum[:, 0:w.shape[1]]
            dve.tensor_reduce(sums, w, AX_X, ALU.add).then_inc(prep, 1)
            dve.wait_ge(prep, 2 * n + 1)
            dve.scalar_tensor_tensor(w, sums.unsqueeze(2).broadcast_to(w.shape), -1.0 / HD, w,
                                     ALU.mult, ALU.add).then_inc(prep, 1)
            dve.wait_ge(prep, 2 * n + 2)

        def sum_squares(k, n, values):
            dve.wait_ge(sq_rdy, n + 1)
            dve.tensor_reduce(vs[0:values.shape[0], k, 0:values.shape[1]], squares(k, values), AX_X,
                              ALU.add).then_inc(var_rdy, 1)

        for c in range(ND):
            for dst, name, half in ((q1[:, c, :], f"DK{c}", 0), (vdca[:, c, :], f"DV{c}", 1)):
                bank = wait_full(dve, "dca", name, 0)
                dve.tensor_tensor(dst, bank[:, :], bd_b[:, half * D:(half + 1) * D],
                                  ALU.add).then_inc(taken("dca", name), 1)
        for c in range(ND):
            sum_squares(c, c, q1[:, c, :].rearrange("p (h d) -> p h d", h=H))
        dve.wait_ge(norm, ND)
        dve.wait_ge(vd_st, 16 * ND)

        def row_stats(b):
            dve.wait_ge(x_ld, 16 * (b + 2))
            for t in range(T):
                dve.bn_stats(st6[:, t, :], xin[:, t, :]).then_inc(ln_st, 1)
            dve.wait_ge(ln_st, T * (b + 2))
            carry_wait(dve, scratch)
            for t in range(T):
                dve.bn_aggr(mv[:, t, :], st6[:, t, :]).then_inc(ln_ag, 1)

        def row_norm(b):
            dve.wait_ge(ln_rs, 2 * (b + 2))
            for t in range(T):
                dve.tensor_scalar(xh[:, t, :], xin[:, t, :], mv[:, t, 0:1], rs[:, t:t + 1],
                                  ALU.subtract, ALU.mult).then_inc(xh_rdy, 1)

        def group_max(b, k):
            t, quad = k // G, k % G
            dve.wait_ge(sc_full[k % 2], 8 * b + k // 2 + 1)
            s = sc[k % 2][:, :, 0:2 * KEYS].rearrange("p a (h n) -> p a h n", h=2)
            mx = mxa[:, t, quad * HP:(quad + 1) * HP]
            dve.tensor_reduce(mx.rearrange("p (a h) -> p a h", a=2), s, AX_X, ALU.max).then_inc(g_max, 1)
            dve.wait_ge(g_max, 16 * b + 2 * k + 1)
            dve.tensor_scalar(nm[:, t, quad * HP:(quad + 1) * HP], mx, -SCALE, None,
                              ALU.mult).then_inc(g_max, 1)

        def bias_out(step, b, k, par):
            bank = wait_full(dve, step, GEMM[k], b)
            if k < T:
                dst, bias, rows = q1[:, k, :], bq_b[:, :], P
            else:
                c, half = (k - T) // 2, (k - T) % 2
                dst = kv1[par][0:CK, c, half, :, :].rearrange("p h w -> p (h w)")
                bias, rows = bkv_b[0:CK, half * D:(half + 1) * D], CK
            dve.tensor_tensor(dst, bank[0:rows, :], bias, ALU.add).then_inc(taken(step, GEMM[k]), 1)

        def split_parts(step, b, n, names, whole, hi, lo, stacked):
            for name in names:
                wait_evac(dve, step, name, b)
            wait(dve, stacked, STACKED * (b + 1))
            dve.tensor_copy(hi[:, :, :], whole[:, :, :]).then_inc(split, 1)
            dve.wait_ge(split, 4 * (b + 1) + n + 1)
            dve.tensor_tensor(lo[:, :, :], whole[:, :, :], hi[:, :, :].bitcast(F32),
                              ALU.subtract).then_inc(split, 1)

        def dca_keys(b):
            for h in range(HP):
                last = dve.tensor_copy(kdb[h * HD:(h + 1) * HD, :, h * DCA:(h + 1) * DCA],
                                       kdT[h * HD:(h + 1) * HD, :, bass.ts(b, DCA)])
            last.then_inc(kd_rdy, 1)

        def ctx_out(step, b, g):
            bank = wait_full(dve, step, f"PV{g}", b)
            dve.tensor_copy(ot[:, g, :], bank[:, 0:S]).then_inc(taken(step, f"PV{g}"), 1)

        def residual(step, b, t):
            if t == 0:
                dve.wait_ge(res_rdy, b)
            bank = wait_full(dve, step, f"WO{t}", b)
            dve.tensor_tensor(xres[:, t, :], bank[:, :], xres[:, t, :],
                              ALU.add).then_inc(taken(step, f"WO{t}"), 1)

        for c in range(ND):
            wait_evac(dve, "dca", f"KD{c}", 0)

        def body(step, b, par):
            attn, proj, wout = step in DOES_ATTN, step in DOES_PROJ, step in DOES_WO
            n = ND + 6 * (b + 1)
            if attn:
                bank = wait_full(dve, step, "SD", b)
                s = bank[:, :].rearrange("p (t h k) -> p t h k", t=T, h=H)
                dve.tensor_reduce(mxa[:, :, H:2 * H], s, AX_X, ALU.max).then_inc(d_max, 1)
                dve.wait_ge(d_max, b + 1)
                dve.tensor_tensor(ed[:, :, :, :], s, mxa[:, :, H:2 * H].unsqueeze(3).broadcast_to(
                    [P, T, H, DCA]), ALU.subtract).then_inc(taken(step, "SD"), 1)
                group_max(b, 0)
            if proj:
                row_stats(b)
            if attn:
                group_max(b, 1)
                dve.wait_ge(d_exp, b + 1)
                dve.tensor_reduce(den[:, :, H:2 * H], ed[:, :, :, :], AX_X, ALU.add).then_inc(d_den, 1)
            if proj:
                row_norm(b)
            if wout:
                residual(step, b, 0)
            if attn:
                group_max(b, 2)
            if wout:
                residual(step, b, 1)
            if attn:
                group_max(b, 3)
                group_max(b, 4)
            if proj:
                bias_out(step, b, 0, 1 - par)
            if attn:
                group_max(b, 5)
            if proj:
                bias_out(step, b, 1, 1 - par)
                sum_squares(0, n, head_norm_values(0, 1 - par))
            if attn:
                group_max(b, 6)
            if proj:
                sum_squares(1, n + 1, head_norm_values(1, 1 - par))
            if attn:
                group_max(b, 7)
            if proj:
                bias_out(step, b, 2, 1 - par)
            if attn:
                dve.wait_ge(ln_rdy, b + 1)
                dve.scalar_tensor_tensor(lt[:, :, :], ld[:, :, :], -1.0 / SCALE, mxa[:, :, :],
                                         ALU.mult, ALU.subtract).then_inc(lt_rdy, 1)
                bank = wait_full(dve, step, "LT", b)
                dve.tensor_copy(s_hi[:, :], bank[0:2 * H, 0:S]).then_inc(sh_hi, 1)
                dve.wait_ge(sh_hi, b + 1)
                dve.tensor_tensor(s_lo[:, :], bank[0:2 * H, 0:S], s_hi[:, :].bitcast(F32),
                                  ALU.subtract).then_inc(taken(step, "LT"), 1)
            if proj:
                for k in range(2, 6):
                    if k > 2:
                        bias_out(step, b, k, 1 - par)
                    sum_squares(k, n + k, head_norm_values(k, 1 - par))
            if proj:
                if attn:
                    wait_evac(dve, step, "SDT", b)
                dca_keys(b + 1)
                split_parts(step, b, 0, ("QT0", "QT1"), qf[1 - par], q_hi, q_lo, q_in)
            if attn:
                ctx_out(step, b, 0)
                ctx_out(step, b, 1)
            if proj:
                split_parts(step, b, 2, ("KT0", "KT1"), kf, k_hi, k_lo, k_in)
            if attn:
                ctx_out(step, b, 2)
                ctx_out(step, b, 3)

        walk(dve, body)


def ffn_phase(nc, stack, x2_dram, gate_W, W1, b1, W2, b2, out):
    B, _, T, D = x2_dram.shape
    NE, _, FF = W1.shape
    S = T * P
    KC = D // P
    FC = -(-FF // P)
    FR = FF - (FC - 1) * P
    TOP = 2
    PAIRS = [(t, e) for t in range(T) for e in range(TOP)]
    out_t = out.rearrange("b (t p) d -> b p t d", p=P)

    def sem(name):
        return stack.enter_context(nc.semaphore(name))

    def sb(name, shape, dt=F32):
        return stack.enter_context(nc.sbuf_tensor(name, shape, dt))

    ident = sb("f_ident", [P, P])
    w1 = sb("w1", [P, NE, KC, FF])
    w2 = sb("w2", [P, NE, FC, D])
    b1_b = sb("b1_b", [P, NE, FF])
    b2_b = sb("b2_b", [P, NE, D])
    gate = sb("gate", [P, KC, NE])
    neg_half, eps_ln = sb("f_neg_half", [P, T]), sb("f_eps_ln", [P, T])
    scratch = sb("f_scratch", [P, 2])
    euler = sb("euler", [P, 1])
    x2 = [sb(f"x2_{i}", [P, T, D]) for i in range(2)]
    xh = sb("f_xh", [P, T, D])
    xT = [sb(f"f_xT{i}", [P, KC, S]) for i in range(2)]
    xsum = sb("xsum", [P, KC])
    st6, mv, rs = sb("f_st6", [P, T, 6]), sb("f_mv", [P, T, 2]), sb("f_rs", [P, T])
    lg = sb("lg", [P, 8])
    top = sb("top", [P, 8])
    idx = [sb(f"idx{i}", [P, 8], U32) for i in range(2)]
    gd = sb("gd", [P, 2])
    gv = [sb(f"gv{i}", [P, TOP]) for i in range(2)]
    hb = sb("hb", [P, len(PAIRS), FF])
    hT = sb("hT", [P, TOP, FC, S])

    ring = [stack.enter_context(nc.psum_tensor(f"f_ring{i}", [P, BANK], F32)) for i in range(8)]
    full = [sem(f"f_full{i}") for i in range(8)]
    evac = [sem(f"f_evac{i}") for i in range(8)]
    w_ld, o_st = sem("f_w_ld"), [sem("o_st0"), sem("o_st1")]
    x_ld = [sem("f_x_ld0"), sem("f_x_ld1")]
    const, ln_st, ln_ag, ln_rs, xh_rdy = (sem("f_" + n) for n in "const ln_st ln_ag ln_rs xh_rdy".split())
    g_log, g_pick, g_pow, g_val = sem("g_log"), sem("g_pick"), sem("g_pow"), sem("g_val")
    h_rdy, res = sem("h_rdy"), sem("res")

    BODY = ["XT0", "XT1", "H0", "H1", "H2", "H3", "GT", "HT0", "HT1", "HR", "OUT0", "OUT1"]
    NEXT = ["XT0", "XT1", "GT"]
    u = Units(8, [("pro", NEXT, -1, 1), ("first", BODY, 0, 1), ("body", BODY, 1, B - 2),
                  ("last", [n for n in BODY if n not in NEXT], B - 1, 1)])
    DOES_FFN, DOES_NEXT = ("first", "body", "last"), ("pro", "first", "body")

    def begin(eng, step, name, b):
        wait(eng, evac[u.bank(step, name)], u.count(step, name, b))
        return ring[u.bank(step, name)]

    def taken(step, name):
        return evac[u.bank(step, name)]

    def wait_full(eng, step, name, b):
        eng.wait_ge(full[u.bank(step, name)], u.count(step, name, b) + 1)
        return ring[u.bank(step, name)]

    def wait_evac(eng, step, name, b):
        eng.wait_ge(evac[u.bank(step, name)], u.count(step, name, b) + 1)

    def walk(eng, body):
        body("pro", -1, 1, 0)
        body("first", 0, 0, 0)
        with eng.Fori(0, (B - 2) // 2) as i:
            body("body", 2 * i + 1, 1, i)
            body("body", 2 * i + 2, 0, i + 1)
        body("last", B - 1, 1, (B - 2) // 2)

    LOADS = 16 * (KC + 5 * NE)
    block = stack.enter_context(nc.Block())

    @block.sync
    def _(sp):
        def load(b, par, half):
            if not isinstance(half, int) or half != 0:
                sp.wait_ge(o_st[par], 16 * half)
            sp.dma_start(x2[par][:, :, :], x2_dram[b]).then_inc(x_ld[par], 16)

        load(0, 0, 0)
        for c in range(KC):
            sp.dma_start(gate[:, c, :], gate_W[:, c * P:(c + 1) * P].rearrange("e p -> p e"),
                         allow_slow_non_contiguous=True).then_inc(w_ld, 16)
        for e in range(NE):
            sp.dma_start(w1[:, e, :, :], W1[e].rearrange("(c p) f -> p c f", p=P)).then_inc(w_ld, 16)
            sp.dma_start(b1_b[:, e, :], b1[e].partition_broadcast(P)).then_inc(w_ld, 16)
        for e in range(NE):
            sp.dma_start(w2[:, e, 0:FC - 1, :],
                         W2[e, 0:(FC - 1) * P].rearrange("(c p) n -> p c n", p=P)).then_inc(w_ld, 16)
            sp.dma_start(w2[0:FR, e, FC - 1, :], W2[e, (FC - 1) * P:FF]).then_inc(w_ld, 16)
            sp.dma_start(b2_b[:, e, :], b2[e].partition_broadcast(P)).then_inc(w_ld, 16)

        def body(step, b, par, half):
            if step in ("first", "body"):
                load(b + 1, 1 - par, half + par)
            if step in DOES_FFN:
                wait_evac(sp, step, f"OUT{T - 1}", b)
                sp.dma_start(out_t[b], x2[par][:, :, :]).then_inc(o_st[par], 16)

        walk(sp, body)
        for par in range(2):
            sp.wait_ge(o_st[par], 16 * (B // 2))

    @block.gpsimd
    def _(pool):
        pool.memset(ident[:, :], 0.0).then_inc(const, 1)
        pool.memset(neg_half[:, :], -0.5).then_inc(const, 1)
        pool.memset(euler[:, :], EULER).then_inc(const, 1)
        pool.memset(lg[:, :], LEAST).then_inc(const, 1)
        pool.memset(eps_ln[:, :], EPS_LN).then_inc(const, 1)
        pool.memset(scratch[:, :], 0.0).then_inc(const, 1)
        pool.wait_ge(const, 6)
        pool.affine_select(out=ident[:, :], in_=ident[:, :], compare_op=ALU.not_equal, fill=1.0,
                           base=0, pattern=[[-1, P]], channel_multiplier=1).then_inc(const, 1)

        def body(step, b, par, half):
            if step in DOES_NEXT:
                pool.wait_ge(ln_ag, T * (b + 2))
                pool.tensor_tensor(rs[:, :], mv[:, :, 1], eps_ln[:, :], ALU.add).then_inc(ln_rs, 1)
                pool.wait_ge(ln_rs, 2 * (b + 1) + 1)
                pool.tensor_tensor(rs[:, :], rs[:, :], neg_half[:, :], ALU.pow).then_inc(ln_rs, 1)
                pool.wait_ge(g_pick, 3 * (b + 2))
                pool.tensor_tensor(gd[:, 1:2], euler[:, :], gd[:, 0:1], ALU.pow).then_inc(g_pow, 1)

        walk(pool, body)

    @block.tensor
    def _(pe):
        pe.wait_ge(const, 7)
        pe.wait_ge(w_ld, LOADS)

        def body(step, b, par, half):
            if step in DOES_FFN:
                pe.wait_ge(g_val, 2 * (b + 1))
            if step in DOES_NEXT:
                pe.wait_ge(xh_rdy, T * (b + 2))
                for j in range(2):
                    bank = begin(pe, step, f"XT{j}", b)
                    for k in range(2):
                        for t in range(T):
                            last = pe.transpose(bank[:, (k * T + t) * P:(k * T + t + 1) * P],
                                                xh[:, t, (2 * j + k) * P:(2 * j + k + 1) * P], ident[:, :])
                    last.then_inc(full[u.bank(step, f"XT{j}")], 1)
            if step in DOES_FFN:
                ex = [pe.value_load(idx[par][0:1, e:e + 1], min_val=0, max_val=NE - 1) for e in range(TOP)]
                for n, (t, e) in enumerate(PAIRS):
                    bank = begin(pe, step, f"H{n}", b)
                    for kc in range(KC):
                        last = pe.matmul(bank[:, 0:FF], xT[par][:, kc, t * P:(t + 1) * P],
                                         w1[:, bass.ds(ex[e], 1), kc, :].rearrange("p a f -> p (a f)"),
                                         start=(kc == 0), stop=(kc == KC - 1))
                    last.then_inc(full[u.bank(step, f"H{n}")], 1)
            if step in DOES_FFN:
                for e in range(TOP):
                    bank = begin(pe, step, f"HT{e}", b)
                    for t in range(T):
                        if e == 0:
                            pe.wait_ge(h_rdy, len(PAIRS) * b + TOP * t + 2)
                        for fc in range(FC - 1):
                            last = pe.transpose(bank[:, fc * S + t * P:fc * S + (t + 1) * P],
                                                hb[:, TOP * t + e, fc * P:(fc + 1) * P], ident[:, :])
                    last.then_inc(full[u.bank(step, f"HT{e}")], 1)
                bank = begin(pe, step, "HR", b)
                for e in range(TOP):
                    for t in range(T):
                        last = pe.transpose(bank[0:FR, e * S + t * P:e * S + (t + 1) * P],
                                            hb[:, TOP * t + e, (FC - 1) * P:FF], ident[:, :])
                last.then_inc(full[u.bank(step, "HR")], 1)
            if step in DOES_NEXT:
                bank = begin(pe, step, "GT", b)
                for j in range(2):
                    wait_evac(pe, step, f"XT{j}", b)
                for kc in range(KC):
                    last = pe.matmul(bank[:, 0:NE], xsum[:, kc:kc + 1].broadcast_to([P, P]),
                                     gate[:, kc, :], start=(kc == 0), stop=(kc == KC - 1))
                last.then_inc(full[u.bank(step, "GT")], 1)
            if step in DOES_FFN:
                for e in range(TOP):
                    wait_evac(pe, step, f"HT{e}", b)
                wait_evac(pe, step, "HR", b)
                for t in range(T):
                    bank = begin(pe, step, f"OUT{t}", b)
                    for e in range(TOP):
                        for fc in range(FC):
                            rows = P if fc < FC - 1 else FR
                            last = pe.matmul(bank[:, :], hT[0:rows, e, fc, t * P:(t + 1) * P],
                                             w2[0:rows, bass.ds(ex[e], 1), fc, :].rearrange("p a n -> p (a n)"),
                                             start=(e == 0 and fc == 0),
                                             stop=(e == TOP - 1 and fc == FC - 1))
                    last.then_inc(full[u.bank(step, f"OUT{t}")], 1)

        walk(pe, body)

    @block.scalar
    def _(act):
        def body(step, b, par, half):
            if step in DOES_NEXT:
                for j in range(2):
                    bank = wait_full(act, step, f"XT{j}", b)
                    for k in range(2):
                        last = act.activation(xT[1 - par][:, 2 * j + k, :], bank[:, k * S:(k + 1) * S],
                                              ACT.Copy, accum_out=xsum[:, 2 * j + k:2 * j + k + 1])
                    last.then_inc(taken(step, f"XT{j}"), 1)
            if step in DOES_FFN:
                for n in range(len(PAIRS)):
                    wait_evac(act, step, f"H{n}", b)
                    act.activation(hb[:, n, :], hb[:, n, :], ACT.Gelu).then_inc(h_rdy, 1)
                act.wait_ge(g_val, 2 * (b + 1))
                for e in range(TOP):
                    bank = wait_full(act, step, f"HT{e}", b)
                    act.activation(hT[:, e, 0:FC - 1, :], bank[:, :].rearrange("p (c n) -> p c n", n=S),
                                   ACT.Copy, scale=gv[par][:, e:e + 1]).then_inc(taken(step, f"HT{e}"), 1)
                bank = wait_full(act, step, "HR", b)
                for e in range(TOP):
                    last = act.activation(hT[0:FR, e, FC - 1, :], bank[0:FR, e * S:(e + 1) * S],
                                          ACT.Copy, scale=gv[par][0:FR, e:e + 1])
                last.then_inc(taken(step, "HR"), 1)

        walk(act, body)

    @block.vector
    def _(dve):
        dve.wait_ge(w_ld, LOADS)
        dve.wait_ge(const, 7)

        def body(step, b, par, half):
            if step in DOES_NEXT:
                nxt = 1 - par
                dve.wait_ge(x_ld[nxt], 16 * (half + par + 1) if step != "pro" else 16)
                for t in range(T):
                    dve.bn_stats(st6[:, t, :], x2[nxt][:, t, :]).then_inc(ln_st, 1)
                dve.wait_ge(ln_st, T * (b + 2))
                carry_wait(dve, scratch)
                for t in range(T):
                    dve.bn_aggr(mv[:, t, :], st6[:, t, :]).then_inc(ln_ag, 1)
                dve.wait_ge(ln_rs, 2 * (b + 2))
                for t in range(T):
                    dve.tensor_scalar(xh[:, t, :], x2[nxt][:, t, :], mv[:, t, 0:1], rs[:, t:t + 1],
                                      ALU.subtract, ALU.mult).then_inc(xh_rdy, 1)
            if step in DOES_FFN:
                ex = [dve.value_load(idx[par][0:1, e:e + 1], min_val=0, max_val=NE - 1) for e in range(TOP)]
                for n, (t, e) in enumerate(PAIRS):
                    bank = wait_full(dve, step, f"H{n}", b)
                    dve.tensor_tensor(hb[:, n, :], bank[:, 0:FF],
                                      b1_b[:, bass.ds(ex[e], 1), :].rearrange("p a f -> p (a f)"),
                                      ALU.add).then_inc(taken(step, f"H{n}"), 1)
                for e in range(TOP):
                    for t in range(T):
                        last = dve.scalar_tensor_tensor(
                            x2[par][:, t, :], b2_b[:, bass.ds(ex[e], 1), :].rearrange("p a n -> p (a n)"),
                            gv[par][:, e:e + 1], x2[par][:, t, :], ALU.mult, ALU.add)
                        last.then_inc(res, 1)
                    dve.wait_ge(res, 2 * T * b + T * (e + 1))
            if step in DOES_NEXT:
                nxt = 1 - par
                bank = wait_full(dve, step, "GT", b)
                dve.tensor_scalar(lg[:, 0:NE], bank[:, 0:NE], 1.0 / S, None,
                                  ALU.mult).then_inc(taken(step, "GT"), 1)
                wait_evac(dve, step, "GT", b)
                carry_wait(dve, scratch)
                dve.max(top[:, :], lg[:, :]).then_inc(g_pick, 1)
                dve.wait_ge(g_pick, 3 * (b + 1) + 1)
                carry_wait(dve, scratch)
                dve.max_index(idx[nxt][:, :], top[:, :], lg[:, :]).then_inc(g_pick, 1)
                dve.tensor_tensor(gd[:, 0:1], top[:, 1:2], top[:, 0:1], ALU.subtract).then_inc(g_pick, 1)
                dve.wait_ge(g_pow, b + 2)
                dve.tensor_scalar(gd[:, 0:1], gd[:, 1:2], 1.0, None, ALU.add).then_inc(g_log, 1)
                dve.wait_ge(g_log, b + 2)
                dve.reciprocal(gv[nxt][:, 0:1], gd[:, 0:1]).then_inc(g_val, 1)
                dve.wait_ge(g_val, 2 * (b + 1) + 1)
                dve.tensor_tensor(gv[nxt][:, 1:2], gv[nxt][:, 0:1], gd[:, 1:2], ALU.mult).then_inc(g_val, 1)
                dve.wait_ge(g_val, 2 * (b + 2))
            if step in DOES_FFN:
                for t in range(T):
                    bank = wait_full(dve, step, f"OUT{t}", b)
                    dve.tensor_tensor(x2[par][:, t, :], bank[:, :], x2[par][:, t, :],
                                      ALU.add).then_inc(taken(step, f"OUT{t}"), 1)

        walk(dve, body)


_INS = ['x', 'ctx_1024', 'L0_xattn_Wq', 'L0_xattn_bq', 'L0_xattn_Wk', 'L0_xattn_bk', 'L0_xattn_Wv',
        'L0_xattn_bv', 'L0_xattn_Wkv_dca', 'L0_xattn_bkv_dca', 'L0_xattn_qn_w', 'L0_xattn_qn_b',
        'L0_xattn_kn_w', 'L0_xattn_kn_b', 'L0_xattn_kn_dca_w', 'L0_xattn_kn_dca_b', 'L0_xattn_Wo',
        'L0_xattn_bo', 'L0_ffn_gate_W', 'L0_ffn_W1', 'L0_ffn_b1', 'L0_ffn_W2', 'L0_ffn_b2']
_OUTS = [((16, 256, 512), 'float32')]


def kernel(**inputs):
    import numpy as _np
    import concourse.bacc as _bacc
    from concourse import mybir as _mybir
    from concourse.bass_utils import run_bass_kernel_spmd as _run

    nc = _bacc.Bacc("TRN2", target_bir_lowering=False, num_devices=1)
    arrays, args = {}, []
    for name in _INS:
        a = _np.ascontiguousarray(inputs[name])
        arrays[f"in_{name}_dram"] = a
        args.append(nc.dram_tensor(f"in_{name}_dram", a.shape, _mybir.dt.from_np(a.dtype), kind="ExternalInput").ap())
    for i, (shape, dtype) in enumerate(_OUTS):
        dt = _mybir.dt.from_np(_np.dtype(dtype))
        args.append(nc.dram_tensor(f"out_{i}_dram", shape, dt, kind="ExternalOutput").ap())
    bass_xattn_moe(nc, *args)
    r = _run(nc, [arrays], core_ids=[0])
    got = tuple(r.results[0][f"out_{i}_dram"] for i in range(len(_OUTS)))
    return got[0]
```

```python
from contextlib import ExitStack

import numpy as np
import concourse.bass as bass
from concourse import mybir

F32 = mybir.dt.float32
F32R = mybir.dt.float32r
U32 = mybir.dt.uint32
ALU = mybir.AluOpType
ACT = mybir.ActivationFunctionType
AX_X = mybir.AxisListType.X

P = 128
BANK = 512
H = 16
HD = 32
HP = P // HD
DCA = 16
SCALE = HD ** -0.5
EPS_LN = 1e-5
EPS_QK = 1e-6
EULER = float(np.e)
LEAST = -3.0e38


class Units:

    def __init__(self, banks, steps):
        self.place, self.slope, self.first = {}, {}, {}
        base = [0] * banks
        for step, names, first_b, times in steps:
            per = [len(range(k, len(names), banks)) for k in range(banks)]
            for n, name in enumerate(names):
                self.place[step, name] = (n % banks, base[n % banks] + n // banks)
            self.slope[step], self.first[step] = per, first_b
            base = [base[k] + per[k] * times for k in range(banks)]

    def bank(self, step, name):
        return self.place[step, name][0]

    def count(self, step, name, b):
        k, n = self.place[step, name]
        return (b - self.first[step]) * self.slope[step][k] + n


def wait(eng, sem, value):
    if not isinstance(value, int) or value > 0:
        eng.wait_ge(sem, value)


def bass_xattn_moe(nc, x, ctx, Wq, bq, Wk, bk, Wv, bv, Wdca, bdca, qn_w, qn_b, kn_w, kn_b,
                   kd_w, kd_b, Wo, bo, gate_W, W1, b1, W2, b2, out):
    B, S, D = x.shape
    x2_dram = nc.dram_tensor("x2_scratch", (B, P, S // P, D), F32, kind="Internal").ap()
    vd_dram = nc.dram_tensor("vdca_scratch", (B, DCA, D), F32, kind="Internal").ap()
    with ExitStack() as stack:
        attention_phase(nc, stack, x, ctx, Wq, bq, Wk, bk, Wv, bv, Wdca, bdca, qn_w, qn_b, kn_w,
                        kn_b, kd_w, kd_b, Wo, bo, x2_dram, vd_dram)
    with ExitStack() as stack:
        ffn_phase(nc, stack, x2_dram, gate_W, W1, b1, W2, b2, out)


def carry_wait(dve, scratch):
    return dve.tensor_copy(scratch[:, 0:1], scratch[:, 1:2])


def attention_phase(nc, stack, x, ctx, Wq, bq, Wk, bk, Wv, bv, Wdca, bdca, qn_w, qn_b, kn_w, kn_b,
                    kd_w, kd_b, Wo, bo, x2_dram, vd_dram):
    B, S, D = x.shape
    KD = ctx.shape[2]
    KEYS = ctx.shape[1] - DCA
    T = S // P
    KC = D // P
    CC = KD // P
    NC = 2
    CK = KEYS // NC
    G = H // HP
    HH = H // 2
    W = 2 * HD
    BLK = 3 * HD
    ST = BLK + 2
    STACKED = 3 * 16
    ND = 2
    BD = B // ND

    x_t = x.rearrange("b (t p) d -> b p t d", p=P)
    ctx_main = ctx[:, 0:KEYS, :].rearrange("b (c p) d -> b p c d", p=CK)

    def sem(name):
        return stack.enter_context(nc.semaphore(name))

    def sb(name, shape, dt=F32):
        return stack.enter_context(nc.sbuf_tensor(name, shape, dt))

    ident = sb("ident", [P, P])
    wq = sb("wq", [P, KC, D])
    wkv = sb("wkv", [P, CC, 2 * D])
    wo = sb("wo", [P, KC, D])
    bq_b = sb("bq_b", [P, D])
    bkv_b = sb("bkv_b", [P, 2 * D])
    bo_b = sb("bo_b", [P, D])
    affine = sb("affine", [P, 6])
    sel = sb("sel", [2 * H, 2, P], F32R)
    own = sb("own", [P, HP])
    mask = sb("mask", [P, 2, HH * HD])
    neg_half = sb("neg_half", [P, H])
    eps_ln = sb("eps_ln", [P, T])
    scratch = sb("scratch", [P, 2])
    xin = sb("xin", [P, T, D])
    xh = sb("xh", [P, T, D])
    xT = sb("xT", [P, KC, S])
    kn = xh
    cin = sb("cin", [P, NC, KD])
    cT = sb("cT", [P, CC, KEYS])
    xres = sb("xres", [P, T, D])
    q1 = sb("q1", [P, T, G, HD, HP])
    kv1 = [sb(f"kv1_{i}", [P, NC, 2, HH, W]) for i in range(2)]
    sq = [sb(f"sq{i}", [P, D]) for i in range(2)]
    vs = sb("vs", [P, 6, H])
    qf = [sb(f"qf{i}", [P, G, S]) for i in range(2)]
    kf = sb("kf", [P, G, KEYS])
    q_hi, q_lo = sb("q_hi", [P, G, S], F32R), sb("q_lo", [P, G, S], F32R)
    k_hi, k_lo = sb("k_hi", [P, G, KEYS], F32R), sb("k_lo", [P, G, KEYS], F32R)
    QS = [sb(f"QS{i}", [ST, HP, G, S], F32R) for i in range(2)]
    KS = [sb(f"KS{i}", [ST, HP, G, KEYS], F32R) for i in range(2)]
    st6, mv, rs = sb("st6", [P, T, 6]), sb("mv", [P, T, 2]), sb("rs", [P, T])
    mxa, den, ld, lt = (sb(n, [P, T, 2 * H]) for n in ("mxa", "den", "ld", "lt"))
    nm = sb("nm", [P, T, H])
    ed = sb("ed", [P, T, H, DCA])
    s_hi, s_lo = sb("s_hi", [2 * H, S], F32R), sb("s_lo", [2 * H, S], F32R)
    pt = [sb(f"pt{i}", [P, HP, NC * S]) for i in range(2)]
    pdt = sb("pdt", [P, 2, S])
    kdT = sb("kdT", [P, G, B * DCA])
    kdb = sb("kdb", [P, G, HP * DCA])
    vrep, vbd = sb("vrep", [P, D]), sb("vbd", [P, D])
    ot = sb("ot", [P, G, S])
    wdca = pt[0][:, :, :].rearrange("p a n -> p (a n)").rearrange("p (c n) -> p c n", c=CC)
    spare = pt[1][:, :, :].rearrange("p a n -> p (a n)")
    bd_b = spare[:, 0:2 * D]
    ydca = spare[:, 2 * D:2 * D + ND * KD].rearrange("p (c n) -> p c n", c=ND)
    ydT = spare[:, 3 * D:3 * D + CC * ND * P].rearrange("p (c n) -> p c n", c=CC)
    vdca = ot[:, :, :].rearrange("p a n -> p (a n)").rearrange("p (c n) -> p c n", c=ND)
    wsum = vs[:, :, :].rearrange("p a n -> p (a n)")

    ring = [stack.enter_context(nc.psum_tensor(f"ring{i}", [P, BANK], F32)) for i in range(4)]
    sc = [stack.enter_context(nc.psum_tensor(f"sc{i}", [P, 2, BANK], F32)) for i in range(2)]

    full = [sem(f"full{i}") for i in range(4)]
    evac = [sem(f"evac{i}") for i in range(4)]
    sc_full = [sem(f"sc_full{i}") for i in range(2)]
    sc_evac = [sem(f"sc_evac{i}") for i in range(2)]
    w_ld, y_ld, x_ld, c_ld, r_ld, vr_ld = (sem(n) for n in "w_ld y_ld x_ld c_ld r_ld vr_ld".split())
    q_in, k_in, sh_in = sem("q_in"), sem("k_in"), sem("sh_in")
    x2_st, vd_st = sem("x2_st"), sem("vd_st")
    const, ones, prep = sem("const"), sem("ones"), sem("prep")
    ln_st, ln_ag, ln_rs, xh_rdy = sem("ln_st"), sem("ln_ag"), sem("ln_rs"), sem("xh_rdy")
    sq_rdy, var_rdy, rstd, norm = sem("sq_rdy"), sem("var_rdy"), sem("rstd"), sem("norm")
    split = sem("split")
    ctx_rdy = sem("ctx_rdy")
    res_rdy, kd_rdy, vbd_rdy = sem("res_rdy"), sem("kd_rdy"), sem("vbd_rdy")
    d_max, d_exp, d_den = sem("d_max"), sem("d_exp"), sem("d_den")
    g_max, ln_rdy, lt_rdy, sh_hi = sem("g_max"), sem("ln_rdy"), sem("lt_rdy"), sem("sh_hi")

    GEMM = ["Q0", "Q1", "KV00", "KV01", "KV10", "KV11"]
    BODY = ["SD", "WO0", "XT0", "XT1", "CT", "Q0", "Q1", "KV00", "KV01", "KV10", "KV11", "WO1",
            "LT", "QT0", "QT1", "SDT", "KT0", "KT1", "PV0", "PV1", "PV2", "PV3"]
    ATTN = ["SD", "LT", "SDT", "PV0", "PV1", "PV2", "PV3"]
    WOUT = ["WO0", "WO1"]
    u = Units(4, [
        ("dca", ["YT", "DK0", "DV0", "DK1", "DV1", "KD0", "KD1"], 0, 1),
        ("pro", [n for n in BODY if n not in ATTN + WOUT], -1, 1),
        ("first", [n for n in BODY if n not in WOUT], 0, 1),
        ("body", BODY, 1, B - 2),
        ("last", [n for n in BODY if n in ATTN + WOUT], B - 1, 1),
        ("tail", WOUT, B, 1)])
    DOES_ATTN, DOES_PROJ, DOES_WO = ("first", "body", "last"), ("pro", "first", "body"), (
        "body", "last", "tail")

    def begin(eng, step, name, b):
        wait(eng, evac[u.bank(step, name)], u.count(step, name, b))
        return ring[u.bank(step, name)]

    def taken(step, name):
        return evac[u.bank(step, name)]

    def wait_full(eng, step, name, b):
        eng.wait_ge(full[u.bank(step, name)], u.count(step, name, b) + 1)
        return ring[u.bank(step, name)]

    def wait_evac(eng, step, name, b):
        eng.wait_ge(evac[u.bank(step, name)], u.count(step, name, b) + 1)

    def walk(eng, body):
        body("pro", -1, 1)
        body("first", 0, 0)
        with eng.Fori(0, (B - 4) // 2) as i:
            body("body", 2 * i + 1, 1)
            body("body", 2 * i + 2, 0)
        body("body", B - 3, 1)
        body("body", B - 2, 0)
        body("last", B - 1, 1)
        body("tail", B, 0)

    def heads(packed):
        return packed.rearrange("p (g d h) -> p g h d", d=HD, h=HP)

    def q_values(k):
        return q1[:, k, :, :, :].rearrange("p g d h -> p g h d")

    def head_norm_values(k, par):
        if k < T:
            return q_values(k)
        half = kv1[par][0:CK, (k - T) // 2, (k - T) % 2, :, 0:HD]
        return half.rearrange("p (g h) d -> p g h d", h=HP)

    def packed_k(k):
        c, half = (k - T) // 2, (k - T) % 2
        return heads(kn[0:CK, c, half * HH * HD:(half + 1) * HH * HD])

    def squares(n, values):
        return sq[n % 2][0:values.shape[0], 0:values.shape[1] * P].rearrange(
            "p (g h d) -> p g h d", h=HP, d=HD)

    def squares_of_head(k, values):
        return vs[0:values.shape[0], k, 0:values.shape[1] * HP].rearrange("p (g h) -> p g h", h=HP)

    block = stack.enter_context(nc.Block())

    @block.sync
    def _(sp):
        for dst, src in (
            (wdca, Wdca.rearrange("(c p) n -> p c n", p=P)),
            (bd_b, bdca.partition_broadcast(P)),
            (wq[:, :, :], Wq.rearrange("(c p) n -> p c n", p=P)),
            (wkv[:, :, 0:D], Wk.rearrange("(c p) n -> p c n", p=P)),
            (wkv[:, :, D:2 * D], Wv.rearrange("(c p) n -> p c n", p=P)),
            (bq_b[:, :], bq.partition_broadcast(P)),
            (bkv_b[:, 0:D], bk.partition_broadcast(P)),
            (bkv_b[:, D:2 * D], bv.partition_broadcast(P)),
            (bo_b[:, :], bo.partition_broadcast(P)),
            (wo[:, :, :], Wo.rearrange("(c p) n -> p c n", p=P)),
        ):
            sp.dma_start(dst, src).then_inc(w_ld, 16)
        for c in range(ND):
            wait_evac(sp, "dca", f"DV{c}", 0)
            sp.dma_start(vd_dram[c * BD:(c + 1) * BD].rearrange("b k n -> (b k) n"),
                         vdca[:, c, :]).then_inc(vd_st, 16)
        sp.wait_ge(vd_st, 16 * ND)

        def load_vrep(b):
            if not isinstance(b, int) or b != 0:
                sp.wait_ge(vbd_rdy, b)
            rows = vd_dram[b].unsqueeze(0) if isinstance(b, int) else vd_dram[bass.ds(b, 1)]
            sp.dma_start(vrep[:, :], rows.broadcast_to([HH, DCA, D])).then_inc(vr_ld, 16)

        def stack_parts(b, par, n):
            tensor, hi, lo, order, done = ((QS, q_hi, q_lo, (0, 2, 1), q_in),
                                           (KS, k_hi, k_lo, (0, 1, 2), k_in))[n]
            sp.wait_ge(split, 4 * b + 2 * n + 2)
            dst = tensor[par][:, :, :, :].rearrange("p h g n -> p h (g n)")
            for part, blk in zip((hi, hi, lo), order):
                sp.dma_start(dst[blk * HD:(blk + 1) * HD, :, :].bitcast(F32),
                             part[:, :, :].rearrange("p g n -> p (g n)").bitcast(F32)).then_inc(done, 16)

        def body(step, b, par):
            if step in DOES_PROJ:
                if step == "pro":
                    sp.dma_start(xin[:, :, :], x_t[0]).then_inc(x_ld, 16)
                    sp.dma_start(cin[0:CK, :, :], ctx_main[0]).then_inc(c_ld, 16)
                if not (isinstance(b, int) and b + 2 >= B):
                    sp.wait_ge(xh_rdy, T * (b + 2))
                    sp.dma_start(xin[:, :, :], x_t[b + 2]).then_inc(x_ld, 16)
                    wait_full(sp, step, "CT", b)
                    sp.dma_start(cin[0:CK, :, :], ctx_main[b + 2]).then_inc(c_ld, 16)
                load_vrep(b + 1)
            if step in DOES_ATTN:
                wait_evac(sp, step, "LT", b)
                for row, part in ((BLK, s_hi), (BLK + 1, s_lo)):
                    sp.dma_start(QS[par][row:row + 1, :, :, :].rearrange("p h g n -> p (h g) n").bitcast(F32),
                                 part[0:H, :].bitcast(F32)).then_inc(sh_in, 16)
            if step in DOES_WO:
                wait_evac(sp, step, "WO0", b)
                wait_evac(sp, step, "WO1", b)
                sp.dma_start(x2_dram[b - 1], xres[:, :, :]).then_inc(x2_st, 16)
            if step in DOES_PROJ:
                stack_parts(b + 1, 1 - par, 0)
            if step in DOES_WO:
                sp.wait_ge(x2_st, 16 * b)
            if step in DOES_ATTN:
                sp.dma_start(xres[:, :, :], x_t[b]).then_inc(r_ld, 16)
            if step in DOES_PROJ:
                stack_parts(b + 1, 1 - par, 1)

        walk(sp, body)

    @block.gpsimd
    def _(pool):
        sel32 = sq[0][0:2 * H, 0:2 * P]
        pool.memset(ident[:, :], 0.0).then_inc(const, 1)
        pool.memset(sel32, 0.0).then_inc(const, 1)
        pool.memset(mask[:, :, :], 1.0).then_inc(const, 1)
        pool.memset(neg_half[:, :], -0.5).then_inc(const, 1)
        pool.memset(eps_ln[:, :], EPS_LN).then_inc(const, 1)
        pool.memset(scratch[:, :], 0.0).then_inc(const, 1)
        pool.wait_ge(const, 6)
        pool.affine_select(out=ident[:, :], in_=ident[:, :], compare_op=ALU.not_equal, fill=1.0,
                           base=0, pattern=[[-1, P]], channel_multiplier=1).then_inc(const, 1)
        sel_v = sel32.rearrange("j (a h k) -> j (a h) k", a=2, h=HH)
        pool.affine_select(out=sel_v, in_=sel_v, compare_op=ALU.not_equal, fill=1.0, base=-H,
                           pattern=[[-1, H], [0, DCA]], channel_multiplier=1).then_inc(const, 1)
        for a in range(2):
            m = mask[:, a, :].rearrange("p (h d) -> p h d", h=HH)
            pool.affine_select(out=m, in_=m, compare_op=ALU.is_ge, fill=0.0, base=0,
                               pattern=[[-DCA, HH], [0, HD]], channel_multiplier=1).then_inc(const, 1)
        pool.wait_ge(const, 10)
        for a in range(2):
            m = mask[:, a, :].rearrange("p (h d) -> p h d", h=HH)
            pool.affine_select(out=m, in_=m, compare_op=ALU.is_ge, fill=0.0, base=DCA - 1,
                               pattern=[[DCA, HH], [0, HD]], channel_multiplier=-1).then_inc(const, 1)
        pool.tensor_copy(sel[:, :, :].rearrange("j a p -> j (a p)"), sel32).then_inc(const, 1)

        def root(k, n, rows, heads):
            w = vs[0:rows, k, 0:heads]
            pool.wait_ge(var_rdy, 2 * (n + 1))
            pool.tensor_tensor(w, w, neg_half[0:rows, 0:heads], ALU.pow).then_inc(rstd, 1)

        for c in range(ND):
            root(c, c, P, H)

        def body(step, b, par):
            if step in DOES_PROJ:
                pool.wait_ge(ln_ag, T * (b + 2))
                pool.tensor_tensor(rs[:, :], mv[:, :, 1], eps_ln[:, :], ALU.add).then_inc(ln_rs, 1)
                pool.wait_ge(ln_rs, 2 * (b + 1) + 1)
                pool.tensor_tensor(rs[:, :], rs[:, :], neg_half[:, 0:T], ALU.pow).then_inc(ln_rs, 1)
            if step in DOES_PROJ:
                for k in range(6):
                    root(k, ND + 6 * (b + 1) + k, P if k < T else CK, H if k < T else HH)
            if step in DOES_ATTN:
                pool.wait_ge(r_ld, 16 * (b + 1))
                pool.wait_ge(w_ld, 16 * 16)
                pool.tensor_tensor(xres[:, :, :], xres[:, :, :],
                                   bo_b[:, :].unsqueeze(1).broadcast_to([P, T, D]),
                                   ALU.add).then_inc(res_rdy, 1)
            if step in DOES_PROJ:
                pool.wait_ge(vr_ld, 16 * (b + 2))
                if step in DOES_ATTN:
                    pool.wait_ge(full[u.bank(step, "PV3")], u.count(step, "PV3", b) + 1)
                pool.tensor_tensor(vbd[:, :], vrep[:, :], mask[:, :, :].rearrange("p a n -> p (a n)"),
                                   ALU.mult).then_inc(vbd_rdy, 1)

        walk(pool, body)

    @block.tensor
    def _(pe):
        pe.wait_ge(const, 13)
        pe.wait_ge(y_ld, 16 * ND)
        bank = begin(pe, "dca", "YT", 0)
        for cc in range(CC):
            for c in range(ND):
                last = pe.transpose(bank[:, (cc * ND + c) * P:(cc * ND + c + 1) * P],
                                    ydca[:, c, cc * P:(cc + 1) * P], ident[:, :])
        last.then_inc(full[u.bank("dca", "YT")], 1)
        wait_evac(pe, "dca", "YT", 0)
        pe.wait_ge(prep, 14)
        for c in range(ND):
            for half, name in enumerate((f"DK{c}", f"DV{c}")):
                bank = begin(pe, "dca", name, 0)
                for cc in range(CC):
                    last = pe.matmul(bank[:, :], ydT[:, cc, c * P:(c + 1) * P],
                                     wdca[:, cc, half * D:(half + 1) * D],
                                     start=(cc == 0), stop=(cc == CC - 1))
                last.then_inc(full[u.bank("dca", name)], 1)
        for j in range(2):
            bank = begin(pe, "dca", f"KD{j}", 0)
            pe.wait_ge(norm, ND)
            for g in range(2):
                for c in range(ND):
                    last = pe.transpose(bank[:, (g * ND + c) * P:(g * ND + c + 1) * P],
                                        q1[:, c, 2 * j + g, :, :].rearrange("p d h -> p (d h)"),
                                        ident[:, :])
            last.then_inc(full[u.bank("dca", f"KD{j}")], 1)

        def x_transposes(step, b):
            pe.wait_ge(xh_rdy, T * (b + 2))
            for j in range(2):
                bank = begin(pe, step, f"XT{j}", b)
                for k in range(2):
                    for t in range(T):
                        last = pe.transpose(bank[:, (k * T + t) * P:(k * T + t + 1) * P],
                                            xh[:, t, (2 * j + k) * P:(2 * j + k + 1) * P], ident[:, :])
                last.then_inc(full[u.bank(step, f"XT{j}")], 1)
            pe.wait_ge(c_ld, 16 * (b + 2))
            bank = begin(pe, step, "CT", b)
            for cc in range(CC):
                for c in range(NC):
                    last = pe.transpose(bank[:, cc * KEYS + c * CK:cc * KEYS + (c + 1) * CK],
                                        cin[0:CK, c, cc * P:(cc + 1) * P], ident[0:CK, 0:CK])
            last.then_inc(full[u.bank(step, "CT")], 1)

        def project(step, b, k):
            name = GEMM[k]
            bank = begin(pe, step, name, b)
            if k < T:
                wait_evac(pe, step, "XT0", b)
                wait_evac(pe, step, "XT1", b)
                for kc in range(KC):
                    last = pe.matmul(bank[:, :], xT[:, kc, k * P:(k + 1) * P], wq[:, kc, :],
                                     start=(kc == 0), stop=(kc == KC - 1))
            else:
                c, half = (k - T) // 2, (k - T) % 2
                wait_evac(pe, step, "CT", b)
                for cc in range(CC):
                    last = pe.matmul(bank[0:CK, :], cT[:, cc, c * CK:(c + 1) * CK],
                                     wkv[:, cc, half * D:(half + 1) * D],
                                     start=(cc == 0), stop=(cc == CC - 1))
            last.then_inc(full[u.bank(step, name)], 1)

        def q_transposes(step, b, j):
            bank = begin(pe, step, f"QT{j}", b)
            pe.wait_ge(norm, ND + 6 * (b + 1) + T)
            for g in range(2):
                for t in range(T):
                    last = pe.transpose(bank[:, g * S + t * P:g * S + (t + 1) * P],
                                        q1[:, t, 2 * j + g, :, :].rearrange("p d h -> p (d h)"),
                                        ident[:, :])
            last.then_inc(full[u.bank(step, f"QT{j}")], 1)

        def k_transposes(step, b):
            pe.wait_ge(norm, ND + 6 * (b + 2))
            for j in range(2):
                bank = begin(pe, step, f"KT{j}", b)
                for g in range(2):
                    for c in range(NC):
                        last = pe.transpose(bank[:, g * KEYS + c * CK:g * KEYS + (c + 1) * CK],
                                            kn[0:CK, c, (2 * j + g) * P:(2 * j + g + 1) * P],
                                            ident[0:CK, 0:CK])
                last.then_inc(full[u.bank(step, f"KT{j}")], 1)

        def dca_scores(step, b, par):
            bank = begin(pe, step, "SD", b)
            pe.wait_ge(split, 4 * b + 1)
            pe.wait_ge(kd_rdy, b + 1)
            for t in range(T):
                for g in range(G):
                    o = (t * G + g) * HP * DCA
                    last = pe.matmul(bank[:, o:o + HP * DCA], qf[par][:, g, t * P:(t + 1) * P],
                                     kdb[:, g, :], start=True, stop=True)
            last.then_inc(full[u.bank(step, "SD")], 1)

        def scores(b, par, k):
            if k == 0:
                pe.wait_ge(q_in, STACKED * (b + 1))
                pe.wait_ge(k_in, STACKED * (b + 1))
            wait(pe, sc_evac[k % 2], 8 * b + k // 2)
            t, quad = k // G, k % G
            for i in range(HP):
                last = pe.matmul(sc[k % 2][:, i // 2, (i % 2) * KEYS:(i % 2 + 1) * KEYS],
                                 QS[par][0:BLK, i, quad, t * P:(t + 1) * P], KS[par][0:BLK, i, quad, :],
                                 start=True, stop=True)
            last.then_inc(sc_full[k % 2], 1)

        def shift_transposes(step, b):
            bank = begin(pe, step, "LT", b)
            pe.wait_ge(lt_rdy, b + 1)
            for t in range(T):
                last = pe.transpose(bank[0:2 * H, t * P:(t + 1) * P], lt[:, t, :], ident[:, :])
            last.then_inc(full[u.bank(step, "LT")], 1)

        def dca_scores_t(step, b, par):
            bank = begin(pe, step, "SDT", b)
            wait_evac(pe, step, "LT", b)
            for a in range(2):
                cols = bank[:, a * S:(a + 1) * S]
                pe.matmul(cols, sel[:, a, :], s_hi[:, :], start=True, stop=False, skip_group_check=True)
                pe.matmul(cols, sel[:, a, :], s_lo[:, :], start=False, stop=False, skip_group_check=True)
                for g in range(2):
                    last = pe.matmul(bank[g * 64:(g + 1) * 64, a * S:(a + 1) * S],
                                     kdb[:, 2 * a + g, :], qf[par][:, 2 * a + g, :],
                                     start=False, stop=True, skip_group_check=True)
            last.then_inc(full[u.bank(step, "SDT")], 1)

        def scores_t(b, par, p):
            if p == 0:
                pe.wait_ge(sh_in, 32 * (b + 1))
                pe.wait_ge(ones, 2)
            pe.wait_ge(sc_evac[p % 2], 8 * b + 4 + p // 2)
            for i in range(2):
                g, h = divmod(2 * p + i, HP)
                for c in range(NC):
                    last = pe.matmul(sc[p % 2][0:CK, i, c * S:(c + 1) * S],
                                     KS[par][:, h, g, c * CK:(c + 1) * CK],
                                     QS[par][:, h, g, :], start=True, stop=True)
            last.then_inc(sc_full[p % 2], 1)

        def values(step, b, par, g):
            bank = begin(pe, step, f"PV{g}", b)
            for i in range(2):
                pe.wait_ge(sc_evac[i], 8 * b + 4 + g + 1)
            for c in range(NC):
                for i in range(HP):
                    h = g * HP + i
                    pe.matmul(bank[i * HD:(i + 1) * HD, 0:S],
                              kv1[par][0:CK, c, h // HH, h % HH, HD:W],
                              pt[g % 2][0:CK, i, c * S:(c + 1) * S],
                              start=(c == 0), stop=False, skip_group_check=True)
            if g == 0:
                wait_evac(pe, step, "SDT", b)
                pe.wait_ge(vbd_rdy, b + 1)
            pe.matmul(bank[:, 0:S], vbd[:, g * P:(g + 1) * P], pdt[:, g // 2, :],
                      start=False, stop=True, skip_group_check=True
                      ).then_inc(full[u.bank(step, f"PV{g}")], 1)

        def out_projection(step, b, t):
            bank = begin(pe, step, f"WO{t}", b)
            for g in range(G):
                last = pe.matmul(bank[:, :], ot[:, g, t * P:(t + 1) * P], wo[:, g, :],
                                 start=(g == 0), stop=(g == G - 1))
            last.then_inc(full[u.bank(step, f"WO{t}")], 1)

        def body(step, b, par):
            attn, proj, wout = step in DOES_ATTN, step in DOES_PROJ, step in DOES_WO
            if attn:
                dca_scores(step, b, par)
            if wout:
                if attn:
                    pe.wait_ge(ctx_rdy, b)
                else:
                    wait_evac(pe, "last", "PV3", B - 1)
                out_projection(step, b, 0)
            if attn:
                scores(b, par, 0)
                scores(b, par, 1)
            if proj:
                x_transposes(step, b)
            for groups, units in (((), (0,)), ((2, 3), (1,)), ((4, 5), (2, 3)), ((6, 7), (4, 5))):
                if attn:
                    for k in groups:
                        scores(b, par, k)
                if proj:
                    for k in units:
                        project(step, b, k)
            if wout:
                out_projection(step, b, 1)
            if attn:
                shift_transposes(step, b)
            if proj:
                q_transposes(step, b, 0)
                q_transposes(step, b, 1)
            if attn:
                dca_scores_t(step, b, par)
                scores_t(b, par, 0)
                scores_t(b, par, 1)
            if proj:
                k_transposes(step, b)
            if attn:
                scores_t(b, par, 2)
                scores_t(b, par, 3)
                for g in range(3):
                    values(step, b, par, g)
                    if g < 2:
                        scores_t(b, par, 4 + 2 * g)
                        scores_t(b, par, 5 + 2 * g)
                values(step, b, par, 3)

        walk(pe, body)

    @block.scalar
    def _(act):
        for c in range(ND):
            act.dma_start(ydca[:, c, :],
                          ctx[c * BD:(c + 1) * BD, KEYS:KEYS + DCA, :]).then_inc(y_ld, 16)
        for n, vec in enumerate((qn_w, qn_b, kn_w, kn_b, kd_w, kd_b)):
            act.dma_start(affine[:, n:n + 1], vec.unsqueeze(1).unsqueeze(2).broadcast_to([HD, HP, 1]),
                          allow_slow_non_contiguous=True).then_inc(w_ld, 16)

        def copy_out(step, b, name, dst, cols):
            bank = wait_full(act, step, name, b)
            act.activation(dst, bank[:, 0:cols].rearrange("p (a n) -> p a n", a=dst.shape[1]),
                           ACT.Copy).then_inc(taken(step, name), 1)

        def square(step, b, name, n, values):
            wait_evac(act, step, name, b)
            wait(act, var_rdy, 2 * (n - 1))
            act.activation(squares(n, values), values, ACT.Square, scale=HD ** -0.5).then_inc(sq_rdy, 1)

        def affine_out(step, b, name, dst, cols, n):
            bank = wait_full(act, step, name, b)
            act.activation(dst, bank[:, 0:cols].rearrange("p (a n) -> p a n", a=2), ACT.Identity,
                           bias=affine[:, n + 1:n + 2], scale=affine[:, n:n + 1]
                           ).then_inc(taken(step, name), 1)

        copy_out("dca", 0, "YT", ydT, CC * ND * P)
        act.wait_ge(w_ld, 16 * 16)
        act.wait_ge(const, 13)
        for c in range(ND):
            square("dca", 0, f"DK{c}", c, q_values(c))
        for j in range(2):
            affine_out("dca", 0, f"KD{j}", kdT[:, 2 * j:2 * j + 2, :], 2 * ND * P, 4)

        def exps(b, k):
            act.wait_ge(g_max, 16 * b + 2 * k + 2)
            t, quad = k // G, k % G
            for i in range(HP):
                h = i * G + quad
                s = sc[k % 2][:, i // 2, (i % 2) * KEYS:(i % 2 + 1) * KEYS]
                last = act.activation(s, s, ACT.Exp, bias=nm[:, t, h:h + 1], scale=SCALE,
                                      accum_out=den[:, t, h:h + 1])
            last.then_inc(sc_evac[k % 2], 1)

        def probabilities(step, b, p):
            g = p // 2
            act.wait_ge(sc_full[p % 2], 8 * b + 4 + p // 2 + 1)
            if g >= 2 and p % 2 == 0:
                wait_full(act, step, f"PV{g - 2}", b)
            act.activation(pt[g % 2][0:CK, (p % 2) * 2:(p % 2) * 2 + 2, :], sc[p % 2][0:CK, :, :],
                           ACT.Exp, scale=SCALE).then_inc(sc_evac[p % 2], 1)

        def body(step, b, par):
            attn, proj = step in DOES_ATTN, step in DOES_PROJ
            n = ND + 6 * (b + 1)

            def sq_unit(k):
                values = head_norm_values(k, 1 - par)
                wait_evac(act, step, GEMM[k], b)
                act.wait_ge(var_rdy, 2 * (n + k - 1))
                act.activation(squares(k, values), values, ACT.Square, scale=HD ** -0.5).then_inc(sq_rdy, 1)

            if attn:
                wait_evac(act, step, "SD", b)
                act.activation(ed[:, :, :, :], ed[:, :, :, :], ACT.Exp, scale=SCALE).then_inc(d_exp, 1)
            if proj:
                copy_out(step, b, "XT0", xT[:, 0:2, :], 2 * S)
                copy_out(step, b, "XT1", xT[:, 2:4, :], 2 * S)
            if attn:
                exps(b, 0)
                exps(b, 1)
            if proj:
                copy_out(step, b, "CT", cT[:, :, :], CC * KEYS)
                sq_unit(0)
            if attn:
                exps(b, 2)
                exps(b, 3)
            if proj:
                sq_unit(1)
            if attn:
                exps(b, 4)
                exps(b, 5)
            if proj:
                sq_unit(2)
                sq_unit(3)
            if attn:
                exps(b, 6)
                exps(b, 7)
            if proj:
                sq_unit(4)
            if attn:
                act.wait_ge(d_den, b + 1)
                for i in range(2):
                    act.wait_ge(sc_evac[i], 8 * b + 4)
                act.activation(ld[:, :, :], den[:, :, :], ACT.Ln).then_inc(ln_rdy, 1)
            if proj:
                sq_unit(5)
                affine_out(step, b, "QT0", qf[1 - par][:, 0:2, :], 2 * S, 0)
                affine_out(step, b, "QT1", qf[1 - par][:, 2:4, :], 2 * S, 0)
            if attn:
                bank = wait_full(act, step, "SDT", b)
                act.activation(pdt[:, :, :], bank[:, :].rearrange("p (a n) -> p a n", a=2), ACT.Exp,
                               scale=SCALE).then_inc(taken(step, "SDT"), 1)
                probabilities(step, b, 0)
                probabilities(step, b, 1)
            if proj:
                wait(act, split, 4 * (b + 1))
                affine_out(step, b, "KT0", kf[:, 0:2, :], 2 * KEYS, 2)
                affine_out(step, b, "KT1", kf[:, 2:4, :], 2 * KEYS, 2)
            if attn:
                for p in range(2, 8):
                    probabilities(step, b, p)

        walk(act, body)

    @block.vector
    def _(dve):
        for i in range(2):
            dve.memset(KS[i][BLK:ST, :, :, :].bitcast(F32), 1.0).then_inc(ones, 1)
        dve.wait_ge(w_ld, 16 * 16)
        dve.wait_ge(const, 13)
        heads = (
            wdca[:, 0, 0:D].rearrange("p (h d) -> p h d", d=HD),
            wdca[:, 1, 0:D].rearrange("p (h d) -> p h d", d=HD),
            bd_b[:, 0:D].rearrange("p (h d) -> p h d", d=HD),
            wq[:, :, :].rearrange("p c (h d) -> p (c h) d", d=HD),
            wkv[:, :, :].rearrange("p c (h w) -> p (c h) w", w=W)[:, :, 0:HD],
            bq_b[:, :].rearrange("p (h d) -> p h d", d=HD),
        )
        bk_heads = bkv_b[:, :].rearrange("p (h w) -> p h w", w=W)[:, :, 0:HD]
        for n, w in enumerate(heads + (bk_heads,)):
            sums = wsum[:, 0:w.shape[1]]
            dve.tensor_reduce(sums, w, AX_X, ALU.add).then_inc(prep, 1)
            dve.wait_ge(prep, 2 * n + 1)
            dve.scalar_tensor_tensor(w, sums.unsqueeze(2).broadcast_to(w.shape), -1.0 / HD, w,
                                     ALU.mult, ALU.add).then_inc(prep, 1)
            dve.wait_ge(prep, 2 * n + 2)

        dve.tensor_reduce(own[:, :], ident[:, :].rearrange("p (d h) -> p h d", h=HP), AX_X,
                          ALU.add).then_inc(prep, 1)
        dve.wait_ge(prep, 15)

        def by_head(columns):
            return columns.rearrange("p (g h d) -> p g h d", h=HP, d=HD)

        def sum_squares(k, n, values):
            dve.wait_ge(sq_rdy, n + 1)
            w = squares_of_head(k, values)
            dve.tensor_reduce(w, squares(k, values), AX_X, ALU.add).then_inc(var_rdy, 1)
            dve.wait_ge(var_rdy, 2 * n + 1)
            dve.tensor_scalar(w, w, EPS_QK, None, ALU.add).then_inc(var_rdy, 1)

        def normalise(k, n, values, normal):
            dve.wait_ge(rstd, n + 1)
            w = squares_of_head(k, values)
            dve.tensor_tensor(normal, values, w.unsqueeze(3).broadcast_to(values.shape),
                              ALU.mult).then_inc(norm, 1)

        for c in range(ND):
            for dst, name, half in ((q_values(c), f"DK{c}", 0), (vdca[:, c, :], f"DV{c}", 1)):
                bank = wait_full(dve, "dca", name, 0)
                made, bias = bank[:, :], bd_b[:, half * D:(half + 1) * D]
                if half == 0:
                    made, bias = by_head(made), by_head(bias)
                dve.tensor_tensor(dst, made, bias, ALU.add).then_inc(taken("dca", name), 1)
        for c in range(ND):
            sum_squares(c, c, q_values(c))
        for c in range(ND):
            normalise(c, c, q_values(c), q_values(c))
        dve.wait_ge(norm, ND)
        dve.wait_ge(vd_st, 16 * ND)

        def row_stats(b):
            dve.wait_ge(x_ld, 16 * (b + 2))
            for t in range(T):
                dve.bn_stats(st6[:, t, :], xin[:, t, :]).then_inc(ln_st, 1)
            dve.wait_ge(ln_st, T * (b + 2))
            carry_wait(dve, scratch)
            for t in range(T):
                dve.bn_aggr(mv[:, t, :], st6[:, t, :]).then_inc(ln_ag, 1)

        def row_norm(b):
            dve.wait_ge(ln_rs, 2 * (b + 2))
            for t in range(T):
                dve.tensor_scalar(xh[:, t, :], xin[:, t, :], mv[:, t, 0:1], rs[:, t:t + 1],
                                  ALU.subtract, ALU.mult).then_inc(xh_rdy, 1)

        def group_max(b, k):
            t, quad = k // G, k % G
            dve.wait_ge(sc_full[k % 2], 8 * b + k // 2 + 1)
            s = sc[k % 2][:, :, 0:2 * KEYS].rearrange("p a (h n) -> p a h n", h=2)
            mx = mxa[:, t, 0:H].rearrange("p (h g) -> p h g", g=G)[:, :, quad]
            dve.tensor_reduce(mx.rearrange("p (a h) -> p a h", a=2), s, AX_X, ALU.max).then_inc(g_max, 1)
            dve.wait_ge(g_max, 16 * b + 2 * k + 1)
            dve.tensor_scalar(nm[:, t, :].rearrange("p (h g) -> p h g", g=G)[:, :, quad], mx, -SCALE, None,
                              ALU.mult).then_inc(g_max, 1)

        def bias_out(step, b, k, par):
            bank = wait_full(dve, step, GEMM[k], b)
            if k < T:
                dst, bias, rows = q_values(k), by_head(bq_b[:, :]), P
            else:
                c, half = (k - T) // 2, (k - T) % 2
                dst = kv1[par][0:CK, c, half, :, :].rearrange("p h w -> p (h w)")
                bias, rows = bkv_b[0:CK, half * D:(half + 1) * D], CK
            made = by_head(bank[:, :]) if k < T else bank[0:rows, :]
            dve.tensor_tensor(dst, made, bias, ALU.add).then_inc(taken(step, GEMM[k]), 1)

        def split_parts(step, b, n, names, whole, hi, lo, stacked):
            for name in names:
                wait_evac(dve, step, name, b)
            wait(dve, stacked, STACKED * (b + 1))
            dve.tensor_copy(hi[:, :, :], whole[:, :, :]).then_inc(split, 1)
            dve.wait_ge(split, 4 * (b + 1) + n + 1)
            dve.tensor_tensor(lo[:, :, :], whole[:, :, :], hi[:, :, :].bitcast(F32),
                              ALU.subtract).then_inc(split, 1)

        def dca_keys(b):
            shape = [P, G, HP, DCA]
            dve.tensor_tensor(kdb[:, :, :].rearrange("p g (h k) -> p g h k", h=HP),
                              kdT[:, :, bass.ts(b, DCA)].unsqueeze(2).broadcast_to(shape),
                              own[:, :].unsqueeze(1).unsqueeze(3).broadcast_to(shape),
                              ALU.mult).then_inc(kd_rdy, 1)

        def ctx_out(step, b, g):
            bank = wait_full(dve, step, f"PV{g}", b)
            dve.tensor_copy(ot[:, g, :], bank[:, 0:S]).then_inc(taken(step, f"PV{g}"), 1)

        def residual(step, b, t):
            if t == 0:
                dve.wait_ge(res_rdy, b)
            bank = wait_full(dve, step, f"WO{t}", b)
            dve.tensor_tensor(xres[:, t, :], bank[:, :], xres[:, t, :],
                              ALU.add).then_inc(taken(step, f"WO{t}"), 1)

        for c in range(ND):
            wait_evac(dve, "dca", f"KD{c}", 0)

        def body(step, b, par):
            attn, proj, wout = step in DOES_ATTN, step in DOES_PROJ, step in DOES_WO
            n = ND + 6 * (b + 1)
            def bias(k):
                bias_out(step, b, k, 1 - par)

            def scale(k):
                values = head_norm_values(k, 1 - par)
                normalise(k, n + k, values, values if k < T else packed_k(k))

            def var(k):
                sum_squares(k, n + k, head_norm_values(k, 1 - par))

            if proj:
                row_stats(b)
            if attn:
                bank = wait_full(dve, step, "SD", b)
                s = bank[:, :].rearrange("p (t h k) -> p t h k", t=T, h=H)
                dve.tensor_reduce(mxa[:, :, H:2 * H], s, AX_X, ALU.max).then_inc(d_max, 1)
                dve.wait_ge(d_max, b + 1)
                dve.tensor_tensor(ed[:, :, :, :], s, mxa[:, :, H:2 * H].unsqueeze(3).broadcast_to(
                    [P, T, H, DCA]), ALU.subtract).then_inc(taken(step, "SD"), 1)
            if proj:
                row_norm(b)
            if wout:
                residual(step, b, 0)
            if attn:
                group_max(b, 0)
                group_max(b, 1)
                dve.wait_ge(d_exp, b + 1)
                dve.tensor_reduce(den[:, :, H:2 * H], ed[:, :, :, :], AX_X, ALU.add).then_inc(d_den, 1)
            if proj:
                bias(0)
            if attn:
                group_max(b, 2)
            if proj:
                var(0)
            if attn:
                group_max(b, 3)
            if proj:
                bias(1)
            if attn:
                group_max(b, 4)
                group_max(b, 5)
            if proj:
                var(1)
                scale(0)
                bias(2)
                bias(3)
            if attn:
                group_max(b, 6)
            if proj:
                var(2)
            if attn:
                group_max(b, 7)
            if proj:
                bias(4)
                var(3)
                scale(1)
                bias(5)
                scale(2)
                var(4)
            if attn:
                dve.wait_ge(ln_rdy, b + 1)
                dve.scalar_tensor_tensor(lt[:, :, :], ld[:, :, :], -1.0 / SCALE, mxa[:, :, :],
                                         ALU.mult, ALU.subtract).then_inc(lt_rdy, 1)
            if wout:
                residual(step, b, 1)
            if attn:
                bank = wait_full(dve, step, "LT", b)
                dve.tensor_copy(s_hi[:, :], bank[0:2 * H, 0:S]).then_inc(sh_hi, 1)
                dve.wait_ge(sh_hi, b + 1)
                dve.tensor_tensor(s_lo[:, :], bank[0:2 * H, 0:S], s_hi[:, :].bitcast(F32),
                                  ALU.subtract).then_inc(taken(step, "LT"), 1)
            if proj:
                var(5)
                for k in range(3, 6):
                    scale(k)
                split_parts(step, b, 0, ("QT0", "QT1"), qf[1 - par], q_hi, q_lo, q_in)
                if attn:
                    wait_evac(dve, step, "SDT", b)
                dca_keys(b + 1)
                split_parts(step, b, 2, ("KT0", "KT1"), kf, k_hi, k_lo, k_in)
            if attn:
                for g in range(G):
                    ctx_out(step, b, g)
                wait_evac(dve, step, f"PV{G - 1}", b)
                carry_wait(dve, scratch).then_inc(ctx_rdy, 1)

        walk(dve, body)


def ffn_phase(nc, stack, x2_dram, gate_W, W1, b1, W2, b2, out):
    B, _, T, D = x2_dram.shape
    NE, _, FF = W1.shape
    S = T * P
    KC = D // P
    FC = -(-FF // P)
    FR = FF - (FC - 1) * P
    TOP = 2
    PAIRS = [(t, e) for t in range(T) for e in range(TOP)]
    out_t = out.rearrange("b (t p) d -> b p t d", p=P)

    def sem(name):
        return stack.enter_context(nc.semaphore(name))

    def sb(name, shape, dt=F32):
        return stack.enter_context(nc.sbuf_tensor(name, shape, dt))

    ident = sb("f_ident", [P, P])
    w1 = [sb(f"w1_{part}", [P, NE, KC, FF], F32R) for part in ("hi", "lo")]
    w2 = [sb(f"w2_{part}", [P, NE, FC, D], F32R) for part in ("hi", "lo")]
    b1_b = sb("b1_b", [P, NE, FF])
    b2_b = sb("b2_b", [P, NE, D])
    gate = sb("gate", [P, KC, NE])
    neg_half, eps_ln = sb("f_neg_half", [P, T]), sb("f_eps_ln", [P, T])
    ones = sb("f_ones", [P, 1])
    scratch = sb("f_scratch", [P, 2])
    euler = sb("euler", [P, 1])
    x2 = [sb(f"x2_{i}", [P, T, D]) for i in range(2)]
    xo = sb("xo", [P, T, D])
    xh = sb("f_xh", [P, T, D])
    xT = [sb(f"f_xT_{part}", [P, KC, S], F32R) for part in ("hi", "lo")]
    xsum = sb("xsum", [P, KC])
    st6, mv, rs = sb("f_st6", [P, T, 6]), sb("f_mv", [P, T, 2]), sb("f_rs", [P, T])
    lg = sb("lg", [P, 8])
    top = sb("top", [P, 8])
    idx = [sb(f"idx{i}", [P, 8], U32) for i in range(2)]
    gd = sb("gd", [P, 2])
    gv = [sb(f"gv{i}", [P, TOP]) for i in range(2)]
    hb = sb("hb", [P, len(PAIRS), FF])
    hT = [sb(f"hT_{part}", [P, TOP, FC, S], F32R) for part in ("hi", "lo")]
    HI, LO = 0, 1
    PASSES = ((HI, HI), (HI, LO), (LO, HI))

    ring = [stack.enter_context(nc.psum_tensor(f"f_ring{i}", [P, BANK], F32)) for i in range(8)]
    full = [sem(f"f_full{i}") for i in range(8)]
    evac = [sem(f"f_evac{i}") for i in range(8)]
    g_ld, o_st, x_ld = sem("g_ld"), sem("o_st"), [sem("f_x_ld0"), sem("f_x_ld1")]
    w_ld = [sem(f"f_w_ld{n}") for n in range(2 * NE)]
    w_hi, w_lo = sem("w_hi"), sem("w_lo")
    const, ln_st, ln_ag, ln_rs, xh_rdy = (sem("f_" + n) for n in "const ln_st ln_ag ln_rs xh_rdy".split())
    g_log, g_pick, g_pow, g_val = sem("g_log"), sem("g_pick"), sem("g_pow"), sem("g_val")
    h_rdy, res = sem("h_rdy"), sem("res")
    x_hi, h_hi = sem("x_hi"), sem("h_hi")

    BODY = ["H0", "H1", "H2", "XS", "H3", "HT0", "GT", "XT0", "HT1", "HR", "XT1", "OUT0", "OUT1"]
    NEXT = ["XS", "GT", "XT0", "XT1"]
    u = Units(8, [("pro", NEXT, -1, 1), ("first", BODY, 0, 1), ("body", BODY, 1, B - 2),
                  ("last", [n for n in BODY if n not in NEXT], B - 1, 1)])
    DOES_FFN, DOES_NEXT = ("first", "body", "last"), ("pro", "first", "body")

    def begin(eng, step, name, b):
        wait(eng, evac[u.bank(step, name)], u.count(step, name, b))
        return ring[u.bank(step, name)]

    def taken(step, name):
        return evac[u.bank(step, name)]

    def wait_full(eng, step, name, b):
        eng.wait_ge(full[u.bank(step, name)], u.count(step, name, b) + 1)
        return ring[u.bank(step, name)]

    def wait_evac(eng, step, name, b):
        eng.wait_ge(evac[u.bank(step, name)], u.count(step, name, b) + 1)

    def walk(eng, body):
        body("pro", -1, 1, 0)
        body("first", 0, 0, 0)
        with eng.Fori(0, (B - 2) // 2) as i:
            body("body", 2 * i + 1, 1, i)
            body("body", 2 * i + 2, 0, i + 1)
        body("last", B - 1, 1, (B - 2) // 2)

    block = stack.enter_context(nc.Block())

    def weights(n):
        e = n % NE
        if n < NE:
            return [(w1[LO][:, e, :, :], w1[HI][:, e, :, :])]
        return [(w2[LO][:, e, 0:FC - 1, :], w2[HI][:, e, 0:FC - 1, :]),
                (w2[LO][0:FR, e, FC - 1, :], w2[HI][0:FR, e, FC - 1, :])]

    @block.sync
    def _(sp):
        sp.dma_start(x2[0][:, :, :], x2_dram[0]).then_inc(x_ld[0], 16)
        for c in range(KC):
            sp.dma_start(gate[:, c, :], gate_W[:, c * P:(c + 1) * P].rearrange("e p -> p e"),
                         allow_slow_non_contiguous=True).then_inc(g_ld, 16)
        for e in range(NE):
            sp.dma_start(w1[LO][:, e, :, :].bitcast(F32),
                         W1[e].rearrange("(c p) f -> p c f", p=P)).then_inc(w_ld[e], 16)
            sp.dma_start(b1_b[:, e, :], b1[e].partition_broadcast(P)).then_inc(w_ld[e], 16)
        for e in range(NE):
            sp.dma_start(w2[LO][:, e, 0:FC - 1, :].bitcast(F32),
                         W2[e, 0:(FC - 1) * P].rearrange("(c p) n -> p c n", p=P)).then_inc(w_ld[NE + e], 16)
            sp.dma_start(w2[LO][0:FR, e, FC - 1, :].bitcast(F32),
                         W2[e, (FC - 1) * P:FF]).then_inc(w_ld[NE + e], 16)
            sp.dma_start(b2_b[:, e, :], b2[e].partition_broadcast(P)).then_inc(w_ld[NE + e], 16)

        def body(step, b, par, half):
            if step in ("first", "body"):
                if step == "body":
                    sp.wait_ge(res, 2 * T * (b - 1) + T)
                sp.dma_start(x2[1 - par][:, :, :], x2_dram[b + 1]).then_inc(x_ld[1 - par], 16)
            if step in ("body", "last"):
                wait_evac(sp, "body", f"OUT{T - 1}", b - 1)
                sp.dma_start(out_t[b - 1], xo[:, :, :]).then_inc(o_st, 16)
            if step == "last":
                wait_evac(sp, step, f"OUT{T - 1}", b)
                sp.dma_start(out_t[B - 1], xo[:, :, :]).then_inc(o_st, 16)

        walk(sp, body)
        sp.wait_ge(o_st, 16 * B)

    @block.gpsimd
    def _(pool):
        pool.memset(ident[:, :], 0.0).then_inc(const, 1)
        pool.memset(neg_half[:, :], -0.5).then_inc(const, 1)
        pool.memset(euler[:, :], EULER).then_inc(const, 1)
        pool.memset(lg[:, :], LEAST).then_inc(const, 1)
        pool.memset(eps_ln[:, :], EPS_LN).then_inc(const, 1)
        pool.memset(scratch[:, :], 0.0).then_inc(const, 1)
        pool.memset(ones[:, :], 1.0).then_inc(const, 1)
        pool.wait_ge(const, 7)
        pool.affine_select(out=ident[:, :], in_=ident[:, :], compare_op=ALU.not_equal, fill=1.0,
                           base=0, pattern=[[-1, P]], channel_multiplier=1).then_inc(const, 1)

        def body(step, b, par, half):
            if step in DOES_NEXT:
                pool.wait_ge(ln_ag, T * (b + 2))
                pool.tensor_tensor(rs[:, :], mv[:, :, 1], eps_ln[:, :], ALU.add).then_inc(ln_rs, 1)
                pool.wait_ge(ln_rs, 2 * (b + 1) + 1)
                pool.tensor_tensor(rs[:, :], rs[:, :], neg_half[:, :], ALU.pow).then_inc(ln_rs, 1)
                pool.wait_ge(g_pick, 3 * (b + 2))
                pool.tensor_tensor(gd[:, 1:2], euler[:, :], gd[:, 0:1], ALU.pow).then_inc(g_pow, 1)

        walk(pool, body)

    @block.tensor
    def _(pe):
        pe.wait_ge(const, 8)
        pe.wait_ge(g_ld, 16 * KC)

        def hidden(step, b, ex, n):
            t, e = PAIRS[n]
            bank = begin(pe, step, f"H{n}", b)
            for kc in range(KC):
                for i, (xp, wp) in enumerate(PASSES):
                    last = pe.matmul(bank[:, 0:FF], xT[xp][:, kc, t * P:(t + 1) * P],
                                     w1[wp][:, bass.ds(ex[e], 1), kc, :].rearrange("p a f -> p (a f)"),
                                     start=(kc == 0 and i == 0), stop=(kc == KC - 1 and i == 2))
            last.then_inc(full[u.bank(step, f"H{n}")], 1)

        def x_transposes(step, b, j):
            bank = begin(pe, step, f"XT{j}", b)
            for k in range(2):
                for t in range(T):
                    last = pe.transpose(bank[:, (k * T + t) * P:(k * T + t + 1) * P],
                                        xh[:, t, (2 * j + k) * P:(2 * j + k + 1) * P], ident[:, :])
            last.then_inc(full[u.bank(step, f"XT{j}")], 1)

        def x_sums(step, b):
            pe.wait_ge(xh_rdy, T * (b + 2))
            bank = begin(pe, step, "XS", b)
            for kc in range(KC):
                for t in range(T):
                    last = pe.matmul(bank[:, kc:kc + 1], xh[:, t, kc * P:(kc + 1) * P], ones[:, :],
                                     start=(t == 0), stop=(t == T - 1))
            last.then_inc(full[u.bank(step, "XS")], 1)

        def gate_logits(step, b):
            bank = begin(pe, step, "GT", b)
            wait_evac(pe, step, "XS", b)
            for kc in range(KC):
                last = pe.matmul(bank[:, 0:NE], xsum[:, kc:kc + 1].broadcast_to([P, P]),
                                 gate[:, kc, :], start=(kc == 0), stop=(kc == KC - 1))
            last.then_inc(full[u.bank(step, "GT")], 1)

        def h_transposes(step, b, t):
            bank = begin(pe, step, f"HT{t}", b)
            pe.wait_ge(h_rdy, len(PAIRS) * b + TOP * (t + 1))
            for e in range(TOP):
                for fc in range(FC - 1):
                    k = e * (FC - 1) + fc
                    last = pe.transpose(bank[:, k * P:(k + 1) * P],
                                        hb[:, TOP * t + e, fc * P:(fc + 1) * P], ident[:, :])
            last.then_inc(full[u.bank(step, f"HT{t}")], 1)

        def last_chunks(step, b):
            bank = begin(pe, step, "HR", b)
            for e in range(TOP):
                for t in range(T):
                    last = pe.transpose(bank[0:FR, e * S + t * P:e * S + (t + 1) * P],
                                        hb[:, TOP * t + e, (FC - 1) * P:FF], ident[:, :])
            last.then_inc(full[u.bank(step, "HR")], 1)

        def output(step, b, ex, t):
            bank = begin(pe, step, f"OUT{t}", b)
            wait_evac(pe, step, f"HT{t}", b)
            if t == 0 and step == "first":
                pe.wait_ge(w_lo, 2 * NE)
            order = [(e, fc) for e in range(TOP) for fc in range(FC - 1)] + [
                (e, FC - 1) for e in range(TOP)]
            for n, (e, fc) in enumerate(order):
                if t == 0 and n == TOP * (FC - 1):
                    wait_evac(pe, step, "HR", b)
                rows = P if fc < FC - 1 else FR
                if t == T - 1 and n == len(order) - 1 and step in DOES_NEXT:
                    pe.wait_ge(g_val, 2 * (b + 2))
                for i, (hp, wp) in enumerate(PASSES):
                    last = pe.matmul(bank[:, :], hT[hp][0:rows, e, fc, t * P:(t + 1) * P],
                                     w2[wp][0:rows, bass.ds(ex[e], 1), fc, :].rearrange("p a n -> p (a n)"),
                                     start=(n == 0 and i == 0),
                                     stop=(n == len(order) - 1 and i == 2))
            last.then_inc(full[u.bank(step, f"OUT{t}")], 1)

        def body(step, b, par, half):
            ffn, nxt = step in DOES_FFN, step in DOES_NEXT
            if ffn:
                if step == "first":
                    pe.wait_ge(g_val, 2)
                ex = [pe.value_load(idx[par][0:1, e:e + 1], min_val=0, max_val=NE - 1) for e in range(TOP)]
                if step == "first":
                    pe.wait_ge(w_lo, NE)
                wait_evac(pe, "pro" if step == "first" else "body", "XT1", b - 1)
                for n in range(3):
                    hidden(step, b, ex, n)
            if nxt:
                x_sums(step, b)
            if ffn:
                hidden(step, b, ex, 3)
                h_transposes(step, b, 0)
            if nxt:
                gate_logits(step, b)
                x_transposes(step, b, 0)
            if ffn:
                h_transposes(step, b, 1)
                last_chunks(step, b)
            if nxt:
                x_transposes(step, b, 1)
            if ffn:
                for t in range(T):
                    output(step, b, ex, t)

        walk(pe, body)

    @block.scalar
    def _(act):
        def high_parts(n):
            act.wait_ge(w_ld[n], 16 * (2 if n < NE else 3))
            for whole, hi in weights(n):
                act.activation(hi, whole.bitcast(F32), ACT.Copy).then_inc(w_hi, 1)

        def body(step, b, par, half):
            ffn, nxt = step in DOES_FFN, step in DOES_NEXT
            if ffn:
                for n in range(len(PAIRS)):
                    if n == 3 and step == "first":
                        for k in range(NE, 2 * NE):
                            high_parts(k)
                    if n == 3 and nxt:
                        bank = wait_full(act, step, "XS", b)
                        act.activation(xsum[:, :], bank[:, 0:KC], ACT.Copy).then_inc(taken(step, "XS"), 1)
                    wait_evac(act, step, f"H{n}", b)
                    act.activation(hb[:, n, :], hb[:, n, :], ACT.Gelu).then_inc(h_rdy, 1)
                for t in range(T):
                    bank = wait_full(act, step, f"HT{t}", b)
                    for e in range(TOP):
                        cols = bank[:, e * (FC - 1) * P:(e + 1) * (FC - 1) * P]
                        act.activation(hT[HI][:, e, 0:FC - 1, t * P:(t + 1) * P],
                                       cols.rearrange("p (c n) -> p c n", n=P),
                                       ACT.Copy, scale=gv[par][:, e:e + 1]).then_inc(h_hi, 1)
                bank = wait_full(act, step, "HR", b)
                for e in range(TOP):
                    act.activation(hT[HI][0:FR, e, FC - 1, :], bank[0:FR, e * S:(e + 1) * S],
                                   ACT.Copy, scale=gv[par][0:FR, e:e + 1]).then_inc(h_hi, 1)
            elif nxt:
                bank = wait_full(act, step, "XS", b)
                act.activation(xsum[:, :], bank[:, 0:KC], ACT.Copy).then_inc(taken(step, "XS"), 1)
            if nxt:
                for j in range(2):
                    bank = wait_full(act, step, f"XT{j}", b)
                    act.activation(xT[HI][:, 2 * j:2 * j + 2, :],
                                   bank[:, :].rearrange("p (a n) -> p a n", a=2), ACT.Copy).then_inc(x_hi, 1)
            if step == "pro":
                for n in range(NE):
                    high_parts(n)

        walk(act, body)

    @block.vector
    def _(dve):
        dve.wait_ge(const, 8)

        def low_parts(n):
            dve.wait_ge(w_hi, n + 1 if n < NE else NE + 2 * (n - NE + 1))
            for whole, hi in weights(n):
                last = dve.tensor_tensor(whole, whole.bitcast(F32), hi.bitcast(F32), ALU.subtract)
            last.then_inc(w_lo, 1)

        def body(step, b, par, half):
            ffn, nxt_step = step in DOES_FFN, step in DOES_NEXT
            nxt = 1 - par

            def x_low(j):
                dve.wait_ge(x_hi, 2 * (b + 1) + j + 1)
                bank = ring[u.bank(step, f"XT{j}")]
                dve.tensor_tensor(xT[LO][:, 2 * j:2 * j + 2, :],
                                  bank[:, :].rearrange("p (a n) -> p a n", a=2),
                                  xT[HI][:, 2 * j:2 * j + 2, :].bitcast(F32),
                                  ALU.subtract).then_inc(taken(step, f"XT{j}"), 1)

            def residual(e):
                for t in range(T):
                    last = dve.scalar_tensor_tensor(
                        xo[:, t, :], b2_b[:, bass.ds(ex[e], 1), :].rearrange("p a n -> p (a n)"),
                        gv[par][:, e:e + 1], (x2[par] if e == 0 else xo)[:, t, :], ALU.mult, ALU.add)
                    last.then_inc(res, 1)

            if nxt_step:
                dve.wait_ge(x_ld[nxt], 16 * (half + par + 1) if step != "pro" else 16)
                for t in range(T):
                    dve.bn_stats(st6[:, t, :], x2[nxt][:, t, :]).then_inc(ln_st, 1)
                dve.wait_ge(ln_st, T * (b + 2))
                carry_wait(dve, scratch)
                for t in range(T):
                    dve.bn_aggr(mv[:, t, :], st6[:, t, :]).then_inc(ln_ag, 1)
                dve.wait_ge(ln_rs, 2 * (b + 2))
                for t in range(T):
                    dve.tensor_scalar(xh[:, t, :], x2[nxt][:, t, :], mv[:, t, 0:1], rs[:, t:t + 1],
                                      ALU.subtract, ALU.mult).then_inc(xh_rdy, 1)
            if ffn:
                ex = [dve.value_load(idx[par][0:1, e:e + 1], min_val=0, max_val=NE - 1) for e in range(TOP)]
                for n, (t, e) in enumerate(PAIRS):
                    if n == 3:
                        if step == "first":
                            for k in range(NE, 2 * NE):
                                low_parts(k)
                        else:
                            dve.wait_ge(o_st, 16 * b)
                        residual(0)
                    bank = wait_full(dve, step, f"H{n}", b)
                    dve.tensor_tensor(hb[:, n, :], bank[:, 0:FF],
                                      b1_b[:, bass.ds(ex[e], 1), :].rearrange("p a f -> p (a f)"),
                                      ALU.add).then_inc(taken(step, f"H{n}"), 1)
                for t in range(T):
                    bank = ring[u.bank(step, f"HT{t}")]
                    for e in range(TOP):
                        dve.wait_ge(h_hi, 6 * b + 2 * t + 2)
                        part = (slice(None), e, slice(0, FC - 1), slice(t * P, (t + 1) * P))
                        cols = bank[:, e * (FC - 1) * P:(e + 1) * (FC - 1) * P]
                        last = dve.scalar_tensor_tensor(
                            hT[LO][part], cols.rearrange("p (c n) -> p c n", n=P), gv[par][:, e:e + 1],
                            hT[HI][part].bitcast(F32), ALU.mult, ALU.subtract)
                    last.then_inc(taken(step, f"HT{t}"), 1)
                bank = ring[u.bank(step, "HR")]
                for e in range(TOP):
                    dve.wait_ge(h_hi, 6 * b + 6)
                    last = dve.scalar_tensor_tensor(
                        hT[LO][0:FR, e, FC - 1, :], bank[0:FR, e * S:(e + 1) * S], gv[par][0:FR, e:e + 1],
                        hT[HI][0:FR, e, FC - 1, :].bitcast(F32), ALU.mult, ALU.subtract)
                last.then_inc(taken(step, "HR"), 1)
            if nxt_step:
                for j in range(2):
                    x_low(j)
            if ffn:
                dve.wait_ge(res, 2 * T * b + T)
                residual(1)
            if nxt_step:
                bank = wait_full(dve, step, "GT", b)
                dve.tensor_scalar(lg[:, 0:NE], bank[:, 0:NE], 1.0 / S, None,
                                  ALU.mult).then_inc(taken(step, "GT"), 1)
                wait_evac(dve, step, "GT", b)
                carry_wait(dve, scratch)
                dve.max(top[:, :], lg[:, :]).then_inc(g_pick, 1)
                dve.wait_ge(g_pick, 3 * (b + 1) + 1)
                carry_wait(dve, scratch)
                dve.max_index(idx[nxt][:, :], top[:, :], lg[:, :]).then_inc(g_pick, 1)
                dve.tensor_tensor(gd[:, 0:1], top[:, 1:2], top[:, 0:1], ALU.subtract).then_inc(g_pick, 1)
                dve.wait_ge(g_pow, b + 2)
                dve.tensor_scalar(gd[:, 0:1], gd[:, 1:2], 1.0, None, ALU.add).then_inc(g_log, 1)
                dve.wait_ge(g_log, b + 2)
                dve.reciprocal(gv[nxt][:, 0:1], gd[:, 0:1]).then_inc(g_val, 1)
                dve.wait_ge(g_val, 2 * (b + 1) + 1)
                dve.tensor_tensor(gv[nxt][:, 1:2], gv[nxt][:, 0:1], gd[:, 1:2], ALU.mult).then_inc(g_val, 1)
                dve.wait_ge(g_val, 2 * (b + 2))
            if ffn:
                dve.wait_ge(res, 2 * T * (b + 1))
                for t in range(T):
                    bank = wait_full(dve, step, f"OUT{t}", b)
                    dve.tensor_tensor(xo[:, t, :], bank[:, :], xo[:, t, :],
                                      ALU.add).then_inc(taken(step, f"OUT{t}"), 1)
            if step == "pro":
                for n in range(NE):
                    low_parts(n)

        walk(dve, body)


_INS = ['x', 'ctx_1024', 'L0_xattn_Wq', 'L0_xattn_bq', 'L0_xattn_Wk', 'L0_xattn_bk', 'L0_xattn_Wv',
        'L0_xattn_bv', 'L0_xattn_Wkv_dca', 'L0_xattn_bkv_dca', 'L0_xattn_qn_w', 'L0_xattn_qn_b',
        'L0_xattn_kn_w', 'L0_xattn_kn_b', 'L0_xattn_kn_dca_w', 'L0_xattn_kn_dca_b', 'L0_xattn_Wo',
        'L0_xattn_bo', 'L0_ffn_gate_W', 'L0_ffn_W1', 'L0_ffn_b1', 'L0_ffn_W2', 'L0_ffn_b2']
_OUTS = [((16, 256, 512), 'float32')]


def kernel(**inputs):
    import numpy as _np
    import concourse.bacc as _bacc
    from concourse import mybir as _mybir
    from concourse.bass_utils import run_bass_kernel_spmd as _run

    nc = _bacc.Bacc("TRN2", target_bir_lowering=False, num_devices=1)
    arrays, args = {}, []
    for name in _INS:
        a = _np.ascontiguousarray(inputs[name])
        arrays[f"in_{name}_dram"] = a
        args.append(nc.dram_tensor(f"in_{name}_dram", a.shape, _mybir.dt.from_np(a.dtype), kind="ExternalInput").ap())
    for i, (shape, dtype) in enumerate(_OUTS):
        dt = _mybir.dt.from_np(_np.dtype(dtype))
        args.append(nc.dram_tensor(f"out_{i}_dram", shape, dt, kind="ExternalOutput").ap())
    bass_xattn_moe(nc, *args)
    r = _run(nc, [arrays], core_ids=[0])
    got = tuple(r.results[0][f"out_{i}_dram"] for i in range(len(_OUTS)))
    return got[0]
```

```python
from contextlib import ExitStack

import numpy as np
import concourse.bass as bass
from concourse import mybir

F32 = mybir.dt.float32
F32R = mybir.dt.float32r
U32 = mybir.dt.uint32
ALU = mybir.AluOpType
ACT = mybir.ActivationFunctionType
AX_X = mybir.AxisListType.X

P = 128
BANK = 512
H = 16
HD = 32
HP = P // HD
DCA = 16
SCALE = HD ** -0.5
EPS_LN = 1e-5
EPS_QK = 1e-6
EULER = float(np.e)
LEAST = -3.0e38


class Units:

    def __init__(self, banks, steps):
        self.place, self.slope, self.first = {}, {}, {}
        base = [0] * banks
        for step, names, first_b, times in steps:
            per = [len(range(k, len(names), banks)) for k in range(banks)]
            for n, name in enumerate(names):
                self.place[step, name] = (n % banks, base[n % banks] + n // banks)
            self.slope[step], self.first[step] = per, first_b
            base = [base[k] + per[k] * times for k in range(banks)]

    def bank(self, step, name):
        return self.place[step, name][0]

    def count(self, step, name, b):
        k, n = self.place[step, name]
        return (b - self.first[step]) * self.slope[step][k] + n


def wait(eng, sem, value):
    if not isinstance(value, int) or value > 0:
        eng.wait_ge(sem, value)


def bass_xattn_moe(nc, x, ctx, Wq, bq, Wk, bk, Wv, bv, Wdca, bdca, qn_w, qn_b, kn_w, kn_b,
                   kd_w, kd_b, Wo, bo, gate_W, W1, b1, W2, b2, out):
    B, S, D = x.shape
    x2_dram = nc.dram_tensor("x2_scratch", (B, P, S // P, D), F32, kind="Internal").ap()
    vd_dram = nc.dram_tensor("vdca_scratch", (B, DCA, D), F32, kind="Internal").ap()
    with ExitStack() as outer:
        with ExitStack() as stack:
            early = early_buffers(nc, stack, x, ctx)
        moe = MoeInputs(nc, outer, W1, b1, W2, gate_W, x2_dram)
        with ExitStack() as stack:
            attention_phase(nc, stack, early, moe, x, ctx, Wq, bq, Wk, bk, Wv, bv, Wdca, bdca, qn_w,
                            qn_b, kn_w, kn_b, kd_w, kd_b, Wo, bo, x2_dram, vd_dram)
        with ExitStack() as stack:
            ffn_phase(nc, stack, moe, x2_dram, gate_W, W1, b1, W2, b2, out)


def early_buffers(nc, stack, x, ctx):
    _, S, D = x.shape
    KD, KEYS = ctx.shape[2], ctx.shape[1] - DCA
    T, KC, CC, G, NC = S // P, D // P, KD // P, H // HP, 2
    buffers = {}
    for name, shape, dt in (
        ("wq", [P, KC, D], F32), ("wkv", [P, CC, 2 * D], F32),
        ("xin", [P, T, D], F32), ("xh", [P, T, D], F32), ("xT", [P, KC, S], F32),
        ("cT", [P, CC, KEYS], F32),
        ("q1", [P, T, G, HD, HP], F32),
        ("kf", [P, G, KEYS], F32),
        ("q_hi", [P, G, S], F32R), ("q_lo", [P, G, S], F32R),
        ("k_hi", [P, G, KEYS], F32R), ("k_lo", [P, G, KEYS], F32R),
        ("kv1_0", [P, NC, 2, H // 2, 2 * HD], F32), ("qf0", [P, G, S], F32),
        ("QS0", [3 * HD + 2, HP, G, S], F32R),
    ):
        buffers[name] = stack.enter_context(nc.sbuf_tensor(name, shape, dt))
    return buffers


class MoeInputs:

    def __init__(self, nc, stack, W1, b1, W2, gate_W, x2_dram):
        self.NE, self.D, self.FF = W1.shape
        self.W1, self.b1, self.W2, self.gate_W, self.x2_dram = W1, b1, W2, gate_W, x2_dram
        self.FC = -(-self.FF // P)
        self.FR = self.FF - (self.FC - 1) * P
        KC = self.D // P

        def sb(name, shape, dt=F32):
            return stack.enter_context(nc.sbuf_tensor(name, shape, dt))

        self.first = sb("w1_lo", [P, self.NE, KC, self.FF], F32R)
        self.second = sb("w2_lo", [P, self.NE, self.FC, self.D], F32R)
        self.x = sb("x2_0", [P, x2_dram.shape[2], self.D])
        self.b1_b = sb("b1_b", [P, self.NE, self.FF])
        self.gate = sb("gate", [P, KC, self.NE])
        self.loaded = [stack.enter_context(nc.semaphore(f"moe_ld{n}")) for n in range(2 * self.NE)]
        self.x_ld, self.g_ld, self.b1_ld = (
            stack.enter_context(nc.semaphore(n)) for n in ("f_x_ld0", "g_ld", "b1_ld"))

    def load_small(self, eng):
        eng.dma_start(self.x[:, :, :], self.x2_dram[0]).then_inc(self.x_ld, 16)
        for c in range(self.D // P):
            eng.dma_start(self.gate[:, c, :], self.gate_W[:, c * P:(c + 1) * P].rearrange("e p -> p e"),
                          allow_slow_non_contiguous=True).then_inc(self.g_ld, 16)
        eng.dma_start(self.b1_b[:, :, :], self.b1.rearrange("e f -> (e f)").partition_broadcast(P)
                      ).then_inc(self.b1_ld, 16)

    def load(self, eng, n):
        e, FC, FR = n % self.NE, self.FC, self.FR
        if n < self.NE:
            eng.dma_start(self.first[:, e, :, :].bitcast(F32),
                          self.W1[e].rearrange("(c p) f -> p c f", p=P)).then_inc(self.loaded[n], 16)
            return
        eng.dma_start(self.second[:, e, 0:FC - 1, :].bitcast(F32),
                      self.W2[e, 0:(FC - 1) * P].rearrange("(c p) n -> p c n", p=P)
                      ).then_inc(self.loaded[n], 16)
        eng.dma_start(self.second[0:FR, e, FC - 1, :].bitcast(F32),
                      self.W2[e, (FC - 1) * P:self.FF]).then_inc(self.loaded[n], 16)


def carry_wait(dve, scratch):
    return dve.tensor_copy(scratch[:, 0:1], scratch[:, 1:2])


def attention_phase(nc, stack, early, moe, x, ctx, Wq, bq, Wk, bk, Wv, bv, Wdca, bdca, qn_w, qn_b, kn_w, kn_b,
                    kd_w, kd_b, Wo, bo, x2_dram, vd_dram):
    B, S, D = x.shape
    KD = ctx.shape[2]
    KEYS = ctx.shape[1] - DCA
    T = S // P
    KC = D // P
    CC = KD // P
    NC = 2
    CK = KEYS // NC
    G = H // HP
    HH = H // 2
    W = 2 * HD
    BLK = 3 * HD
    ST = BLK + 2
    STACKED = 3 * 16
    EARLY_LOADS = 4
    ND = 2
    BD = B // ND

    x_t = x.rearrange("b (t p) d -> b p t d", p=P)
    ctx_main = ctx[:, 0:KEYS, :].rearrange("b (c p) d -> b p c d", p=CK)

    def sem(name):
        return stack.enter_context(nc.semaphore(name))

    def sb(name, shape, dt=F32):
        return stack.enter_context(nc.sbuf_tensor(name, shape, dt))

    wq, wkv, xin, xh, xT, cT, q1, kf, q_hi, q_lo, k_hi, k_lo = (
        early[n] for n in "wq wkv xin xh xT cT q1 kf q_hi q_lo k_hi k_lo".split())
    cin = sb("cin", [P, NC, KD])
    ident = sb("ident", [P, P])
    wo = sb("wo", [P, KC, D])
    bq_b = sb("bq_b", [P, D])
    bkv_b = sb("bkv_b", [P, 2 * D])
    bo_b = sb("bo_b", [P, D])
    affine = sb("affine", [P, 6])
    sel = sb("sel", [2 * H, 2, P], F32R)
    own = sb("own", [P, HP])
    mask = sb("mask", [P, 2, HH * HD])
    neg_half = sb("neg_half", [P, H])
    eps_ln = sb("eps_ln", [P, T])
    scratch = sb("scratch", [P, 2])
    kn = xh
    xres = sb("xres", [P, T, D])
    kv1 = [early["kv1_0"], sb("kv1_1", [P, NC, 2, HH, W])]
    sq = [sb(f"sq{i}", [P, D]) for i in range(2)]
    vs = sb("vs", [P, 6, H])
    qf = [early["qf0"], sb("qf1", [P, G, S])]
    QS = [early["QS0"], sb("QS1", [ST, HP, G, S], F32R)]
    KS = [sb(f"KS{i}", [ST, HP, G, KEYS], F32R) for i in range(2)]
    st6, mv, rs = sb("st6", [P, T, 6]), sb("mv", [P, T, 2]), sb("rs", [P, T])
    mxa, den, ld, lt = (sb(n, [P, T, 2 * H]) for n in ("mxa", "den", "ld", "lt"))
    nm = sb("nm", [P, T, H])
    ed = sb("ed", [P, T, H, DCA])
    s_hi, s_lo = sb("s_hi", [2 * H, S], F32R), sb("s_lo", [2 * H, S], F32R)
    pt = [sb(f"pt{i}", [P, HP, NC * S]) for i in range(2)]
    pdt = sb("pdt", [P, 2, S])
    kdT = sb("kdT", [P, G, B * DCA])
    kdb = sb("kdb", [P, G, HP * DCA])
    vrep, vbd = sb("vrep", [P, D]), sb("vbd", [P, D])
    ot = sb("ot", [P, G, S])
    wdca = pt[0][:, :, :].rearrange("p a n -> p (a n)").rearrange("p (c n) -> p c n", c=CC)
    spare = pt[1][:, :, :].rearrange("p a n -> p (a n)")
    bd_b = spare[:, 0:2 * D]
    ydca = spare[:, 2 * D:2 * D + ND * KD].rearrange("p (c n) -> p c n", c=ND)
    ydT = spare[:, 3 * D:3 * D + CC * ND * P].rearrange("p (c n) -> p c n", c=CC)
    vdca = ot[:, :, :].rearrange("p a n -> p (a n)").rearrange("p (c n) -> p c n", c=ND)
    dk = kv1[1][:, :, :, :, :].rearrange("p c a h w -> p (c a h w)")
    wsum = den[:, :, :].rearrange("p t n -> p (t n)")

    ring = [stack.enter_context(nc.psum_tensor(f"ring{i}", [P, BANK], F32)) for i in range(4)]
    sc = [stack.enter_context(nc.psum_tensor(f"sc{i}", [P, 2, BANK], F32)) for i in range(2)]

    full = [sem(f"full{i}") for i in range(4)]
    evac = [sem(f"evac{i}") for i in range(4)]
    sc_full = [sem(f"sc_full{i}") for i in range(2)]
    sc_evac = [sem(f"sc_evac{i}") for i in range(2)]
    wq_ld, wkv_ld, b_ld, wd_ld, wo_ld, af_ld = (
        sem(n) for n in "wq_ld wkv_ld b_ld wd_ld wo_ld af_ld".split())
    y_ld, x_ld, c_ld, r_ld, vr_ld = (sem(n) for n in "y_ld x_ld c_ld r_ld vr_ld".split())
    q_in, k_in, sh_in = sem("q_in"), sem("k_in"), sem("sh_in")
    x2_st, vd_st = sem("x2_st"), sem("vd_st")
    const, ones, prep = sem("const"), sem("ones"), sem("prep")
    ln_st, ln_ag, ln_rs, xh_rdy = sem("ln_st"), sem("ln_ag"), sem("ln_rs"), sem("xh_rdy")
    sq_rdy, var_rdy, rstd, norm = sem("sq_rdy"), sem("var_rdy"), sem("rstd"), sem("norm")
    split = sem("split")
    ctx_rdy = sem("ctx_rdy")
    res_rdy, kd_rdy, vbd_rdy = sem("res_rdy"), sem("kd_rdy"), sem("vbd_rdy")
    d_max, d_exp, d_den = sem("d_max"), sem("d_exp"), sem("d_den")
    g_max, ln_rdy, lt_rdy, sh_hi = sem("g_max"), sem("ln_rdy"), sem("lt_rdy"), sem("sh_hi")

    GEMM = ["Q0", "Q1", "KV00", "KV01", "KV10", "KV11"]
    BODY = ["SD", "WO0", "XT0", "XT1", "CT", "Q0", "Q1", "KV00", "KV01", "KV10", "KV11", "WO1",
            "LT", "QT0", "QT1", "SDT", "KT0", "KT1", "PV0", "PV1", "PV2", "PV3"]
    ATTN = ["SD", "LT", "SDT", "PV0", "PV1", "PV2", "PV3"]
    WOUT = ["WO0", "WO1"]
    u = Units(4, [
        ("pro", [n for n in BODY if n not in ATTN + WOUT + ["KT0", "KT1"]] + [
            "YT", "DK0", "DV0", "DK1", "DV1", "KT0", "KT1", "KD0", "KD1"], -1, 1),
        ("first", [n for n in BODY if n not in WOUT], 0, 1),
        ("body", BODY, 1, B - 2),
        ("last", [n for n in BODY if n in ATTN + WOUT], B - 1, 1),
        ("tail", WOUT, B, 1)])
    DOES_ATTN, DOES_PROJ, DOES_WO = ("first", "body", "last"), ("pro", "first", "body"), (
        "body", "last", "tail")

    def begin(eng, step, name, b):
        wait(eng, evac[u.bank(step, name)], u.count(step, name, b))
        return ring[u.bank(step, name)]

    def taken(step, name):
        return evac[u.bank(step, name)]

    def wait_full(eng, step, name, b):
        eng.wait_ge(full[u.bank(step, name)], u.count(step, name, b) + 1)
        return ring[u.bank(step, name)]

    def wait_evac(eng, step, name, b):
        eng.wait_ge(evac[u.bank(step, name)], u.count(step, name, b) + 1)

    def walk(eng, body):
        body("pro", -1, 1)
        body("first", 0, 0)
        with eng.Fori(0, (B - 4) // 2) as i:
            body("body", 2 * i + 1, 1)
            body("body", 2 * i + 2, 0)
        body("body", B - 3, 1)
        body("body", B - 2, 0)
        body("last", B - 1, 1)
        body("tail", B, 0)

    def norms(step, b):
        return 0 if step == "pro" else ND + 6 * (b + 1)

    def heads(packed):
        return packed.rearrange("p (g d h) -> p g h d", d=HD, h=HP)

    def q_values(k):
        return q1[:, k, :, :, :].rearrange("p g d h -> p g h d")

    def dca_values(c):
        return heads(dk[:, c * D:(c + 1) * D])

    def head_norm_values(k, par):
        if k < T:
            return q_values(k)
        half = kv1[par][0:CK, (k - T) // 2, (k - T) % 2, :, 0:HD]
        return half.rearrange("p (g h) d -> p g h d", h=HP)

    def packed_k(k):
        c, half = (k - T) // 2, (k - T) % 2
        return heads(kn[0:CK, c, half * HH * HD:(half + 1) * HH * HD])

    def squares(n, values):
        return sq[n % 2][0:values.shape[0], 0:values.shape[1] * P].rearrange(
            "p (g h d) -> p g h d", h=HP, d=HD)

    def squares_of_head(k, values):
        return vs[0:values.shape[0], k, 0:values.shape[1] * HP].rearrange("p (g h) -> p g h", h=HP)

    block = stack.enter_context(nc.Block())

    @block.sync
    def _(sp):
        sp.dma_start(xin[:, :, :], x_t[0]).then_inc(x_ld, 16)
        sp.dma_start(wq[:, :, :], Wq.rearrange("(c p) n -> p c n", p=P)).then_inc(wq_ld, 16)
        sp.dma_start(cin[0:CK, :, :], ctx_main[0]).then_inc(c_ld, 16)
        sp.dma_start(wkv[:, :, 0:D], Wk.rearrange("(c p) n -> p c n", p=P)).then_inc(wkv_ld, 16)
        sp.dma_start(wkv[:, :, D:2 * D], Wv.rearrange("(c p) n -> p c n", p=P)).then_inc(wkv_ld, 16)
        for dst, src in ((bq_b[:, :], bq), (bkv_b[:, 0:D], bk), (bkv_b[:, D:2 * D], bv)):
            sp.dma_start(dst, src.partition_broadcast(P)).then_inc(b_ld, 16)
        sp.dma_start(wdca, Wdca.rearrange("(c p) n -> p c n", p=P)).then_inc(wd_ld, 16)
        sp.dma_start(bd_b, bdca.partition_broadcast(P)).then_inc(wd_ld, 16)
        sp.dma_start(wo[:, :, :], Wo.rearrange("(c p) n -> p c n", p=P)).then_inc(wo_ld, 16)
        sp.dma_start(bo_b[:, :], bo.partition_broadcast(P)).then_inc(wo_ld, 16)

        def store_vdca():
            for c in range(ND):
                wait_evac(sp, "pro", f"DV{c}", -1)
                sp.dma_start(vd_dram[c * BD:(c + 1) * BD].rearrange("b k n -> (b k) n"),
                             vdca[:, c, :]).then_inc(vd_st, 16)
            sp.wait_ge(vd_st, 16 * ND)

        def load_vrep(b):
            wait(sp, vbd_rdy, b)
            rows = vd_dram[b].unsqueeze(0) if isinstance(b, int) else vd_dram[bass.ds(b, 1)]
            sp.dma_start(vrep[:, :], rows.broadcast_to([HH, DCA, D])).then_inc(vr_ld, 16)

        def stack_parts(b, par, n):
            tensor, hi, lo, order, done = ((QS, q_hi, q_lo, (0, 2, 1), q_in),
                                           (KS, k_hi, k_lo, (0, 1, 2), k_in))[n]
            sp.wait_ge(split, 4 * b + 2 * n + 2)
            dst = tensor[par][:, :, :, :].rearrange("p h g n -> p h (g n)")
            for part, blk in zip((hi, hi, lo), order):
                sp.dma_start(dst[blk * HD:(blk + 1) * HD, :, :].bitcast(F32),
                             part[:, :, :].rearrange("p g n -> p (g n)").bitcast(F32)).then_inc(done, 16)

        def body(step, b, par):
            if step in DOES_PROJ:
                if not (isinstance(b, int) and b + 2 >= B):
                    sp.wait_ge(xh_rdy, T * (b + 2))
                    sp.dma_start(xin[:, :, :], x_t[b + 2]).then_inc(x_ld, 16)
                    wait_full(sp, step, "CT", b)
                    sp.dma_start(cin[0:CK, :, :], ctx_main[b + 2]).then_inc(c_ld, 16)
                if step != "pro":
                    load_vrep(b + 1)
            if step == "last":
                sp.wait_ge(ctx_rdy, B - 1)
                sp.wait_ge(q_in, STACKED * B)
                sp.wait_ge(k_in, STACKED * B)
                moe.load_small(sp)
                for n in range(EARLY_LOADS):
                    moe.load(sp, n)
            if step in DOES_ATTN:
                wait_evac(sp, step, "LT", b)
                for row, part in ((BLK, s_hi), (BLK + 1, s_lo)):
                    sp.dma_start(QS[par][row:row + 1, :, :, :].rearrange("p h g n -> p (h g) n").bitcast(F32),
                                 part[0:H, :].bitcast(F32)).then_inc(sh_in, 16)
            if step in DOES_WO:
                wait_evac(sp, step, "WO0", b)
                wait_evac(sp, step, "WO1", b)
                sp.dma_start(x2_dram[b - 1], xres[:, :, :]).then_inc(x2_st, 16)
            if step in DOES_PROJ:
                stack_parts(b + 1, 1 - par, 0)
            if step in DOES_WO:
                sp.wait_ge(x2_st, 16 * b)
            if step in DOES_ATTN:
                sp.dma_start(xres[:, :, :], x_t[b]).then_inc(r_ld, 16)
            if step == "last":
                for n in range(EARLY_LOADS, 2 * moe.NE):
                    moe.load(sp, n)
            if step in DOES_PROJ:
                stack_parts(b + 1, 1 - par, 1)
            if step == "pro":
                store_vdca()
                load_vrep(0)

        walk(sp, body)

    @block.gpsimd
    def _(pool):
        sel32 = sq[0][0:2 * H, 0:2 * P]
        pool.memset(ident[:, :], 0.0).then_inc(const, 1)
        pool.memset(sel32, 0.0).then_inc(const, 1)
        pool.memset(mask[:, :, :], 1.0).then_inc(const, 1)
        pool.memset(neg_half[:, :], -0.5).then_inc(const, 1)
        pool.memset(eps_ln[:, :], EPS_LN).then_inc(const, 1)
        pool.memset(scratch[:, :], 0.0).then_inc(const, 1)
        pool.wait_ge(const, 6)
        pool.affine_select(out=ident[:, :], in_=ident[:, :], compare_op=ALU.not_equal, fill=1.0,
                           base=0, pattern=[[-1, P]], channel_multiplier=1).then_inc(const, 1)
        sel_v = sel32.rearrange("j (a h k) -> j (a h) k", a=2, h=HH)
        pool.affine_select(out=sel_v, in_=sel_v, compare_op=ALU.not_equal, fill=1.0, base=-H,
                           pattern=[[-1, H], [0, DCA]], channel_multiplier=1).then_inc(const, 1)
        for a in range(2):
            m = mask[:, a, :].rearrange("p (h d) -> p h d", h=HH)
            pool.affine_select(out=m, in_=m, compare_op=ALU.is_ge, fill=0.0, base=0,
                               pattern=[[-DCA, HH], [0, HD]], channel_multiplier=1).then_inc(const, 1)
        pool.wait_ge(const, 10)
        for a in range(2):
            m = mask[:, a, :].rearrange("p (h d) -> p h d", h=HH)
            pool.affine_select(out=m, in_=m, compare_op=ALU.is_ge, fill=0.0, base=DCA - 1,
                               pattern=[[DCA, HH], [0, HD]], channel_multiplier=-1).then_inc(const, 1)
        pool.tensor_copy(sel[:, :, :].rearrange("j a p -> j (a p)"), sel32).then_inc(const, 1)
        for i in range(2):
            wait(pool, ones, i)
            pool.wait_ge(const, 13)
            pool.memset(KS[i][BLK:ST, :, :, :].bitcast(F32), 1.0).then_inc(ones, 1)
        pool.wait_ge(ones, 2)

        def root(k, n, rows, heads):
            w = vs[0:rows, k, 0:heads]
            pool.wait_ge(var_rdy, 2 * (n + 1))
            pool.tensor_tensor(w, w, neg_half[0:rows, 0:heads], ALU.pow).then_inc(rstd, 1)

        def body(step, b, par):
            if step in DOES_PROJ:
                pool.wait_ge(ln_ag, T * (b + 2))
                pool.tensor_tensor(rs[:, :], mv[:, :, 1], eps_ln[:, :], ALU.add).then_inc(ln_rs, 1)
                pool.wait_ge(ln_rs, 2 * (b + 1) + 1)
                pool.tensor_tensor(rs[:, :], rs[:, :], neg_half[:, 0:T], ALU.pow).then_inc(ln_rs, 1)
            if step in DOES_PROJ:
                for k in range(6):
                    root(k, norms(step, b) + k, P if k < T else CK, H if k < T else HH)
            if step == "pro":
                for c in range(ND):
                    root(c, 6 + c, P, H)
            if step in DOES_ATTN:
                pool.wait_ge(r_ld, 16 * (b + 1))
                pool.wait_ge(wo_ld, 32)
                pool.tensor_tensor(xres[:, :, :], xres[:, :, :],
                                   bo_b[:, :].unsqueeze(1).broadcast_to([P, T, D]),
                                   ALU.add).then_inc(res_rdy, 1)
            if step in DOES_PROJ:
                pool.wait_ge(vr_ld, 16 * (b + 2))
                if step in DOES_ATTN:
                    pool.wait_ge(full[u.bank(step, "PV3")], u.count(step, "PV3", b) + 1)
                pool.tensor_tensor(vbd[:, :], vrep[:, :], mask[:, :, :].rearrange("p a n -> p (a n)"),
                                   ALU.mult).then_inc(vbd_rdy, 1)

        walk(pool, body)

    @block.tensor
    def _(pe):
        pe.wait_ge(const, 13)

        def project_dca():
            pe.wait_ge(y_ld, 16 * ND)
            bank = begin(pe, "pro", "YT", -1)
            for cc in range(CC):
                for c in range(ND):
                    last = pe.transpose(bank[:, (cc * ND + c) * P:(cc * ND + c + 1) * P],
                                        ydca[:, c, cc * P:(cc + 1) * P], ident[:, :])
            last.then_inc(full[u.bank("pro", "YT")], 1)
            wait_evac(pe, "pro", "YT", -1)
            pe.wait_ge(prep, 14)
            for c in range(ND):
                for half, name in enumerate((f"DK{c}", f"DV{c}")):
                    bank = begin(pe, "pro", name, -1)
                    for cc in range(CC):
                        last = pe.matmul(bank[:, :], ydT[:, cc, c * P:(c + 1) * P],
                                         wdca[:, cc, half * D:(half + 1) * D],
                                         start=(cc == 0), stop=(cc == CC - 1))
                    last.then_inc(full[u.bank("pro", name)], 1)

        def dca_k_transposes():
            for j in range(2):
                bank = begin(pe, "pro", f"KD{j}", -1)
                pe.wait_ge(norm, 6 + ND)
                for g in range(2):
                    for c in range(ND):
                        first = c * D + (2 * j + g) * P
                        last = pe.transpose(bank[:, (g * ND + c) * P:(g * ND + c + 1) * P],
                                            dk[:, first:first + P], ident[:, :])
                last.then_inc(full[u.bank("pro", f"KD{j}")], 1)

        def x_transposes(step, b):
            pe.wait_ge(xh_rdy, T * (b + 2))
            for j in range(2):
                bank = begin(pe, step, f"XT{j}", b)
                for k in range(2):
                    for t in range(T):
                        last = pe.transpose(bank[:, (k * T + t) * P:(k * T + t + 1) * P],
                                            xh[:, t, (2 * j + k) * P:(2 * j + k + 1) * P], ident[:, :])
                last.then_inc(full[u.bank(step, f"XT{j}")], 1)

        def context_transposes(step, b):
            pe.wait_ge(c_ld, 16 * (b + 2))
            bank = begin(pe, step, "CT", b)
            for cc in range(CC):
                for c in range(NC):
                    last = pe.transpose(bank[:, cc * KEYS + c * CK:cc * KEYS + (c + 1) * CK],
                                        cin[0:CK, c, cc * P:(cc + 1) * P], ident[0:CK, 0:CK])
            last.then_inc(full[u.bank(step, "CT")], 1)

        def project(step, b, k):
            name = GEMM[k]
            bank = begin(pe, step, name, b)
            if k < T:
                wait_evac(pe, step, "XT0", b)
                wait_evac(pe, step, "XT1", b)
                if step == "pro":
                    pe.wait_ge(prep, 2)
                for kc in range(KC):
                    last = pe.matmul(bank[:, :], xT[:, kc, k * P:(k + 1) * P], wq[:, kc, :],
                                     start=(kc == 0), stop=(kc == KC - 1))
            else:
                c, half = (k - T) // 2, (k - T) % 2
                wait_evac(pe, step, "CT", b)
                if step == "pro":
                    pe.wait_ge(prep, 4)
                for cc in range(CC):
                    last = pe.matmul(bank[0:CK, :], cT[:, cc, c * CK:(c + 1) * CK],
                                     wkv[:, cc, half * D:(half + 1) * D],
                                     start=(cc == 0), stop=(cc == CC - 1))
            last.then_inc(full[u.bank(step, name)], 1)

        def q_transposes(step, b, j):
            bank = begin(pe, step, f"QT{j}", b)
            pe.wait_ge(norm, norms(step, b) + T)
            for g in range(2):
                for t in range(T):
                    last = pe.transpose(bank[:, g * S + t * P:g * S + (t + 1) * P],
                                        q1[:, t, 2 * j + g, :, :].rearrange("p d h -> p (d h)"),
                                        ident[:, :])
            last.then_inc(full[u.bank(step, f"QT{j}")], 1)

        def k_transposes(step, b):
            pe.wait_ge(norm, norms(step, b) + 6)
            for j in range(2):
                bank = begin(pe, step, f"KT{j}", b)
                for g in range(2):
                    for c in range(NC):
                        last = pe.transpose(bank[:, g * KEYS + c * CK:g * KEYS + (c + 1) * CK],
                                            kn[0:CK, c, (2 * j + g) * P:(2 * j + g + 1) * P],
                                            ident[0:CK, 0:CK])
                last.then_inc(full[u.bank(step, f"KT{j}")], 1)

        def dca_scores(step, b, par):
            bank = begin(pe, step, "SD", b)
            pe.wait_ge(split, 4 * b + 1)
            pe.wait_ge(kd_rdy, b + 1)
            for t in range(T):
                for g in range(G):
                    o = (t * G + g) * HP * DCA
                    last = pe.matmul(bank[:, o:o + HP * DCA], qf[par][:, g, t * P:(t + 1) * P],
                                     kdb[:, g, :], start=True, stop=True)
            last.then_inc(full[u.bank(step, "SD")], 1)

        def scores(b, par, k):
            if k == 0:
                pe.wait_ge(q_in, STACKED * (b + 1))
                pe.wait_ge(k_in, STACKED * (b + 1))
            wait(pe, sc_evac[k % 2], 8 * b + k // 2)
            t, quad = k // G, k % G
            for i in range(HP):
                last = pe.matmul(sc[k % 2][:, i // 2, (i % 2) * KEYS:(i % 2 + 1) * KEYS],
                                 QS[par][0:BLK, i, quad, t * P:(t + 1) * P], KS[par][0:BLK, i, quad, :],
                                 start=True, stop=True)
            last.then_inc(sc_full[k % 2], 1)

        def shift_transposes(step, b):
            bank = begin(pe, step, "LT", b)
            pe.wait_ge(lt_rdy, b + 1)
            for t in range(T):
                last = pe.transpose(bank[0:2 * H, t * P:(t + 1) * P], lt[:, t, :], ident[:, :])
            last.then_inc(full[u.bank(step, "LT")], 1)

        def dca_scores_t(step, b, par):
            bank = begin(pe, step, "SDT", b)
            wait_evac(pe, step, "LT", b)
            for a in range(2):
                cols = bank[:, a * S:(a + 1) * S]
                pe.matmul(cols, sel[:, a, :], s_hi[:, :], start=True, stop=False, skip_group_check=True)
                pe.matmul(cols, sel[:, a, :], s_lo[:, :], start=False, stop=False, skip_group_check=True)
                for g in range(2):
                    last = pe.matmul(bank[g * 64:(g + 1) * 64, a * S:(a + 1) * S],
                                     kdb[:, 2 * a + g, :], qf[par][:, 2 * a + g, :],
                                     start=False, stop=True, skip_group_check=True)
            last.then_inc(full[u.bank(step, "SDT")], 1)

        def scores_t(b, par, p):
            if p == 0:
                pe.wait_ge(sh_in, 32 * (b + 1))
                pe.wait_ge(ones, 2)
            pe.wait_ge(sc_evac[p % 2], 8 * b + 4 + p // 2)
            for i in range(2):
                g, h = divmod(2 * p + i, HP)
                for c in range(NC):
                    last = pe.matmul(sc[p % 2][0:CK, i, c * S:(c + 1) * S],
                                     KS[par][:, h, g, c * CK:(c + 1) * CK],
                                     QS[par][:, h, g, :], start=True, stop=True)
            last.then_inc(sc_full[p % 2], 1)

        def values(step, b, par, g):
            bank = begin(pe, step, f"PV{g}", b)
            for i in range(2):
                pe.wait_ge(sc_evac[i], 8 * b + 4 + g + 1)
            for c in range(NC):
                for i in range(HP):
                    h = g * HP + i
                    pe.matmul(bank[i * HD:(i + 1) * HD, 0:S],
                              kv1[par][0:CK, c, h // HH, h % HH, HD:W],
                              pt[g % 2][0:CK, i, c * S:(c + 1) * S],
                              start=(c == 0), stop=False, skip_group_check=True)
            if g == 0:
                wait_evac(pe, step, "SDT", b)
                pe.wait_ge(vbd_rdy, b + 1)
            pe.matmul(bank[:, 0:S], vbd[:, g * P:(g + 1) * P], pdt[:, g // 2, :],
                      start=False, stop=True, skip_group_check=True
                      ).then_inc(full[u.bank(step, f"PV{g}")], 1)

        def out_projection(step, b, t):
            bank = begin(pe, step, f"WO{t}", b)
            for g in range(G):
                last = pe.matmul(bank[:, :], ot[:, g, t * P:(t + 1) * P], wo[:, g, :],
                                 start=(g == 0), stop=(g == G - 1))
            last.then_inc(full[u.bank(step, f"WO{t}")], 1)

        def body(step, b, par):
            attn, proj, wout = step in DOES_ATTN, step in DOES_PROJ, step in DOES_WO
            if attn:
                dca_scores(step, b, par)
            if wout:
                if attn:
                    pe.wait_ge(ctx_rdy, b)
                else:
                    wait_evac(pe, "last", "PV3", B - 1)
                out_projection(step, b, 0)
            if proj:
                x_transposes(step, b)
            if attn:
                scores(b, par, 0)
                scores(b, par, 1)
            if proj:
                context_transposes(step, b)
            for groups, units in (
                    ((), (0,)), ((2, 3), (1,)), ((4,), (2,)), ((5,), (3,)), ((6, 7), (4, 5))):
                if attn:
                    for k in groups:
                        scores(b, par, k)
                if proj:
                    for k in units:
                        project(step, b, k)
            if wout:
                out_projection(step, b, 1)
            if attn:
                shift_transposes(step, b)
            if proj:
                q_transposes(step, b, 0)
                q_transposes(step, b, 1)
            if attn:
                dca_scores_t(step, b, par)
                scores_t(b, par, 0)
                scores_t(b, par, 1)
            if step == "pro":
                project_dca()
            if proj:
                k_transposes(step, b)
            if step == "pro":
                dca_k_transposes()
                pe.wait_ge(wo_ld, 32)
            if attn:
                scores_t(b, par, 2)
                scores_t(b, par, 3)
                for g in range(3):
                    values(step, b, par, g)
                    if g < 2:
                        scores_t(b, par, 4 + 2 * g)
                        scores_t(b, par, 5 + 2 * g)
                values(step, b, par, 3)

        walk(pe, body)

    @block.scalar
    def _(act):
        for c in range(ND):
            act.dma_start(ydca[:, c, :],
                          ctx[c * BD:(c + 1) * BD, KEYS:KEYS + DCA, :]).then_inc(y_ld, 16)
        for n, vec in enumerate((qn_w, qn_b, kn_w, kn_b, kd_w, kd_b)):
            act.dma_start(affine[:, n:n + 1], vec.unsqueeze(1).unsqueeze(2).broadcast_to([HD, HP, 1]),
                          allow_slow_non_contiguous=True).then_inc(af_ld, 16)

        def copy_out(step, b, name, dst, cols):
            bank = wait_full(act, step, name, b)
            act.activation(dst, bank[:, 0:cols].rearrange("p (a n) -> p a n", a=dst.shape[1]),
                           ACT.Copy).then_inc(taken(step, name), 1)

        def square(step, b, name, n, values):
            wait_evac(act, step, name, b)
            wait(act, var_rdy, 2 * (n - 1))
            act.activation(squares(n, values), values, ACT.Square, scale=HD ** -0.5).then_inc(sq_rdy, 1)

        def affine_out(step, b, name, dst, cols, n):
            bank = wait_full(act, step, name, b)
            act.activation(dst, bank[:, 0:cols].rearrange("p (a n) -> p a n", a=2), ACT.Identity,
                           bias=affine[:, n + 1:n + 2], scale=affine[:, n:n + 1]
                           ).then_inc(taken(step, name), 1)

        act.wait_ge(const, 13)
        act.wait_ge(af_ld, 16 * 6)

        def exps(b, k):
            act.wait_ge(g_max, 16 * b + 2 * k + 2)
            t, quad = k // G, k % G
            for i in range(HP):
                h = i * G + quad
                s = sc[k % 2][:, i // 2, (i % 2) * KEYS:(i % 2 + 1) * KEYS]
                last = act.activation(s, s, ACT.Exp, bias=nm[:, t, h:h + 1], scale=SCALE,
                                      accum_out=den[:, t, h:h + 1])
            last.then_inc(sc_evac[k % 2], 1)

        def probabilities(step, b, p):
            g = p // 2
            act.wait_ge(sc_full[p % 2], 8 * b + 4 + p // 2 + 1)
            if g >= 2 and p % 2 == 0:
                wait_full(act, step, f"PV{g - 2}", b)
            act.activation(pt[g % 2][0:CK, (p % 2) * 2:(p % 2) * 2 + 2, :], sc[p % 2][0:CK, :, :],
                           ACT.Exp, scale=SCALE).then_inc(sc_evac[p % 2], 1)

        def body(step, b, par):
            attn, proj = step in DOES_ATTN, step in DOES_PROJ

            def sq_unit(k):
                square(step, b, GEMM[k], norms(step, b) + k, head_norm_values(k, 1 - par))

            if attn:
                wait_evac(act, step, "SD", b)
                act.activation(ed[:, :, :, :], ed[:, :, :, :], ACT.Exp, scale=SCALE).then_inc(d_exp, 1)
            if proj:
                copy_out(step, b, "XT0", xT[:, 0:2, :], 2 * S)
                copy_out(step, b, "XT1", xT[:, 2:4, :], 2 * S)
            if attn:
                exps(b, 0)
                exps(b, 1)
            if proj:
                copy_out(step, b, "CT", cT[:, :, :], CC * KEYS)
                sq_unit(0)
            if attn:
                exps(b, 2)
                exps(b, 3)
            if proj:
                sq_unit(1)
            if attn:
                exps(b, 4)
                exps(b, 5)
            if proj:
                sq_unit(2)
                sq_unit(3)
            if attn:
                exps(b, 6)
                exps(b, 7)
            if proj:
                sq_unit(4)
            if attn:
                act.wait_ge(d_den, b + 1)
                for i in range(2):
                    act.wait_ge(sc_evac[i], 8 * b + 4)
                act.activation(ld[:, :, :], den[:, :, :], ACT.Ln).then_inc(ln_rdy, 1)
            if proj:
                sq_unit(5)
                affine_out(step, b, "QT0", qf[1 - par][:, 0:2, :], 2 * S, 0)
                affine_out(step, b, "QT1", qf[1 - par][:, 2:4, :], 2 * S, 0)
            if attn:
                bank = wait_full(act, step, "SDT", b)
                act.activation(pdt[:, :, :], bank[:, :].rearrange("p (a n) -> p a n", a=2), ACT.Exp,
                               scale=SCALE).then_inc(taken(step, "SDT"), 1)
                probabilities(step, b, 0)
                probabilities(step, b, 1)
            if step == "pro":
                copy_out("pro", -1, "YT", ydT, CC * ND * P)
                for c in range(ND):
                    square("pro", -1, f"DK{c}", 6 + c, dca_values(c))
            if proj:
                wait(act, split, 4 * (b + 1))
                affine_out(step, b, "KT0", kf[:, 0:2, :], 2 * KEYS, 2)
                affine_out(step, b, "KT1", kf[:, 2:4, :], 2 * KEYS, 2)
            if step == "pro":
                for j in range(2):
                    affine_out("pro", -1, f"KD{j}", kdT[:, 2 * j:2 * j + 2, :], 2 * ND * P, 4)
            if attn:
                for p in range(2, 8):
                    probabilities(step, b, p)

        walk(act, body)

    @block.vector
    def _(dve):
        dve.wait_ge(const, 13)
        per_head = (
            (wq_ld, 16, wq[:, :, :].rearrange("p c (h d) -> p (c h) d", d=HD)),
            (wkv_ld, 32, wkv[:, :, :].rearrange("p c (h w) -> p (c h) w", w=W)[:, :, 0:HD]),
            (b_ld, 48, bq_b[:, :].rearrange("p (h d) -> p h d", d=HD)),
            (b_ld, 48, bkv_b[:, :].rearrange("p (h w) -> p h w", w=W)[:, :, 0:HD]),
            (wd_ld, 32, wdca[:, 0, 0:D].rearrange("p (h d) -> p h d", d=HD)),
            (wd_ld, 32, wdca[:, 1, 0:D].rearrange("p (h d) -> p h d", d=HD)),
            (wd_ld, 32, bd_b[:, 0:D].rearrange("p (h d) -> p h d", d=HD)),
        )

        def centre(n):
            loaded, count, w = per_head[n]
            dve.wait_ge(loaded, count)
            sums = wsum[:, 0:w.shape[1]]
            dve.tensor_reduce(sums, w, AX_X, ALU.add).then_inc(prep, 1)
            dve.wait_ge(prep, 2 * n + 1)
            dve.scalar_tensor_tensor(w, sums.unsqueeze(2).broadcast_to(w.shape), -1.0 / HD, w,
                                     ALU.mult, ALU.add).then_inc(prep, 1)
            dve.wait_ge(prep, 2 * n + 2)

        def by_head(columns):
            return columns.rearrange("p (g h d) -> p g h d", h=HP, d=HD)

        def sum_squares(k, n, values):
            dve.wait_ge(sq_rdy, n + 1)
            w = squares_of_head(k, values)
            dve.tensor_reduce(w, squares(n, values), AX_X, ALU.add).then_inc(var_rdy, 1)
            dve.wait_ge(var_rdy, 2 * n + 1)
            dve.tensor_scalar(w, w, EPS_QK, None, ALU.add).then_inc(var_rdy, 1)

        def normalise(k, n, values, normal):
            dve.wait_ge(rstd, n + 1)
            w = squares_of_head(k, values)
            dve.tensor_tensor(normal, values, w.unsqueeze(3).broadcast_to(values.shape),
                              ALU.mult).then_inc(norm, 1)

        def dca_units():
            for c in range(ND):
                for dst, name, half in ((dca_values(c), f"DK{c}", 0), (vdca[:, c, :], f"DV{c}", 1)):
                    bank = wait_full(dve, "pro", name, -1)
                    made, bias = bank[:, :], bd_b[:, half * D:(half + 1) * D]
                    if half == 0:
                        made, bias = by_head(made), by_head(bias)
                    dve.tensor_tensor(dst, made, bias, ALU.add).then_inc(taken("pro", name), 1)
            for c in range(ND):
                sum_squares(c, 6 + c, dca_values(c))

        def row_stats(b):
            dve.wait_ge(x_ld, 16 * (b + 2))
            for t in range(T):
                dve.bn_stats(st6[:, t, :], xin[:, t, :]).then_inc(ln_st, 1)
            dve.wait_ge(ln_st, T * (b + 2))
            carry_wait(dve, scratch)
            for t in range(T):
                dve.bn_aggr(mv[:, t, :], st6[:, t, :]).then_inc(ln_ag, 1)

        def row_norm(b):
            dve.wait_ge(ln_rs, 2 * (b + 2))
            for t in range(T):
                dve.tensor_scalar(xh[:, t, :], xin[:, t, :], mv[:, t, 0:1], rs[:, t:t + 1],
                                  ALU.subtract, ALU.mult).then_inc(xh_rdy, 1)

        def group_max(b, k):
            t, quad = k // G, k % G
            dve.wait_ge(sc_full[k % 2], 8 * b + k // 2 + 1)
            s = sc[k % 2][:, :, 0:2 * KEYS].rearrange("p a (h n) -> p a h n", h=2)
            mx = mxa[:, t, 0:H].rearrange("p (h g) -> p h g", g=G)[:, :, quad]
            dve.tensor_reduce(mx.rearrange("p (a h) -> p a h", a=2), s, AX_X, ALU.max).then_inc(g_max, 1)
            dve.wait_ge(g_max, 16 * b + 2 * k + 1)
            dve.tensor_scalar(nm[:, t, :].rearrange("p (h g) -> p h g", g=G)[:, :, quad], mx, -SCALE, None,
                              ALU.mult).then_inc(g_max, 1)

        def bias_out(step, b, k, par):
            bank = wait_full(dve, step, GEMM[k], b)
            if k < T:
                dst, bias, rows = q_values(k), by_head(bq_b[:, :]), P
            else:
                c, half = (k - T) // 2, (k - T) % 2
                dst = kv1[par][0:CK, c, half, :, :].rearrange("p h w -> p (h w)")
                bias, rows = bkv_b[0:CK, half * D:(half + 1) * D], CK
            made = by_head(bank[:, :]) if k < T else bank[0:rows, :]
            dve.tensor_tensor(dst, made, bias, ALU.add).then_inc(taken(step, GEMM[k]), 1)

        def split_parts(step, b, n, names, whole, hi, lo, stacked):
            for name in names:
                wait_evac(dve, step, name, b)
            wait(dve, stacked, STACKED * (b + 1))
            dve.tensor_copy(hi[:, :, :], whole[:, :, :]).then_inc(split, 1)
            dve.wait_ge(split, 4 * (b + 1) + n + 1)
            dve.tensor_tensor(lo[:, :, :], whole[:, :, :], hi[:, :, :].bitcast(F32),
                              ALU.subtract).then_inc(split, 1)

        def dca_keys(b):
            shape = [P, G, HP, DCA]
            dve.tensor_tensor(kdb[:, :, :].rearrange("p g (h k) -> p g h k", h=HP),
                              kdT[:, :, bass.ts(b, DCA)].unsqueeze(2).broadcast_to(shape),
                              own[:, :].unsqueeze(1).unsqueeze(3).broadcast_to(shape),
                              ALU.mult).then_inc(kd_rdy, 1)

        def ctx_out(step, b, g):
            bank = wait_full(dve, step, f"PV{g}", b)
            dve.tensor_copy(ot[:, g, :], bank[:, 0:S]).then_inc(taken(step, f"PV{g}"), 1)

        def residual(step, b, t):
            if t == 0:
                dve.wait_ge(res_rdy, b)
            bank = wait_full(dve, step, f"WO{t}", b)
            dve.tensor_tensor(xres[:, t, :], bank[:, :], xres[:, t, :],
                              ALU.add).then_inc(taken(step, f"WO{t}"), 1)

        def body(step, b, par):
            attn, proj, wout = step in DOES_ATTN, step in DOES_PROJ, step in DOES_WO
            n = norms(step, b)

            def bias(k):
                bias_out(step, b, k, 1 - par)

            def scale(k):
                values = head_norm_values(k, 1 - par)
                normalise(k, n + k, values, values if k < T else packed_k(k))

            def var(k):
                sum_squares(k, n + k, head_norm_values(k, 1 - par))

            if proj:
                row_stats(b)
            if step == "pro":
                centre(0)
            if attn:
                bank = wait_full(dve, step, "SD", b)
                s = bank[:, :].rearrange("p (t h k) -> p t h k", t=T, h=H)
                dve.tensor_reduce(mxa[:, :, H:2 * H], s, AX_X, ALU.max).then_inc(d_max, 1)
                dve.wait_ge(d_max, b + 1)
                dve.tensor_tensor(ed[:, :, :, :], s, mxa[:, :, H:2 * H].unsqueeze(3).broadcast_to(
                    [P, T, H, DCA]), ALU.subtract).then_inc(taken(step, "SD"), 1)
            if proj:
                row_norm(b)
            if step == "pro":
                for k in range(1, 7):
                    centre(k)
            if wout:
                residual(step, b, 0)
            if attn:
                group_max(b, 0)
                group_max(b, 1)
                dve.wait_ge(d_exp, b + 1)
                dve.tensor_reduce(den[:, :, H:2 * H], ed[:, :, :, :], AX_X, ALU.add).then_inc(d_den, 1)
            if proj:
                bias(0)
            if attn:
                group_max(b, 2)
            if proj:
                var(0)
            if attn:
                group_max(b, 3)
            if proj:
                bias(1)
            if attn:
                group_max(b, 4)
                group_max(b, 5)
            if proj:
                var(1)
                scale(0)
                bias(2)
                bias(3)
            if attn:
                group_max(b, 6)
            if proj:
                var(2)
            if attn:
                group_max(b, 7)
            if proj:
                bias(4)
                var(3)
                scale(1)
                bias(5)
                scale(2)
                var(4)
            if attn:
                dve.wait_ge(ln_rdy, b + 1)
                dve.scalar_tensor_tensor(lt[:, :, :], ld[:, :, :], -1.0 / SCALE, mxa[:, :, :],
                                         ALU.mult, ALU.subtract).then_inc(lt_rdy, 1)
            if wout:
                residual(step, b, 1)
            if attn:
                bank = wait_full(dve, step, "LT", b)
                dve.tensor_copy(s_hi[:, :], bank[0:2 * H, 0:S]).then_inc(sh_hi, 1)
                dve.wait_ge(sh_hi, b + 1)
                dve.tensor_tensor(s_lo[:, :], bank[0:2 * H, 0:S], s_hi[:, :].bitcast(F32),
                                  ALU.subtract).then_inc(taken(step, "LT"), 1)
            if proj:
                var(5)
                for k in range(3, 6):
                    scale(k)
                split_parts(step, b, 0, ("QT0", "QT1"), qf[1 - par], q_hi, q_lo, q_in)
                if attn:
                    wait_evac(dve, step, "SDT", b)
                    dca_keys(b + 1)
            if step == "pro":
                dve.tensor_reduce(own[:, :], ident[:, :].rearrange("p (d h) -> p h d", h=HP), AX_X,
                                  ALU.add).then_inc(prep, 1)
                dve.wait_ge(prep, 15)
                dca_units()
            if proj:
                split_parts(step, b, 2, ("KT0", "KT1"), kf, k_hi, k_lo, k_in)
            if step == "pro":
                for c in range(ND):
                    normalise(c, 6 + c, dca_values(c), dca_values(c))
                for c in range(ND):
                    wait_evac(dve, "pro", f"KD{c}", -1)
                dca_keys(0)
                dve.wait_ge(vd_st, 16 * ND)
            if attn:
                for g in range(G):
                    ctx_out(step, b, g)
                wait_evac(dve, step, f"PV{G - 1}", b)
                carry_wait(dve, scratch).then_inc(ctx_rdy, 1)

        walk(dve, body)


def ffn_phase(nc, stack, moe, x2_dram, gate_W, W1, b1, W2, b2, out):
    B, _, T, D = x2_dram.shape
    NE, _, FF = W1.shape
    S = T * P
    KC = D // P
    FC, FR = moe.FC, moe.FR
    TOP = 2
    PAIRS = [(t, e) for t in range(T) for e in range(TOP)]
    out_t = out.rearrange("b (t p) d -> b p t d", p=P)

    def sem(name):
        return stack.enter_context(nc.semaphore(name))

    def sb(name, shape, dt=F32):
        return stack.enter_context(nc.sbuf_tensor(name, shape, dt))

    ident = sb("f_ident", [P, P])
    w1 = [sb("w1_hi", [P, NE, KC, FF], F32R), moe.first]
    w2 = [sb("w2_hi", [P, NE, FC, D], F32R), moe.second]
    b2_b = sb("b2_b", [P, NE, D])
    b1_b, gate = moe.b1_b, moe.gate
    neg_half, eps_ln = sb("f_neg_half", [P, T]), sb("f_eps_ln", [P, T])
    ones = sb("f_ones", [P, 1])
    scratch = sb("f_scratch", [P, 2])
    euler = sb("euler", [P, 1])
    x2 = [moe.x, sb("x2_1", [P, T, D])]
    xo = sb("xo", [P, T, D])
    xh = sb("f_xh", [P, T, D])
    xT = [sb(f"f_xT_{part}", [P, KC, S], F32R) for part in ("hi", "lo")]
    xsum = sb("xsum", [P, KC])
    st6, mv, rs = sb("f_st6", [P, T, 6]), sb("f_mv", [P, T, 2]), sb("f_rs", [P, T])
    lg = sb("lg", [P, 8])
    top = sb("top", [P, 8])
    idx = [sb(f"idx{i}", [P, 8], U32) for i in range(2)]
    gd = sb("gd", [P, 2])
    gv = [sb(f"gv{i}", [P, TOP]) for i in range(2)]
    hb = sb("hb", [P, len(PAIRS), FF])
    hT = [sb(f"hT_{part}", [P, TOP, FC, S], F32R) for part in ("hi", "lo")]
    HI, LO = 0, 1
    SPLIT_PRO = 3
    PASSES = ((HI, HI), (HI, LO), (LO, HI))

    ring = [stack.enter_context(nc.psum_tensor(f"f_ring{i}", [P, BANK], F32)) for i in range(8)]
    full = [sem(f"f_full{i}") for i in range(8)]
    evac = [sem(f"f_evac{i}") for i in range(8)]
    g_ld, o_st, x_ld = moe.g_ld, sem("o_st"), [moe.x_ld, sem("f_x_ld1")]
    b_ld = sem("f_b_ld")
    w_hi, w_lo = sem("w_hi"), sem("w_lo")
    const, ln_st, ln_ag, ln_rs, xh_rdy = (sem("f_" + n) for n in "const ln_st ln_ag ln_rs xh_rdy".split())
    g_log, g_pick, g_pow, g_val = sem("g_log"), sem("g_pick"), sem("g_pow"), sem("g_val")
    h_rdy, res = sem("h_rdy"), sem("res")
    x_hi, h_hi = sem("x_hi"), sem("h_hi")

    BODY = ["H0", "H1", "H2", "XS", "H3", "HT0", "GT", "XT0", "HT1", "HR", "XT1", "OUT0", "OUT1"]
    NEXT = ["XS", "GT", "XT0", "XT1"]
    u = Units(8, [("pro", NEXT, -1, 1), ("first", BODY, 0, 1), ("body", BODY, 1, B - 2),
                  ("last", [n for n in BODY if n not in NEXT], B - 1, 1)])
    DOES_FFN, DOES_NEXT = ("first", "body", "last"), ("pro", "first", "body")

    def begin(eng, step, name, b):
        wait(eng, evac[u.bank(step, name)], u.count(step, name, b))
        return ring[u.bank(step, name)]

    def taken(step, name):
        return evac[u.bank(step, name)]

    def wait_full(eng, step, name, b):
        eng.wait_ge(full[u.bank(step, name)], u.count(step, name, b) + 1)
        return ring[u.bank(step, name)]

    def wait_evac(eng, step, name, b):
        eng.wait_ge(evac[u.bank(step, name)], u.count(step, name, b) + 1)

    def walk(eng, body):
        body("pro", -1, 1, 0)
        body("first", 0, 0, 0)
        with eng.Fori(0, (B - 2) // 2) as i:
            body("body", 2 * i + 1, 1, i)
            body("body", 2 * i + 2, 0, i + 1)
        body("last", B - 1, 1, (B - 2) // 2)

    block = stack.enter_context(nc.Block())

    def weights(n):
        e = n % NE
        if n < NE:
            return [(w1[LO][:, e, :, :], w1[HI][:, e, :, :])]
        return [(w2[LO][:, e, 0:FC - 1, :], w2[HI][:, e, 0:FC - 1, :]),
                (w2[LO][0:FR, e, FC - 1, :], w2[HI][0:FR, e, FC - 1, :])]

    @block.sync
    def _(sp):
        sp.dma_start(b2_b[:, :, :], b2.rearrange("e n -> (e n)").partition_broadcast(P)).then_inc(b_ld, 16)

        def body(step, b, par, half):
            if step in ("first", "body"):
                if step == "body":
                    sp.wait_ge(res, 2 * T * (b - 1) + T)
                sp.dma_start(x2[1 - par][:, :, :], x2_dram[b + 1]).then_inc(x_ld[1 - par], 16)
            if step in ("body", "last"):
                wait_evac(sp, "body", f"OUT{T - 1}", b - 1)
                sp.dma_start(out_t[b - 1], xo[:, :, :]).then_inc(o_st, 16)
            if step == "last":
                wait_evac(sp, step, f"OUT{T - 1}", b)
                sp.dma_start(out_t[B - 1], xo[:, :, :]).then_inc(o_st, 16)

        walk(sp, body)
        sp.wait_ge(o_st, 16 * B)

    @block.gpsimd
    def _(pool):
        pool.memset(ident[:, :], 0.0).then_inc(const, 1)
        pool.memset(neg_half[:, :], -0.5).then_inc(const, 1)
        pool.memset(euler[:, :], EULER).then_inc(const, 1)
        pool.memset(lg[:, :], LEAST).then_inc(const, 1)
        pool.memset(eps_ln[:, :], EPS_LN).then_inc(const, 1)
        pool.memset(scratch[:, :], 0.0).then_inc(const, 1)
        pool.memset(ones[:, :], 1.0).then_inc(const, 1)
        pool.wait_ge(const, 7)
        pool.affine_select(out=ident[:, :], in_=ident[:, :], compare_op=ALU.not_equal, fill=1.0,
                           base=0, pattern=[[-1, P]], channel_multiplier=1).then_inc(const, 1)

        def body(step, b, par, half):
            if step in DOES_NEXT:
                pool.wait_ge(ln_ag, T * (b + 2))
                pool.tensor_tensor(rs[:, :], mv[:, :, 1], eps_ln[:, :], ALU.add).then_inc(ln_rs, 1)
                pool.wait_ge(ln_rs, 2 * (b + 1) + 1)
                pool.tensor_tensor(rs[:, :], rs[:, :], neg_half[:, :], ALU.pow).then_inc(ln_rs, 1)
                pool.wait_ge(g_pick, 3 * (b + 2))
                pool.tensor_tensor(gd[:, 1:2], euler[:, :], gd[:, 0:1], ALU.pow).then_inc(g_pow, 1)

        walk(pool, body)

    @block.tensor
    def _(pe):
        pe.wait_ge(const, 8)
        pe.wait_ge(g_ld, 16 * KC)

        def hidden(step, b, ex, n):
            t, e = PAIRS[n]
            bank = begin(pe, step, f"H{n}", b)
            for kc in range(KC):
                for i, (xp, wp) in enumerate(PASSES):
                    last = pe.matmul(bank[:, 0:FF], xT[xp][:, kc, t * P:(t + 1) * P],
                                     w1[wp][:, bass.ds(ex[e], 1), kc, :].rearrange("p a f -> p (a f)"),
                                     start=(kc == 0 and i == 0), stop=(kc == KC - 1 and i == 2))
            last.then_inc(full[u.bank(step, f"H{n}")], 1)

        def x_transposes(step, b, j):
            bank = begin(pe, step, f"XT{j}", b)
            for k in range(2):
                for t in range(T):
                    last = pe.transpose(bank[:, (k * T + t) * P:(k * T + t + 1) * P],
                                        xh[:, t, (2 * j + k) * P:(2 * j + k + 1) * P], ident[:, :])
            last.then_inc(full[u.bank(step, f"XT{j}")], 1)

        def x_sums(step, b):
            pe.wait_ge(xh_rdy, T * (b + 2))
            bank = begin(pe, step, "XS", b)
            for kc in range(KC):
                for t in range(T):
                    last = pe.matmul(bank[:, kc:kc + 1], xh[:, t, kc * P:(kc + 1) * P], ones[:, :],
                                     start=(t == 0), stop=(t == T - 1))
            last.then_inc(full[u.bank(step, "XS")], 1)

        def gate_logits(step, b):
            bank = begin(pe, step, "GT", b)
            wait_evac(pe, step, "XS", b)
            for kc in range(KC):
                last = pe.matmul(bank[:, 0:NE], xsum[:, kc:kc + 1].broadcast_to([P, P]),
                                 gate[:, kc, :], start=(kc == 0), stop=(kc == KC - 1))
            last.then_inc(full[u.bank(step, "GT")], 1)

        def h_transposes(step, b, t):
            bank = begin(pe, step, f"HT{t}", b)
            pe.wait_ge(h_rdy, len(PAIRS) * b + TOP * (t + 1))
            for e in range(TOP):
                for fc in range(FC - 1):
                    k = e * (FC - 1) + fc
                    last = pe.transpose(bank[:, k * P:(k + 1) * P],
                                        hb[:, TOP * t + e, fc * P:(fc + 1) * P], ident[:, :])
            last.then_inc(full[u.bank(step, f"HT{t}")], 1)

        def last_chunks(step, b):
            bank = begin(pe, step, "HR", b)
            for e in range(TOP):
                for t in range(T):
                    last = pe.transpose(bank[0:FR, e * S + t * P:e * S + (t + 1) * P],
                                        hb[:, TOP * t + e, (FC - 1) * P:FF], ident[:, :])
            last.then_inc(full[u.bank(step, "HR")], 1)

        def output(step, b, ex, t):
            bank = begin(pe, step, f"OUT{t}", b)
            wait_evac(pe, step, f"HT{t}", b)
            if t == 0 and step == "first":
                pe.wait_ge(w_lo, 2 * NE)
            order = [(e, fc) for e in range(TOP) for fc in range(FC - 1)] + [
                (e, FC - 1) for e in range(TOP)]
            for n, (e, fc) in enumerate(order):
                if t == 0 and n == TOP * (FC - 1):
                    wait_evac(pe, step, "HR", b)
                rows = P if fc < FC - 1 else FR
                if t == T - 1 and n == len(order) - 1 and step in DOES_NEXT:
                    pe.wait_ge(g_val, 2 * (b + 2))
                for i, (hp, wp) in enumerate(PASSES):
                    last = pe.matmul(bank[:, :], hT[hp][0:rows, e, fc, t * P:(t + 1) * P],
                                     w2[wp][0:rows, bass.ds(ex[e], 1), fc, :].rearrange("p a n -> p (a n)"),
                                     start=(n == 0 and i == 0),
                                     stop=(n == len(order) - 1 and i == 2))
            last.then_inc(full[u.bank(step, f"OUT{t}")], 1)

        def body(step, b, par, half):
            ffn, nxt = step in DOES_FFN, step in DOES_NEXT
            if ffn:
                if step == "first":
                    pe.wait_ge(g_val, 2)
                ex = [pe.value_load(idx[par][0:1, e:e + 1], min_val=0, max_val=NE - 1) for e in range(TOP)]
                if step == "first":
                    pe.wait_ge(w_lo, NE)
                wait_evac(pe, "pro" if step == "first" else "body", "XT1", b - 1)
                for n in range(3):
                    hidden(step, b, ex, n)
            if nxt:
                x_sums(step, b)
            if ffn:
                hidden(step, b, ex, 3)
                h_transposes(step, b, 0)
            if nxt:
                gate_logits(step, b)
                x_transposes(step, b, 0)
            if ffn:
                h_transposes(step, b, 1)
                last_chunks(step, b)
            if nxt:
                x_transposes(step, b, 1)
            if ffn:
                for t in range(T):
                    output(step, b, ex, t)

        walk(pe, body)

    @block.scalar
    def _(act):
        def high_parts(n):
            act.wait_ge(moe.loaded[n], 16 * (1 if n < NE else 2))
            for whole, hi in weights(n):
                act.activation(hi, whole.bitcast(F32), ACT.Copy).then_inc(w_hi, 1)

        def body(step, b, par, half):
            ffn, nxt = step in DOES_FFN, step in DOES_NEXT
            if step == "pro":
                for n in range(NE):
                    high_parts(n)
            if ffn:
                for n in range(len(PAIRS)):
                    if n == 3 and step == "first":
                        for k in range(NE + SPLIT_PRO, 2 * NE):
                            high_parts(k)
                    if n == 3 and nxt:
                        bank = wait_full(act, step, "XS", b)
                        act.activation(xsum[:, :], bank[:, 0:KC], ACT.Copy).then_inc(taken(step, "XS"), 1)
                    wait_evac(act, step, f"H{n}", b)
                    act.activation(hb[:, n, :], hb[:, n, :], ACT.Gelu).then_inc(h_rdy, 1)
                for t in range(T):
                    bank = wait_full(act, step, f"HT{t}", b)
                    for e in range(TOP):
                        cols = bank[:, e * (FC - 1) * P:(e + 1) * (FC - 1) * P]
                        act.activation(hT[HI][:, e, 0:FC - 1, t * P:(t + 1) * P],
                                       cols.rearrange("p (c n) -> p c n", n=P),
                                       ACT.Copy, scale=gv[par][:, e:e + 1]).then_inc(h_hi, 1)
                bank = wait_full(act, step, "HR", b)
                for e in range(TOP):
                    act.activation(hT[HI][0:FR, e, FC - 1, :], bank[0:FR, e * S:(e + 1) * S],
                                   ACT.Copy, scale=gv[par][0:FR, e:e + 1]).then_inc(h_hi, 1)
            elif nxt:
                bank = wait_full(act, step, "XS", b)
                act.activation(xsum[:, :], bank[:, 0:KC], ACT.Copy).then_inc(taken(step, "XS"), 1)
            if nxt:
                for j in range(2):
                    bank = wait_full(act, step, f"XT{j}", b)
                    act.activation(xT[HI][:, 2 * j:2 * j + 2, :],
                                   bank[:, :].rearrange("p (a n) -> p a n", a=2), ACT.Copy).then_inc(x_hi, 1)
            if step == "pro":
                for n in range(NE, NE + SPLIT_PRO):
                    high_parts(n)

        walk(act, body)

    @block.vector
    def _(dve):
        dve.wait_ge(const, 8)
        dve.wait_ge(moe.b1_ld, 16)

        def low_parts(n):
            dve.wait_ge(w_hi, n + 1 if n < NE else NE + 2 * (n - NE + 1))
            for whole, hi in weights(n):
                last = dve.tensor_tensor(whole, whole.bitcast(F32), hi.bitcast(F32), ALU.subtract)
            last.then_inc(w_lo, 1)

        def body(step, b, par, half):
            ffn, does_next = step in DOES_FFN, step in DOES_NEXT
            nxt = 1 - par

            def x_low(j):
                dve.wait_ge(x_hi, 2 * (b + 1) + j + 1)
                bank = ring[u.bank(step, f"XT{j}")]
                dve.tensor_tensor(xT[LO][:, 2 * j:2 * j + 2, :],
                                  bank[:, :].rearrange("p (a n) -> p a n", a=2),
                                  xT[HI][:, 2 * j:2 * j + 2, :].bitcast(F32),
                                  ALU.subtract).then_inc(taken(step, f"XT{j}"), 1)

            def residual(e):
                for t in range(T):
                    last = dve.scalar_tensor_tensor(
                        xo[:, t, :], b2_b[:, bass.ds(ex[e], 1), :].rearrange("p a n -> p (a n)"),
                        gv[par][:, e:e + 1], (x2[par] if e == 0 else xo)[:, t, :], ALU.mult, ALU.add)
                    last.then_inc(res, 1)

            if does_next:
                dve.wait_ge(x_ld[nxt], 16 * (half + par + 1) if step != "pro" else 16)
                for t in range(T):
                    dve.bn_stats(st6[:, t, :], x2[nxt][:, t, :]).then_inc(ln_st, 1)
                dve.wait_ge(ln_st, T * (b + 2))
                carry_wait(dve, scratch)
                for t in range(T):
                    dve.bn_aggr(mv[:, t, :], st6[:, t, :]).then_inc(ln_ag, 1)
                dve.wait_ge(ln_rs, 2 * (b + 2))
                for t in range(T):
                    dve.tensor_scalar(xh[:, t, :], x2[nxt][:, t, :], mv[:, t, 0:1], rs[:, t:t + 1],
                                      ALU.subtract, ALU.mult).then_inc(xh_rdy, 1)
            if step == "pro":
                for n in range(NE):
                    low_parts(n)
            if ffn:
                ex = [dve.value_load(idx[par][0:1, e:e + 1], min_val=0, max_val=NE - 1) for e in range(TOP)]
                for n, (t, e) in enumerate(PAIRS):
                    if n == 3:
                        if step == "first":
                            dve.wait_ge(b_ld, 16)
                            for k in range(NE + SPLIT_PRO, 2 * NE):
                                low_parts(k)
                        else:
                            dve.wait_ge(o_st, 16 * b)
                        residual(0)
                    bank = wait_full(dve, step, f"H{n}", b)
                    dve.tensor_tensor(hb[:, n, :], bank[:, 0:FF],
                                      b1_b[:, bass.ds(ex[e], 1), :].rearrange("p a f -> p (a f)"),
                                      ALU.add).then_inc(taken(step, f"H{n}"), 1)
                for t in range(T):
                    bank = ring[u.bank(step, f"HT{t}")]
                    for e in range(TOP):
                        dve.wait_ge(h_hi, 6 * b + 2 * t + 2)
                        part = (slice(None), e, slice(0, FC - 1), slice(t * P, (t + 1) * P))
                        cols = bank[:, e * (FC - 1) * P:(e + 1) * (FC - 1) * P]
                        last = dve.scalar_tensor_tensor(
                            hT[LO][part], cols.rearrange("p (c n) -> p c n", n=P), gv[par][:, e:e + 1],
                            hT[HI][part].bitcast(F32), ALU.mult, ALU.subtract)
                    last.then_inc(taken(step, f"HT{t}"), 1)
                bank = ring[u.bank(step, "HR")]
                for e in range(TOP):
                    dve.wait_ge(h_hi, 6 * b + 6)
                    last = dve.scalar_tensor_tensor(
                        hT[LO][0:FR, e, FC - 1, :], bank[0:FR, e * S:(e + 1) * S], gv[par][0:FR, e:e + 1],
                        hT[HI][0:FR, e, FC - 1, :].bitcast(F32), ALU.mult, ALU.subtract)
                last.then_inc(taken(step, "HR"), 1)
            if does_next:
                for j in range(2):
                    x_low(j)
            if ffn:
                dve.wait_ge(res, 2 * T * b + T)
                residual(1)
            if does_next:
                bank = wait_full(dve, step, "GT", b)
                dve.tensor_scalar(lg[:, 0:NE], bank[:, 0:NE], 1.0 / S, None,
                                  ALU.mult).then_inc(taken(step, "GT"), 1)
                wait_evac(dve, step, "GT", b)
                carry_wait(dve, scratch)
                dve.max(top[:, :], lg[:, :]).then_inc(g_pick, 1)
                dve.wait_ge(g_pick, 3 * (b + 1) + 1)
                carry_wait(dve, scratch)
                dve.max_index(idx[nxt][:, :], top[:, :], lg[:, :]).then_inc(g_pick, 1)
                dve.tensor_tensor(gd[:, 0:1], top[:, 1:2], top[:, 0:1], ALU.subtract).then_inc(g_pick, 1)
                dve.wait_ge(g_pow, b + 2)
                dve.tensor_scalar(gd[:, 0:1], gd[:, 1:2], 1.0, None, ALU.add).then_inc(g_log, 1)
                dve.wait_ge(g_log, b + 2)
                dve.reciprocal(gv[nxt][:, 0:1], gd[:, 0:1]).then_inc(g_val, 1)
                dve.wait_ge(g_val, 2 * (b + 1) + 1)
                dve.tensor_tensor(gv[nxt][:, 1:2], gv[nxt][:, 0:1], gd[:, 1:2], ALU.mult).then_inc(g_val, 1)
                dve.wait_ge(g_val, 2 * (b + 2))
            if step == "pro":
                for n in range(NE, NE + SPLIT_PRO):
                    low_parts(n)
            if ffn:
                dve.wait_ge(res, 2 * T * (b + 1))
                for t in range(T):
                    bank = wait_full(dve, step, f"OUT{t}", b)
                    dve.tensor_tensor(xo[:, t, :], bank[:, :], xo[:, t, :],
                                      ALU.add).then_inc(taken(step, f"OUT{t}"), 1)

        walk(dve, body)


_INS = ['x', 'ctx_1024', 'L0_xattn_Wq', 'L0_xattn_bq', 'L0_xattn_Wk', 'L0_xattn_bk', 'L0_xattn_Wv',
        'L0_xattn_bv', 'L0_xattn_Wkv_dca', 'L0_xattn_bkv_dca', 'L0_xattn_qn_w', 'L0_xattn_qn_b',
        'L0_xattn_kn_w', 'L0_xattn_kn_b', 'L0_xattn_kn_dca_w', 'L0_xattn_kn_dca_b', 'L0_xattn_Wo',
        'L0_xattn_bo', 'L0_ffn_gate_W', 'L0_ffn_W1', 'L0_ffn_b1', 'L0_ffn_W2', 'L0_ffn_b2']
_OUTS = [((16, 256, 512), 'float32')]


def kernel(**inputs):
    import numpy as _np
    import concourse.bacc as _bacc
    from concourse import mybir as _mybir
    from concourse.bass_utils import run_bass_kernel_spmd as _run

    nc = _bacc.Bacc("TRN2", target_bir_lowering=False, num_devices=1)
    arrays, args = {}, []
    for name in _INS:
        a = _np.ascontiguousarray(inputs[name])
        arrays[f"in_{name}_dram"] = a
        args.append(nc.dram_tensor(f"in_{name}_dram", a.shape, _mybir.dt.from_np(a.dtype), kind="ExternalInput").ap())
    for i, (shape, dtype) in enumerate(_OUTS):
        dt = _mybir.dt.from_np(_np.dtype(dtype))
        args.append(nc.dram_tensor(f"out_{i}_dram", shape, dt, kind="ExternalOutput").ap())
    bass_xattn_moe(nc, *args)
    r = _run(nc, [arrays], core_ids=[0])
    got = tuple(r.results[0][f"out_{i}_dram"] for i in range(len(_OUTS)))
    return got[0]
```
